# Optimizing a Trainium2 kernel written in Bass

```python
import numpy as np
import jax
import jax.numpy as jnp

def _softmax(x, axis=-1):
    return jax.nn.softmax(x, axis=axis)

def _gelu(x):
    return jax.nn.gelu(x, approximate=True)

def _silu(x):
    return jax.nn.silu(x)

def _sigmoid(x):
    return jax.nn.sigmoid(x)

def _layernorm(x, axis=-1, eps=1e-05):
    m = jnp.mean(x, axis=axis, keepdims=True)
    v = jnp.var(x, axis=axis, keepdims=True)
    return (x - m) / jnp.sqrt(v + eps)

def _scatter_add(tgt, idx, src, axis=0):
    return tgt.at[idx].add(src)

def _segment_sum(src, seg, n):
    return jax.ops.segment_sum(src, seg, n)
kernel_name = 'mk_flamingo_gated_d4_seqx_r4_3ed393'

def setup_inputs(seed: int=0):
    np.random.seed(seed)
    _w = jnp.asarray

    def _rec_inputs():
        import jax
        import jax.numpy as jnp
        _rk = jax.random.key(seed)
        x = 7.22e-05 + 1 * jax.random.normal(jax.random.fold_in(_rk, 1), (4, 1024, 256), jnp.float32)
        _lenS = 1024 - jax.random.randint(jax.random.fold_in(_rk, 7), (4,), 0, max(1, 1024 // 4) + 1, jnp.int32)
        _lenS2 = 77 - jax.random.randint(jax.random.fold_in(_rk, 8), (4,), 0, max(1, 77 // 4) + 1, jnp.int32)
        _ctx_1024P = jax.random.normal(jax.random.fold_in(_rk, 11), (4, 16, 256), jnp.float32)
        _ctx_1024c = jax.random.dirichlet(jax.random.fold_in(_rk, 511), 0.3 * jnp.ones((16,), jnp.float32), (4, 77))
        _ctx_1024t = jnp.einsum('bsk,bkd->bsd', _ctx_1024c, _ctx_1024P)
        _ctx_1024t = _ctx_1024t * jax.lax.rsqrt(jnp.mean(jnp.square(_ctx_1024t)) + 1e-12) * 0.953939
        ctx_1024 = 4.13588e-05 + 0.999923 * (_ctx_1024t + 0.3 * jax.random.normal(jax.random.fold_in(_rk, 611), (4, 77, 256), jnp.float32))
        _validS = jnp.arange(1024)[None, :] < _lenS[:, None]
        _validS2 = jnp.arange(77)[None, :] < _lenS2[:, None]
        _causal = jnp.tril(jnp.ones((1024, 1024), dtype=bool))
        mask_BxS2_bk0 = jnp.logical_not(jnp.broadcast_to(_validS2[:, :], (4, 77)))
        _g = jax.random.normal(jax.random.fold_in(_rk, 9001), (2, 4), jnp.float32)
        _g = jnp.sign(_g) * jnp.maximum(jnp.abs(_g), 1.0) + (_g == 0) * 1.0
        g_xattn = _g[0]
        g_ffn = _g[1]
        return (x, ctx_1024, mask_BxS2_bk0, g_xattn, g_ffn)
    x, ctx_1024, mask_BxS2_bk0, g_xattn, g_ffn = _rec_inputs()

    def _L0_xattn_setup():
        import jax, jax.numpy as jnp
        import numpy as np
        HEADS = 16
        DIM_HEAD = 64
        SCALE = DIM_HEAD ** (-0.5)
        key = jax.random.key(seed)
        ks = jax.random.split(key, 5)
        B, S, D = (4, 512, 256)
        _dim = HEADS * DIM_HEAD
        return {'q': jax.random.normal(ks[0], (B, S, D), dtype=jnp.float32), 'kv': jax.random.normal(ks[1], (B, S, D), dtype=jnp.float32), 'Wq': jax.random.normal(ks[2], (_dim, D), dtype=jnp.float32) * 0.02, 'Wkv': jax.random.normal(ks[3], (2 * _dim, D), dtype=jnp.float32) * 0.02, 'W0': jax.random.normal(ks[4], (D, _dim), dtype=jnp.float32) * 0.02}
    _L0_xattn_all = _L0_xattn_setup()
    _L0_xattn_in = {k: v for k, v in _L0_xattn_all.items() if k in ('Wq', 'Wkv', 'W0')}
    del _L0_xattn_all

    def _L0_ffn_setup():
        import jax, jax.numpy as jnp
        import numpy as np
        B, S, H = (2, 256, 256)
        KD, NH, K = (128, 8, 8)
        NE = 16384
        NK = 64
        EPS = 1e-05
        key = jax.random.key(seed)
        ks = jax.random.split(key, 5)
        inputs = jax.random.normal(ks[0], (B, S, H), jnp.float32)
        bn_gamma = jnp.ones((H,), jnp.float32)
        bn_beta = jnp.zeros((H,), jnp.float32)
        w_q = jax.random.normal(ks[1], (2 * NH * KD, H), jnp.float32) * (1.0 / np.sqrt(H))
        keys_p = jax.random.normal(ks[2], (NH, NK, 2, KD), jnp.float32) * 0.02
        lim = float(np.sqrt(6.0 / (NE + H)))
        down = jax.random.uniform(ks[3], (NE, H), jnp.float32, -lim, lim)
        up = jax.random.uniform(ks[4], (NE, H), jnp.float32, -lim, lim)
        return {'inputs': inputs, 'bn_gamma': bn_gamma, 'bn_beta': bn_beta, 'w_q': w_q, 'keys_p': keys_p, 'down': down, 'up': up}
    _L0_ffn_all = _L0_ffn_setup()
    _L0_ffn_in = {k: v for k, v in _L0_ffn_all.items() if k in ('bn_gamma', 'bn_beta', 'w_q', 'keys_p', 'down', 'up')}
    del _L0_ffn_all

    def _L1_xattn_setup():
        import jax, jax.numpy as jnp
        import numpy as np
        DIM = 256
        HEADS = 16
        DIM_HEAD = 64
        INNER = HEADS * DIM_HEAD
        EPS = 1e-05

        def layernorm(t, g, b):
            mu = jnp.mean(t, axis=-1, keepdims=True)
            var = jnp.var(t, axis=-1, keepdims=True)
            return (t - mu) * jax.lax.rsqrt(var + EPS) * g + b
        key = jax.random.key(seed)
        ks = jax.random.split(key, 8)
        b, n, m = (8, 1024, 64)
        x = jax.random.normal(ks[0], (b, n, DIM), dtype=jnp.float32)
        latents = jax.random.normal(ks[1], (b, m, DIM), dtype=jnp.float32)
        mask = jax.random.randint(ks[2], (b, n), 0, 2).astype(bool)
        s = 0.02
        Wq = jax.random.normal(ks[3], (DIM, INNER), dtype=jnp.float32) * s
        Wkv = jax.random.normal(ks[4], (DIM, 2 * INNER), dtype=jnp.float32) * s
        Wout = jax.random.normal(ks[5], (INNER, DIM), dtype=jnp.float32) * s
        ln_x_g = jnp.ones((DIM,), jnp.float32)
        ln_x_b = jnp.zeros((DIM,), jnp.float32)
        ln_l_g = jnp.ones((DIM,), jnp.float32)
        ln_l_b = jnp.zeros((DIM,), jnp.float32)
        ln_o_g = jnp.ones((DIM,), jnp.float32)
        ln_o_b = jnp.zeros((DIM,), jnp.float32)
        return {'x': x, 'latents': latents, 'mask': mask, 'ln_x_g': ln_x_g, 'ln_x_b': ln_x_b, 'ln_l_g': ln_l_g, 'ln_l_b': ln_l_b, 'Wq': Wq, 'Wkv': Wkv, 'Wout': Wout, 'ln_o_g': ln_o_g, 'ln_o_b': ln_o_b}
    _L1_xattn_all = _L1_xattn_setup()
    _L1_xattn_in = {k: v for k, v in _L1_xattn_all.items() if k in ('ln_x_g', 'ln_x_b', 'ln_l_g', 'ln_l_b', 'Wq', 'Wkv', 'Wout', 'ln_o_g', 'ln_o_b')}
    del _L1_xattn_all

    def _L1_ffn_setup():
        import jax, jax.numpy as jnp
        import numpy as np
        B, S, H, F, E = (8, 512, 256, 1024, 8)
        INIT_LAMBDA = 0.2
        key = jax.random.key(seed)
        ks = jax.random.split(key, 12)
        std = 0.02
        return {'hidden_states': jax.random.normal(ks[0], (B, S, H), jnp.float32), 'gate_w1': jax.random.normal(ks[1], (H, H), jnp.float32) * 0.01, 'gate_b1': jnp.zeros((H,), jnp.float32), 'gate_w2': jax.random.normal(ks[2], (E, H), jnp.float32) * 0.01, 'gate_b2': jnp.full((E,), INIT_LAMBDA, jnp.float32), 'W1': jax.random.normal(ks[3], (F, H), jnp.float32) * std, 'b1': jax.random.normal(ks[4], (F,), jnp.float32) * std, 'W2': jax.random.normal(ks[5], (H, F), jnp.float32) * std, 'b2': jax.random.normal(ks[6], (H,), jnp.float32) * std, 'TW1': jax.random.normal(ks[7], (E, F, H), jnp.float32) * std, 'Tb1': jax.random.normal(ks[8], (E, F), jnp.float32) * std, 'TW2': jax.random.normal(ks[9], (E, H, F), jnp.float32) * std, 'Tb2': jax.random.normal(ks[10], (E, H), jnp.float32) * std}
    _L1_ffn_all = _L1_ffn_setup()
    _L1_ffn_in = {k: v for k, v in _L1_ffn_all.items() if k in ('gate_w1', 'gate_b1', 'gate_w2', 'gate_b2', 'W1', 'b1', 'W2', 'b2', 'TW1', 'Tb1', 'TW2', 'Tb2')}
    del _L1_ffn_all

    def _L2_xattn_setup():
        import jax, jax.numpy as jnp
        import numpy as np
        HIDDEN = 256
        B, S = (8, 512)
        key = jax.random.key(seed)
        ks = jax.random.split(key, 6)
        scale = 1.0 / np.sqrt(HIDDEN)
        return {'q': jax.random.normal(ks[0], (B, S, HIDDEN), jnp.float32), 'k': jax.random.normal(ks[1], (B, S, HIDDEN), jnp.float32), 'v': jax.random.normal(ks[2], (B, S, HIDDEN), jnp.float32), 'Wq': jax.random.normal(ks[3], (HIDDEN, HIDDEN), jnp.float32) * scale, 'bq': jnp.zeros((HIDDEN,), jnp.float32), 'Wk': jax.random.normal(ks[4], (HIDDEN, HIDDEN), jnp.float32) * scale, 'bk': jnp.zeros((HIDDEN,), jnp.float32), 'Wv': jax.random.normal(ks[5], (HIDDEN, HIDDEN), jnp.float32) * scale, 'bv': jnp.zeros((HIDDEN,), jnp.float32)}
    _L2_xattn_all = _L2_xattn_setup()
    _L2_xattn_in = {k: v for k, v in _L2_xattn_all.items() if k in ('Wq', 'bq', 'Wk', 'bk', 'Wv', 'bv')}
    del _L2_xattn_all

    def _L2_ffn_setup():
        import jax, jax.numpy as jnp
        import numpy as np
        HID = 256
        INTER = 1024
        RDIM = 128
        HEADS = 4
        NUM_EXPERTS = 4096
        NUM_KEYS = 128
        TOPK = 8
        B, T = (2, 512)
        key = jax.random.key(seed)
        ks = jax.random.split(key, 8)
        s = lambda fan_in: 1.0 / np.sqrt(fan_in)
        return {'hidden_states': jax.random.normal(ks[0], (B, T, HID), jnp.float32), 'Wq': jax.random.normal(ks[1], (HEADS * RDIM, HID), jnp.float32) * s(HID), 'keys': jax.random.normal(ks[2], (HEADS, NUM_KEYS, 2, RDIM // 2), jnp.float32) * s(RDIM // 2), 'down_embed': jax.random.normal(ks[3], (NUM_EXPERTS, HID), jnp.float32) * 0.02, 'up_embed': jax.random.normal(ks[4], (NUM_EXPERTS, HID), jnp.float32) * 0.02, 'Wg': jax.random.normal(ks[5], (INTER, HID), jnp.float32) * s(HID), 'Wu': jax.random.normal(ks[6], (INTER, HID), jnp.float32) * s(HID), 'Wd': jax.random.normal(ks[7], (HID, INTER), jnp.float32) * s(INTER)}
    _L2_ffn_all = _L2_ffn_setup()
    _L2_ffn_in = {k: v for k, v in _L2_ffn_all.items() if k in ('Wq', 'keys', 'down_embed', 'up_embed', 'Wg', 'Wu', 'Wd')}
    del _L2_ffn_all

    def _L3_xattn_setup():
        import jax, jax.numpy as jnp
        import numpy as np
        B, SD, SE, D, H = (4, 512, 512, 256, 16)
        HD = D // H

        def _mha(xq, xk, xv, Wq, bq, Wk, bk, Wv, bv, Wo, bo, causal):
            q = jnp.einsum('bsd,hde->bhse', xq, Wq) + bq[None, :, None, :]
            k = jnp.einsum('bsd,hde->bhse', xk, Wk) + bk[None, :, None, :]
            v = jnp.einsum('bsd,hde->bhse', xv, Wv) + bv[None, :, None, :]
            scale = 1.0 / jnp.sqrt(jnp.asarray(HD, q.dtype))
            scores = jnp.einsum('bhqe,bhke->bhqk', q, k) * scale
            if causal:
                mask = jnp.tril(jnp.ones((q.shape[2], k.shape[2]), bool))
                scores = jnp.where(mask, scores, jnp.finfo(scores.dtype).min)
            w = jax.nn.softmax(scores, axis=-1)
            out = jnp.einsum('bhqk,bhke->bhqe', w, v)
            out = out.transpose(0, 2, 1, 3).reshape(out.shape[0], out.shape[2], D)
            return out @ Wo + bo
        key = jax.random.key(seed)
        ks = jax.random.split(key, 19)
        sd = 1.0 / np.sqrt(D)
        n = lambda k, shape, s: jax.random.normal(k, shape, jnp.float32) * s
        inp = {'x': n(ks[0], (B, SD, D), 1.0), 'encoder_k': n(ks[1], (B, SE, D), 1.0), 'encoder_v': n(ks[2], (B, SE, D), 1.0), 'Wq1': n(ks[3], (H, D, HD), sd), 'bq1': jnp.zeros((H, HD), jnp.float32), 'Wk1': n(ks[4], (H, D, HD), sd), 'bk1': jnp.zeros((H, HD), jnp.float32), 'Wv1': n(ks[5], (H, D, HD), sd), 'bv1': jnp.zeros((H, HD), jnp.float32), 'Wo1': n(ks[6], (D, D), sd), 'bo1': jnp.zeros((D,), jnp.float32), 'Wq2': n(ks[7], (H, D, HD), sd), 'bq2': jnp.zeros((H, HD), jnp.float32), 'Wk2': n(ks[8], (H, D, HD), sd), 'bk2': jnp.zeros((H, HD), jnp.float32), 'Wv2': n(ks[9], (H, D, HD), sd), 'bv2': jnp.zeros((H, HD), jnp.float32), 'Wo2': n(ks[10], (D, D), sd), 'bo2': jnp.zeros((D,), jnp.float32)}
        return inp
    _L3_xattn_all = _L3_xattn_setup()
    _L3_xattn_in = {k: v for k, v in _L3_xattn_all.items() if k in ('Wq1', 'bq1', 'Wk1', 'bk1', 'Wv1', 'bv1', 'Wo1', 'bo1', 'Wq2', 'bq2', 'Wk2', 'bk2', 'Wv2', 'bv2', 'Wo2', 'bo2')}
    del _L3_xattn_all

    def _L3_ffn_setup():
        import jax, jax.numpy as jnp
        import numpy as np
        HIDDEN = 256
        INNER = 1024

        def _weight_quant(w):
            scale = 1.0 / jnp.clip(jnp.mean(jnp.abs(w)), 1e-05)
            wq = jnp.clip(jnp.round(w * scale), -1.0, 1.0) / scale
            return w + jax.lax.stop_gradient(wq - w)

        def _act_quant(x):
            scale = 127.0 / jnp.clip(jnp.max(jnp.abs(x), axis=-1, keepdims=True), 1e-05)
            xq = jnp.clip(jnp.round(x * scale), -128.0, 127.0) / scale
            return x + jax.lax.stop_gradient(xq - x)

        def _bitlinear(x, w):
            return jnp.einsum('bsi,oi->bso', _act_quant(x), _weight_quant(w))
        key = jax.random.key(seed)
        k0, k1, k2, k3 = jax.random.split(key, 4)
        x = jax.random.normal(k0, (4, 512, HIDDEN), dtype=jnp.float32)
        w_gate = jax.random.normal(k1, (INNER, HIDDEN), dtype=jnp.float32) / np.sqrt(HIDDEN)
        w_up = jax.random.normal(k2, (INNER, HIDDEN), dtype=jnp.float32) / np.sqrt(HIDDEN)
        w_down = jax.random.normal(k3, (HIDDEN, INNER), dtype=jnp.float32) / np.sqrt(INNER)
        return {'x': x, 'w_gate': w_gate, 'w_up': w_up, 'w_down': w_down}
    _L3_ffn_all = _L3_ffn_setup()
    _L3_ffn_in = {k: v for k, v in _L3_ffn_all.items() if k in ('w_gate', 'w_up', 'w_down')}
    del _L3_ffn_all
    return {'x': x, 'ctx_1024': ctx_1024, 'mask_BxS2_bk0': mask_BxS2_bk0, 'g_xattn': g_xattn, 'g_ffn': g_ffn, 'L0_xattn_Wq': _L0_xattn_in['Wq'], 'L0_xattn_Wkv': _L0_xattn_in['Wkv'], 'L0_xattn_W0': _L0_xattn_in['W0'], 'L0_ffn_bn_gamma': _L0_ffn_in['bn_gamma'], 'L0_ffn_bn_beta': _L0_ffn_in['bn_beta'], 'L0_ffn_w_q': _L0_ffn_in['w_q'], 'L0_ffn_keys_p': _L0_ffn_in['keys_p'], 'L0_ffn_down': _L0_ffn_in['down'], 'L0_ffn_up': _L0_ffn_in['up'], 'L1_xattn_ln_x_g': _L1_xattn_in['ln_x_g'], 'L1_xattn_ln_x_b': _L1_xattn_in['ln_x_b'], 'L1_xattn_ln_l_g': _L1_xattn_in['ln_l_g'], 'L1_xattn_ln_l_b': _L1_xattn_in['ln_l_b'], 'L1_xattn_Wq': _L1_xattn_in['Wq'], 'L1_xattn_Wkv': _L1_xattn_in['Wkv'], 'L1_xattn_Wout': _L1_xattn_in['Wout'], 'L1_xattn_ln_o_g': _L1_xattn_in['ln_o_g'], 'L1_xattn_ln_o_b': _L1_xattn_in['ln_o_b'], 'L1_ffn_gate_w1': _L1_ffn_in['gate_w1'], 'L1_ffn_gate_b1': _L1_ffn_in['gate_b1'], 'L1_ffn_gate_w2': _L1_ffn_in['gate_w2'], 'L1_ffn_gate_b2': _L1_ffn_in['gate_b2'], 'L1_ffn_W1': _L1_ffn_in['W1'], 'L1_ffn_b1': _L1_ffn_in['b1'], 'L1_ffn_W2': _L1_ffn_in['W2'], 'L1_ffn_b2': _L1_ffn_in['b2'], 'L1_ffn_TW1': _L1_ffn_in['TW1'], 'L1_ffn_Tb1': _L1_ffn_in['Tb1'], 'L1_ffn_TW2': _L1_ffn_in['TW2'], 'L1_ffn_Tb2': _L1_ffn_in['Tb2'], 'L2_xattn_Wq': _L2_xattn_in['Wq'], 'L2_xattn_bq': _L2_xattn_in['bq'], 'L2_xattn_Wk': _L2_xattn_in['Wk'], 'L2_xattn_bk': _L2_xattn_in['bk'], 'L2_xattn_Wv': _L2_xattn_in['Wv'], 'L2_xattn_bv': _L2_xattn_in['bv'], 'L2_ffn_Wq': _L2_ffn_in['Wq'], 'L2_ffn_keys': _L2_ffn_in['keys'], 'L2_ffn_down_embed': _L2_ffn_in['down_embed'], 'L2_ffn_up_embed': _L2_ffn_in['up_embed'], 'L2_ffn_Wg': _L2_ffn_in['Wg'], 'L2_ffn_Wu': _L2_ffn_in['Wu'], 'L2_ffn_Wd': _L2_ffn_in['Wd'], 'L3_xattn_Wq1': _L3_xattn_in['Wq1'], 'L3_xattn_bq1': _L3_xattn_in['bq1'], 'L3_xattn_Wk1': _L3_xattn_in['Wk1'], 'L3_xattn_bk1': _L3_xattn_in['bk1'], 'L3_xattn_Wv1': _L3_xattn_in['Wv1'], 'L3_xattn_bv1': _L3_xattn_in['bv1'], 'L3_xattn_Wo1': _L3_xattn_in['Wo1'], 'L3_xattn_bo1': _L3_xattn_in['bo1'], 'L3_xattn_Wq2': _L3_xattn_in['Wq2'], 'L3_xattn_bq2': _L3_xattn_in['bq2'], 'L3_xattn_Wk2': _L3_xattn_in['Wk2'], 'L3_xattn_bk2': _L3_xattn_in['bk2'], 'L3_xattn_Wv2': _L3_xattn_in['Wv2'], 'L3_xattn_bv2': _L3_xattn_in['bv2'], 'L3_xattn_Wo2': _L3_xattn_in['Wo2'], 'L3_xattn_bo2': _L3_xattn_in['bo2'], 'L3_ffn_w_gate': _L3_ffn_in['w_gate'], 'L3_ffn_w_up': _L3_ffn_in['w_up'], 'L3_ffn_w_down': _L3_ffn_in['w_down']}

def reference(x, ctx_1024, mask_BxS2_bk0, g_xattn, g_ffn, L0_xattn_Wq, L0_xattn_Wkv, L0_xattn_W0, L0_ffn_bn_gamma, L0_ffn_bn_beta, L0_ffn_w_q, L0_ffn_keys_p, L0_ffn_down, L0_ffn_up, L1_xattn_ln_x_g, L1_xattn_ln_x_b, L1_xattn_ln_l_g, L1_xattn_ln_l_b, L1_xattn_Wq, L1_xattn_Wkv, L1_xattn_Wout, L1_xattn_ln_o_g, L1_xattn_ln_o_b, L1_ffn_gate_w1, L1_ffn_gate_b1, L1_ffn_gate_w2, L1_ffn_gate_b2, L1_ffn_W1, L1_ffn_b1, L1_ffn_W2, L1_ffn_b2, L1_ffn_TW1, L1_ffn_Tb1, L1_ffn_TW2, L1_ffn_Tb2, L2_xattn_Wq, L2_xattn_bq, L2_xattn_Wk, L2_xattn_bk, L2_xattn_Wv, L2_xattn_bv, L2_ffn_Wq, L2_ffn_keys, L2_ffn_down_embed, L2_ffn_up_embed, L2_ffn_Wg, L2_ffn_Wu, L2_ffn_Wd, L3_xattn_Wq1, L3_xattn_bq1, L3_xattn_Wk1, L3_xattn_bk1, L3_xattn_Wv1, L3_xattn_bv1, L3_xattn_Wo1, L3_xattn_bo1, L3_xattn_Wq2, L3_xattn_bq2, L3_xattn_Wk2, L3_xattn_bk2, L3_xattn_Wv2, L3_xattn_bv2, L3_xattn_Wo2, L3_xattn_bo2, L3_ffn_w_gate, L3_ffn_w_up, L3_ffn_w_down):
    import jax
    import jax.numpy as jnp

    def _L0_xattn_ref(q, kv, Wq, Wkv, W0):
        import jax, jax.numpy as jnp
        import numpy as np
        HEADS = 16
        DIM_HEAD = 64
        SCALE = DIM_HEAD ** (-0.5)
        b, tq, _ = q.shape
        _, tk, _ = kv.shape
        qp = jnp.einsum('btm,em->bte', q, Wq)
        kvp = jnp.einsum('btm,em->bte', kv, Wkv)
        kvp = kvp.reshape(b, tk, DIM_HEAD, 2, HEADS)
        kvp = jnp.transpose(kvp, (3, 0, 4, 1, 2))
        k, v = (kvp[0], kvp[1])
        qh = jnp.transpose(qp.reshape(b, tq, DIM_HEAD, HEADS), (0, 3, 1, 2))
        scores = jnp.einsum('bhid,bhjd->bhij', qh, k) * SCALE
        attn = jax.nn.softmax(scores, axis=-1)
        attn = jnp.nan_to_num(attn)
        out = jnp.einsum('bhij,bhjd->bhid', attn, v)
        out = jnp.transpose(out, (0, 2, 1, 3)).reshape(b, tq, HEADS * DIM_HEAD)
        return jnp.einsum('bte,de->btd', out, W0)

    def _L0_ffn_ref(inputs, bn_gamma, bn_beta, w_q, keys_p, down, up):
        import jax, jax.numpy as jnp
        import numpy as np
        B, S, H = (2, 256, 256)
        KD, NH, K = (128, 8, 8)
        NE = 16384
        NK = 64
        EPS = 1e-05
        b, s, d = inputs.shape
        x = inputs.reshape(b * s, d)
        mean = x.mean(axis=0)
        var = x.var(axis=0)
        xn = (x - mean) * jax.lax.rsqrt(var + EPS) * bn_gamma + bn_beta
        xn = xn.reshape(b, s, d)
        q = (xn @ w_q.T).reshape(b, s, 2, NH, KD).transpose(2, 0, 1, 3, 4)
        sim = jnp.einsum('pbnhd,hkpd->pbnhk', q, keys_p)
        scores, idx = jax.lax.top_k(sim, K)
        all_scores = (scores[0][..., :, None] + scores[1][..., None, :]).reshape(b, s, NH, K * K)
        all_idx = (idx[0][..., :, None] * NK + idx[1][..., None, :]).reshape(b, s, NH, K * K)
        sc, pk = jax.lax.top_k(all_scores, K)
        indices = jnp.take_along_axis(all_idx, pk, axis=-1)
        wd = down[indices]
        hmid = jnp.einsum('bnd,bnhkd->bnhk', inputs, wd)
        hmid = jax.nn.sigmoid(sc) * jax.nn.gelu(hmid, approximate=False)
        wu = up[indices]
        return jnp.einsum('bnhk,bnhkd->bnd', hmid, wu)

    def _L1_xattn_ref(x, latents, mask, ln_x_g, ln_x_b, ln_l_g, ln_l_b, Wq, Wkv, Wout, ln_o_g, ln_o_b):
        import jax, jax.numpy as jnp
        import numpy as np
        DIM = 256
        HEADS = 16
        DIM_HEAD = 64
        INNER = HEADS * DIM_HEAD
        EPS = 1e-05

        def layernorm(t, g, b):
            mu = jnp.mean(t, axis=-1, keepdims=True)
            var = jnp.var(t, axis=-1, keepdims=True)
            return (t - mu) * jax.lax.rsqrt(var + EPS) * g + b
        b, n, _ = x.shape
        m = latents.shape[1]
        scale = DIM_HEAD ** (-0.5)
        xn = layernorm(x, ln_x_g, ln_x_b)
        ln = layernorm(latents, ln_l_g, ln_l_b)
        q = ln @ Wq
        kv_input = jnp.concatenate((xn, ln), axis=1)
        kv = kv_input @ Wkv
        k, v = jnp.split(kv, 2, axis=-1)

        def heads(t):
            return t.reshape(t.shape[0], t.shape[1], HEADS, DIM_HEAD).transpose(0, 2, 1, 3)
        q, k, v = (heads(q) * scale, heads(k), heads(v))
        sim = jnp.einsum('bhid,bhjd->bhij', q, k)
        mask_full = jnp.concatenate((mask, jnp.ones((b, m), dtype=bool)), axis=1)
        max_neg = -jnp.finfo(sim.dtype).max
        sim = jnp.where(mask_full[:, None, None, :], sim, max_neg)
        attn = jax.nn.softmax(sim.astype(jnp.float32), axis=-1).astype(sim.dtype)
        out = jnp.einsum('bhij,bhjd->bhid', attn, v)
        out = out.transpose(0, 2, 1, 3).reshape(b, m, INNER)
        out = out @ Wout
        return layernorm(out, ln_o_g, ln_o_b)

    def _L1_ffn_ref(hidden_states, gate_w1, gate_b1, gate_w2, gate_b2, W1, b1, W2, b2, TW1, Tb1, TW2, Tb2):
        import jax, jax.numpy as jnp
        import numpy as np
        B, S, H, F, E = (8, 512, 256, 1024, 8)
        INIT_LAMBDA = 0.2
        x = hidden_states
        h = jax.nn.relu(jnp.einsum('bsh,oh->bso', x, gate_w1) + gate_b1)
        g = jnp.einsum('bso,eo->bse', h, gate_w2) + gate_b2
        g = g.mean(axis=1)
        mW1 = W1 + jnp.einsum('be,efh->bfh', g, TW1)
        mb1 = b1 + g @ Tb1
        mW2 = W2 + jnp.einsum('be,ehf->bhf', g, TW2)
        mb2 = b2 + g @ Tb2
        u = jax.nn.gelu(jnp.einsum('bsh,bfh->bsf', x, mW1) + mb1[:, None, :])
        out = jnp.einsum('bsf,bhf->bsh', u, mW2) + mb2[:, None, :]
        return out

    def _L2_xattn_ref(q, k, v, Wq, bq, Wk, bk, Wv, bv):
        import jax, jax.numpy as jnp
        import numpy as np
        HIDDEN = 256
        B, S = (8, 512)
        query = jnp.einsum('bsd,de->bse', q, Wq) + bq
        key_p = jnp.einsum('bsd,de->bse', k, Wk) + bk
        value = jnp.einsum('bsd,de->bse', v, Wv) + bv
        d = key_p.shape[-1]
        inv_sqrt_d = 1.0 / jnp.sqrt(jnp.asarray(d, query.dtype))
        scores = jnp.einsum('bqd,bkd->bqk', query, key_p) * inv_sqrt_d
        attn = jax.nn.softmax(scores, axis=-1)
        context = jnp.einsum('bqk,bkd->bqd', attn, value)
        return context

    def _L2_ffn_ref(hidden_states, Wq, keys, down_embed, up_embed, Wg, Wu, Wd):
        import jax, jax.numpy as jnp
        import numpy as np
        HID = 256
        INTER = 1024
        RDIM = 128
        HEADS = 4
        NUM_EXPERTS = 4096
        NUM_KEYS = 128
        TOPK = 8
        B, T = (2, 512)
        b, t, _ = hidden_states.shape
        q = hidden_states @ Wq.T
        q = q.reshape(b, t, 2, HEADS, RDIM // 2)
        q = jnp.transpose(q, (2, 0, 1, 3, 4))
        sim = jnp.einsum('pbthn,hkpn->pbthk', q, keys)
        sx, ix = jax.lax.top_k(sim[0], TOPK)
        sy, iy = jax.lax.top_k(sim[1], TOPK)
        all_scores = (sx[..., :, None] + sy[..., None, :]).reshape(b, t, HEADS, TOPK * TOPK)
        all_indices = (ix[..., :, None] * NUM_KEYS + iy[..., None, :]).reshape(b, t, HEADS, TOPK * TOPK)
        scores, pk = jax.lax.top_k(all_scores, TOPK)
        indices = jnp.take_along_axis(all_indices, pk, axis=-1)
        down = down_embed[indices]
        up = up_embed[indices]
        w = jnp.einsum('btd,bthkd->bthk', hidden_states, down)
        w = jax.nn.silu(w) * jax.nn.softmax(scores, axis=-1)
        experts_states = jnp.einsum('bthk,bthkd->btd', w, up)
        mlp = jax.nn.silu(hidden_states @ Wg.T) * (hidden_states @ Wu.T) @ Wd.T
        return mlp + experts_states

    def _L3_xattn_ref(x, encoder_k, encoder_v, Wq1, bq1, Wk1, bk1, Wv1, bv1, Wo1, bo1, Wq2, bq2, Wk2, bk2, Wv2, bv2, Wo2, bo2):
        import jax, jax.numpy as jnp
        import numpy as np
        B, SD, SE, D, H = (4, 512, 512, 256, 16)
        HD = D // H

        def _mha(xq, xk, xv, Wq, bq, Wk, bk, Wv, bv, Wo, bo, causal):
            q = jnp.einsum('bsd,hde->bhse', xq, Wq) + bq[None, :, None, :]
            k = jnp.einsum('bsd,hde->bhse', xk, Wk) + bk[None, :, None, :]
            v = jnp.einsum('bsd,hde->bhse', xv, Wv) + bv[None, :, None, :]
            scale = 1.0 / jnp.sqrt(jnp.asarray(HD, q.dtype))
            scores = jnp.einsum('bhqe,bhke->bhqk', q, k) * scale
            if causal:
                mask = jnp.tril(jnp.ones((q.shape[2], k.shape[2]), bool))
                scores = jnp.where(mask, scores, jnp.finfo(scores.dtype).min)
            w = jax.nn.softmax(scores, axis=-1)
            out = jnp.einsum('bhqk,bhke->bhqe', w, v)
            out = out.transpose(0, 2, 1, 3).reshape(out.shape[0], out.shape[2], D)
            return out @ Wo + bo
        h = _mha(x, x, x, Wq1, bq1, Wk1, bk1, Wv1, bv1, Wo1, bo1, causal=True)
        out = _mha(h, encoder_k, encoder_v, Wq2, bq2, Wk2, bk2, Wv2, bv2, Wo2, bo2, causal=False)
        return out

    def _L3_ffn_ref(x, w_gate, w_up, w_down):
        import jax, jax.numpy as jnp
        import numpy as np
        HIDDEN = 256
        INNER = 1024

        def _weight_quant(w):
            scale = 1.0 / jnp.clip(jnp.mean(jnp.abs(w)), 1e-05)
            wq = jnp.clip(jnp.round(w * scale), -1.0, 1.0) / scale
            return w + jax.lax.stop_gradient(wq - w)

        def _act_quant(x):
            scale = 127.0 / jnp.clip(jnp.max(jnp.abs(x), axis=-1, keepdims=True), 1e-05)
            xq = jnp.clip(jnp.round(x * scale), -128.0, 127.0) / scale
            return x + jax.lax.stop_gradient(xq - x)

        def _bitlinear(x, w):
            return jnp.einsum('bsi,oi->bso', _act_quant(x), _weight_quant(w))
        gate = jax.nn.silu(_bitlinear(x, w_gate))
        up = _bitlinear(x, w_up)
        return _bitlinear(gate * up, w_down)
    x = x + jnp.tanh(g_xattn[0]) * _L0_xattn_ref(_layernorm(x, axis=-1), ctx_1024, L0_xattn_Wq, L0_xattn_Wkv, L0_xattn_W0)
    x = x + jnp.tanh(g_ffn[0]) * _L0_ffn_ref(_layernorm(x, axis=-1), L0_ffn_bn_gamma, L0_ffn_bn_beta, L0_ffn_w_q, L0_ffn_keys_p, L0_ffn_down, L0_ffn_up)
    x = x + jnp.tanh(g_xattn[1]) * _L1_xattn_ref(ctx_1024, _layernorm(x, axis=-1), mask_BxS2_bk0, L1_xattn_ln_x_g, L1_xattn_ln_x_b, L1_xattn_ln_l_g, L1_xattn_ln_l_b, L1_xattn_Wq, L1_xattn_Wkv, L1_xattn_Wout, L1_xattn_ln_o_g, L1_xattn_ln_o_b)
    x = x + jnp.tanh(g_ffn[1]) * _L1_ffn_ref(_layernorm(x, axis=-1), L1_ffn_gate_w1, L1_ffn_gate_b1, L1_ffn_gate_w2, L1_ffn_gate_b2, L1_ffn_W1, L1_ffn_b1, L1_ffn_W2, L1_ffn_b2, L1_ffn_TW1, L1_ffn_Tb1, L1_ffn_TW2, L1_ffn_Tb2)
    x = x + jnp.tanh(g_xattn[2]) * _L2_xattn_ref(_layernorm(x, axis=-1), ctx_1024, ctx_1024, L2_xattn_Wq, L2_xattn_bq, L2_xattn_Wk, L2_xattn_bk, L2_xattn_Wv, L2_xattn_bv)
    x = x + jnp.tanh(g_ffn[2]) * _L2_ffn_ref(_layernorm(x, axis=-1), L2_ffn_Wq, L2_ffn_keys, L2_ffn_down_embed, L2_ffn_up_embed, L2_ffn_Wg, L2_ffn_Wu, L2_ffn_Wd)
    x = x + jnp.tanh(g_xattn[3]) * _L3_xattn_ref(_layernorm(x, axis=-1), ctx_1024, ctx_1024, L3_xattn_Wq1, L3_xattn_bq1, L3_xattn_Wk1, L3_xattn_bk1, L3_xattn_Wv1, L3_xattn_bv1, L3_xattn_Wo1, L3_xattn_bo1, L3_xattn_Wq2, L3_xattn_bq2, L3_xattn_Wk2, L3_xattn_bk2, L3_xattn_Wv2, L3_xattn_bv2, L3_xattn_Wo2, L3_xattn_bo2)
    x = x + jnp.tanh(g_ffn[3]) * _L3_ffn_ref(_layernorm(x, axis=-1), L3_ffn_w_gate, L3_ffn_w_up, L3_ffn_w_down)
    return x

_drawn_inputs = setup_inputs


def setup_inputs(seed=0):
    import zlib

    import numpy as np

    out = dict(_drawn_inputs(seed))
    spreads = {'L0_ffn_bn_gamma': (1.0, 0.6),
     'L0_ffn_bn_beta': (0.0, 0.8),
     'L1_xattn_ln_x_g': (1.0, 0.6),
     'L1_xattn_ln_x_b': (0.0, 0.8),
     'L1_xattn_ln_l_g': (1.0, 0.2),
     'L1_xattn_ln_l_b': (0.0, 0.1),
     'L1_xattn_ln_o_g': (1.0, 0.2),
     'L1_xattn_ln_o_b': (0.0, 0.1),
     'L1_ffn_gate_b1': (0.0, 0.8),
     'L1_ffn_gate_b2': (0.20000000298023224, 0.6),
     'L2_xattn_bq': (0.0, 0.689),
     'L2_xattn_bk': (0.0, 0.8),
     'L2_xattn_bv': (0.0, 0.1),
     'L3_xattn_bq1': (0.0, 0.8),
     'L3_xattn_bk1': (0.0, 0.8),
     'L3_xattn_bv1': (0.0, 0.653),
     'L3_xattn_bo1': (0.0, 0.728),
     'L3_xattn_bq2': (0.0, 0.668),
     'L3_xattn_bk2': (0.0, 0.8),
     'L3_xattn_bv2': (0.0, 0.1),
     'L3_xattn_bo2': (0.0, 0.1)}
    factors = {'g_ffn': 8.0,
     'L0_xattn_Wq': 8.0,
     'L0_ffn_w_q': 8.0,
     'L0_ffn_keys_p': 8.0,
     'L0_ffn_down': 8.0,
     'L0_ffn_up': 8.0,
     'L1_ffn_gate_w1': 8.0,
     'L1_ffn_gate_w2': 8.0,
     'L1_ffn_b1': 8.0,
     'L1_ffn_b2': 4.011,
     'L1_ffn_Tb1': 8.0,
     'L1_ffn_Tb2': 6.822,
     'L2_ffn_Wq': 8.0,
     'L2_ffn_keys': 8.0,
     'L2_ffn_down_embed': 8.0,
     'L2_ffn_up_embed': 8.0,
     'L3_xattn_Wq1': 8.0,
     'L3_xattn_Wk1': 8.0}
    for name, (base, spread) in spreads.items():
        noise = np.random.default_rng([zlib.crc32(name.encode()), seed]).standard_normal(out[name].shape)
        drawn = base * np.exp(spread * noise) if base else spread * noise
        out[name] = jnp.asarray(drawn.astype(out[name].dtype))
    for name, factor in factors.items():
        out[name] = (out[name] * factor).astype(out[name].dtype)
    return out
```

```python
from contextlib import ExitStack

import numpy as np

import concourse.bass as bass
from concourse import mybir

F32 = mybir.dt.float32
BF16 = mybir.dt.bfloat16
U32 = mybir.dt.uint32
I32 = mybir.dt.int32
U8 = mybir.dt.uint8
ALU = mybir.AluOpType
ACT = mybir.ActivationFunctionType
AX = mybir.AxisListType

P = 128
B, S, D = 4, 1024, 256
NT = B * S // P
TB = S // P
DC = D // P
SC = 77
CT = B * SC
EPS = 1e-5
MASKED = -1e30
ROUND = 1.5 * 2.0 ** 23


class Core:

    def __init__(self, nc, stack):
        self.nc = nc
        self.stack = stack
        self.x = stack.enter_context(nc.sbuf_tensor("x_res", [P, NT, D], F32))
        self.mean = stack.enter_context(nc.sbuf_tensor("row_mean", [P, NT], F32))
        self.rstd = stack.enter_context(nc.sbuf_tensor("row_rstd", [P, NT], F32))
        self.ident = stack.enter_context(nc.sbuf_tensor("ident", [P, P], F32))
        self.ones = stack.enter_context(nc.sbuf_tensor("ones_row", [1, P], F32))
        self.ctxT = stack.enter_context(nc.sbuf_tensor("ctxT", [P, DC, CT], F32))
        self.gates = stack.enter_context(nc.sbuf_tensor("gates", [P, 2, 4], F32))

        self.sems = []

    def sem(self, name):
        self.sems.append(self.nc.alloc_semaphore(name=name))
        return self.sems[-1]

    def end_layer(self):
        self.nc.clear_and_free_semaphores(self.sems)
        self.nc.all_engine_barrier()
        self.sems = []


class Stage:

    def __init__(self, core, tag, stack):
        self.core, self.tag, self.stack = core, tag, stack

    def sb(self, name, shape, dt=F32):
        return self.stack.enter_context(self.core.nc.sbuf_tensor(f"{self.tag}_{name}", shape, dt))

    def ps(self, name, shape, dt=F32):
        return self.stack.enter_context(self.core.nc.psum_tensor(f"{self.tag}_{name}", shape, dt))

    def sem(self, name):
        return self.core.sem(f"{self.tag}_{name}")


def load_inputs(core, A):
    nc = core.nc
    with ExitStack() as stack:
        st = Stage(core, "in", stack)
        loaded, ready = st.sem("loaded"), st.sem("ready")
        block = stack.enter_context(nc.Block())

        @block.sync
        def _(sp):
            sp.dma_start(core.x[:, :, :], A["x"].rearrange("b (n p) d -> p (b n) d", p=P)).then_inc(loaded, 16)
            sp.dma_start(core.ident[:, :], A["ident"]).then_inc(loaded, 16)
            sp.dma_start(core.ctxT[:, :, :], A["ctxT"].rearrange("(c p) t -> p c t", p=P)).then_inc(loaded, 16)
            sp.dma_start(core.gates[:, :, :], A["gates"]).then_inc(loaded, 16)
            sp.wait_ge(loaded, 64)

        @block.vector
        def _(dve):
            dve.memset(core.ones[:, :], 1.0)

        @block.scalar
        def _(act):
            act.wait_ge(loaded, 64)
            act.activation(core.gates[:, :, :], core.gates[:, :, :], ACT.Tanh).then_inc(ready, 1)
            act.wait_ge(ready, 1)


def row_stats(core, tag, twice=False):
    nc = core.nc
    with ExitStack() as stack:
        st = Stage(core, tag, stack)
        stats = st.sb("stats", [P, NT, 6])
        var = st.sb("var", [P, NT])
        tmp = st.sb("tmp", [P, NT])
        std = st.sb("std", [P, NT])
        var_ready, std_ready = st.sem("var_ready"), st.sem("std_ready")
        block = stack.enter_context(nc.Block())

        @block.vector
        def _(dve):
            with dve.Fori(0, NT) as t:
                dve.bn_stats(stats[:, t, :], core.x[:, t, :])
            dve.drain()
            dve.tensor_tensor(core.mean[:, :], stats[:, :, 1], stats[:, :, 4], ALU.add)
            dve.tensor_tensor(tmp[:, :], stats[:, :, 1], stats[:, :, 4], ALU.subtract)
            dve.tensor_tensor(var[:, :], stats[:, :, 2], stats[:, :, 5], ALU.add)
            dve.drain()
            dve.tensor_scalar(core.mean[:, :], core.mean[:, :], 0.5, None, ALU.mult)
            dve.tensor_tensor(tmp[:, :], tmp[:, :], tmp[:, :], ALU.mult)
            dve.tensor_scalar(var[:, :], var[:, :], 1.0 / D, None, ALU.mult)
            dve.drain()
            dve.tensor_scalar(tmp[:, :], tmp[:, :], 0.25, None, ALU.mult)
            dve.drain()
            dve.tensor_tensor(var[:, :], var[:, :], tmp[:, :], ALU.add)
            dve.drain()
            dve.tensor_scalar(tmp[:, :], var[:, :], EPS, None, ALU.add).then_inc(var_ready, 1)
            dve.wait_ge(std_ready, 1)
            dve.reciprocal(core.rstd[:, :], std[:, :])
            if twice:
                dve.drain()
                dve.tensor_tensor(tmp[:, :], core.rstd[:, :], core.rstd[:, :], ALU.mult)
                dve.drain()
                dve.tensor_tensor(tmp[:, :], tmp[:, :], var[:, :], ALU.mult)
                dve.drain()
                dve.tensor_scalar(tmp[:, :], tmp[:, :], EPS, None, ALU.add).then_inc(var_ready, 1)
                dve.wait_ge(std_ready, 2)
                dve.reciprocal(tmp[:, :], std[:, :])
                dve.drain()
                dve.tensor_tensor(core.rstd[:, :], core.rstd[:, :], tmp[:, :], ALU.mult)

        @block.scalar
        def _(act):
            act.wait_ge(var_ready, 1)
            act.activation(std[:, :], tmp[:, :], ACT.Sqrt).then_inc(std_ready, 1)
            if twice:
                act.wait_ge(var_ready, 2)
                act.activation(std[:, :], tmp[:, :], ACT.Sqrt).then_inc(std_ready, 1)


def normalise(dve, core, out, t):
    return dve.tensor_scalar(out, core.x[:, t, :], core.mean[:, bass.ds(t, 1)], core.rstd[:, bass.ds(t, 1)],
                             ALU.subtract, ALU.mult)


def cross_prep(core, tag, A, nh, hd, M, n_dram, biased, cM=None):
    nc = core.nc
    with ExitStack() as stack:
        st = Stage(core, tag, stack)
        wk = st.sb("wk", [P, DC, nh * hd])
        wv = st.sb("wv", [P, DC, nh * hd])
        wq = st.sb("wq", [hd, nh, D])
        wo = st.sb("wo", [hd, nh, D])
        kT = st.sb("kT", [hd, CT])
        vT = st.sb("vT", [hd, CT])
        Nst = st.sb("Nst", [SC, B, D])
        bias = st.sb("bias", [hd, 3, nh])
        k_ps = st.ps("k_ps", [hd, CT])
        v_ps = st.ps("v_ps", [hd, CT])
        m_ps = st.ps("m_ps", [P, DC, 512])
        n_ps = st.ps("n_ps", [SC, B, D])
        c_ps = st.ps("c_ps", [1, CT])
        loaded = st.sem("loaded")
        kv_ready = st.sem("kv_ready")
        kT_ready = st.sem("kT_ready")
        vT_ready = st.sem("vT_ready")
        mn_ready = st.sem("mn_ready")
        m_done = st.sem("m_done")
        n_done = st.sem("n_done")
        n_stored = st.sem("n_stored")
        nload = 4 + biased
        block = stack.enter_context(nc.Block())

        @block.sync
        def _(sp):
            sp.dma_start(wk[:, :, :], A["wk"].rearrange("(c p) e -> p c e", p=P)).then_inc(loaded, 16)
            sp.dma_start(wv[:, :, :], A["wv"].rearrange("(c p) e -> p c e", p=P)).then_inc(loaded, 16)
            sp.dma_start(wq[:, :, :], A["wq"]).then_inc(loaded, 16)
            sp.dma_start(wo[:, :, :], A["wo"]).then_inc(loaded, 16)
            if biased:
                sp.dma_start(bias[:, :, :], A["bias"]).then_inc(loaded, 16)
            for h in range(nh):
                sp.wait_ge(n_done, h + 1)
                sp.dma_start(n_dram[:, h * SC:(h + 1) * SC, :].rearrange("b j o -> j b o"), Nst[:, :, :]).then_inc(n_stored, 16)
            sp.wait_ge(n_stored, 16 * nh)

        @block.tensor
        def _(pe):
            pe.wait_ge(loaded, 16 * nload)
            for h in range(nh):
                e = slice(h * hd, (h + 1) * hd)
                if h:
                    pe.wait_ge(kT_ready, h)
                    pe.wait_ge(vT_ready, h)
                for w, ps in ((wk, k_ps), (wv, v_ps)):
                    for c in range(DC):
                        mm = pe.matmul(ps[:, :], w[:, c, e], core.ctxT[:, c, :], start=(c == 0), stop=(c == DC - 1))
                mm.then_inc(kv_ready, 1)
                pe.wait_ge(kT_ready, h + 1)
                pe.wait_ge(vT_ready, h + 1)
                if h:
                    pe.wait_ge(m_done, h)
                    pe.wait_ge(n_done, h)
                for c in range(DC):
                    pe.matmul(m_ps[:, c, 0:CT], wq[:, h, c * P:(c + 1) * P], kT[:, :], start=True, stop=True)
                if biased:
                    pe.matmul(c_ps[:, :], bias[:, 0, h:h + 1], kT[:, :], start=True, stop=True)
                for b in range(B):
                    mm = pe.matmul(n_ps[:, b, :], vT[:, b * SC:(b + 1) * SC], wo[:, h, :], start=True, stop=True)
                mm.then_inc(mn_ready, 1)

        @block.scalar
        def _(act):
            for h in range(nh):
                act.wait_ge(kv_ready, h + 1)
                if h:
                    act.wait_ge(mn_ready, h)
                if biased:
                    act.activation(kT[:, :], k_ps[:, :], ACT.Identity, bias=bias[:, 1, h:h + 1]).then_inc(kT_ready, 1)
                else:
                    act.copy(kT[:, :], k_ps[:, :]).then_inc(kT_ready, 1)
                act.wait_ge(mn_ready, h + 1)
                for c in range(DC):
                    cp = act.copy(M[:, c, :, h * SC:(h + 1) * SC], m_ps[:, c, 0:CT].rearrange("p (b j) -> p b j", b=B))
                cp.then_inc(m_done, 1)

        @block.vector
        def _(dve):
            for h in range(nh):
                dve.wait_ge(kv_ready, h + 1)
                if h:
                    dve.wait_ge(mn_ready, h)
                if biased:
                    dve.tensor_scalar(vT[:, :], v_ps[:, :], bias[:, 2, h:h + 1], None, ALU.add).then_inc(vT_ready, 1)
                else:
                    dve.tensor_copy(vT[:, :], v_ps[:, :]).then_inc(vT_ready, 1)
                dve.wait_ge(mn_ready, h + 1)
                if h:
                    dve.wait_ge(n_stored, 16 * h)
                if biased:
                    dve.tensor_copy(cM[:, :, h * SC:(h + 1) * SC], c_ps[:, :].rearrange("p (b j) -> p b j", b=B))
                dve.tensor_copy(Nst[:, :, :], n_ps[:, :, :]).then_inc(n_done, 1)


def cross_attend(core, tag, nh, M, N, scale, gate, src=None, cM=None, out_row=None, guard=False):
    nc = core.nc
    W = nh * SC
    chunks = -(-W // P)
    groups = [list(range(k, min(k + 4, chunks))) for k in range(0, chunks, 4)]
    ngr = len(groups)
    cuts = [(a, min(a + 512, W)) for a in range(0, W, 512)]
    with ExitStack() as stack:
        st = Stage(core, tag, stack)
        hn = st.sb("hn", [P, D])
        hT = st.sb("hT", [P, DC, P])
        E = st.sb("E", [P, nh, SC])
        Pn = st.sb("Pn", [P, chunks * P])
        PT = st.sb("PT", [P, chunks, P])
        mx = st.sb("mx", [P, nh])
        l = st.sb("l", [P, nh])
        h_ps = st.ps("h_ps", [P, DC, P])
        s_ps = st.ps("s_ps", [P, 512 * len(cuts)])
        pt_ps = [st.ps(f"pt_ps{i}", [P, 4, P]) for i in range(2)]
        o_ps = st.ps("o_ps", [P, D])
        hn_ready = st.sem("hn_ready")
        ht_ready = st.sem("ht_ready")
        hT_ready = st.sem("hT_ready")
        s_ready = st.sem("s_ready")
        e_ready = st.sem("e_ready")
        exp_done = st.sem("exp_done")
        p_ready = st.sem("p_ready")
        pt_ready = st.sem("pt_ready")
        pT_ready = st.sem("pT_ready")
        o_ready = st.sem("o_ready")
        x_done = st.sem("x_done")
        block = stack.enter_context(nc.Block())
        s3 = s_ps[:, 0:W].rearrange("p (h j) -> p h j", h=nh)
        p3 = Pn[:, 0:W].rearrange("p (h j) -> p h j", h=nh)

        @block.vector
        def _(dve):
            def front(t, first=False):
                if not first:
                    dve.wait_ge(ht_ready, t)
                if src is None:
                    normalise(dve, core, hn[:, :], t).then_inc(hn_ready, 1)
                else:
                    dve.tensor_copy(hn[:, :], src[:, t, :]).then_inc(hn_ready, 1)
                dve.wait_ge(s_ready, t + 1)
                dve.tensor_reduce(mx[:, :], s3, AX.X, ALU.max)
                dve.drain()
                dve.tensor_tensor(E[:, :, :], s3, mx[:, :].unsqueeze(2).to_broadcast([P, nh, SC]),
                                  ALU.subtract).then_inc(e_ready, 1)
                dve.wait_ge(exp_done, t + 1)
                dve.tensor_reduce(l[:, :], E[:, :, :], AX.X, ALU.add)
                dve.drain()
                dve.reciprocal(l[:, :], l[:, :])
                dve.drain()
                if not first:
                    dve.wait_ge(pt_ready, t * ngr)
                if guard:
                    dve.tensor_scalar(l[:, :], l[:, :], 0.0, None, ALU.max)
                    dve.drain()
                    dve.scalar_tensor_tensor(p3, E[:, :, :], 0.0, l[:, :].unsqueeze(2).to_broadcast([P, nh, SC]),
                                             ALU.max, ALU.mult).then_inc(p_ready, 1)
                else:
                    dve.tensor_tensor(p3, E[:, :, :], l[:, :].unsqueeze(2).to_broadcast([P, nh, SC]),
                                      ALU.mult).then_inc(p_ready, 1)

            def back(t):
                dve.wait_ge(o_ready, t + 1)
                dve.scalar_tensor_tensor(core.x[:, t, :], o_ps[:, :], gate, core.x[:, t, :],
                                         ALU.mult, ALU.add).then_inc(x_done, 1)

            dve.sem_inc(x_done, 1)
            if W % P:
                dve.memset(Pn[:, W:chunks * P], 0.0)
            front(0, first=True)
            with dve.Fori(1, NT) as t:
                front(t)
                back(t - 1)
            back(NT - 1)

        @block.scalar
        def _(act):
            def front(t, first=False):
                act.wait_ge(ht_ready, t + 1)
                if not first:
                    act.wait_ge(s_ready, t)
                act.copy(hT[:, :, :], h_ps[:, :, :]).then_inc(hT_ready, 1)
                act.wait_ge(e_ready, t + 1)
                act.activation(E[:, :, :], E[:, :, :], ACT.Exp, scale=scale).then_inc(exp_done, 1)

            def back(t):
                for g, ks in enumerate(groups):
                    act.wait_ge(pt_ready, t * ngr + g + 1)
                    act.copy(PT[:, ks[0]:ks[-1] + 1, :], pt_ps[g % 2][:, 0:len(ks), :]).then_inc(pT_ready, 1)

            front(0, first=True)
            with act.Fori(1, NT) as t:
                front(t)
                back(t - 1)
            back(NT - 1)

        @block.tensor
        def _(pe):
            def front(t, first=False):
                pe.wait_ge(hn_ready, t + 1)
                for c in range(DC):
                    mm = pe.transpose(h_ps[:, c, :], hn[:, c * P:(c + 1) * P], core.ident[:, :])
                mm.then_inc(ht_ready, 1)
                pe.wait_ge(hT_ready, t + 1)
                if not first:
                    pe.wait_ge(e_ready, t)
                b = t // TB
                for a, z in cuts:
                    for c in range(DC):
                        mm = pe.matmul(s_ps[:, a:z], hT[:, c, :], M[:, c, b, a:z], start=(c == 0),
                                       stop=(c == DC - 1 and cM is None))
                    if cM is not None:
                        mm = pe.matmul(s_ps[:, a:z], core.ones[:, :], cM[:, b, a:z], start=False, stop=True)
                mm.then_inc(s_ready, 1)

            def back(t):
                pe.wait_ge(p_ready, t + 1)
                for g, ks in enumerate(groups):
                    if g >= 2:
                        pe.wait_ge(pT_ready, t * ngr + g - 1)
                    for i, k in enumerate(ks):
                        mm = pe.transpose(pt_ps[g % 2][:, i, :], Pn[:, k * P:(k + 1) * P], core.ident[:, :])
                    mm.then_inc(pt_ready, 1)
                pe.wait_ge(pT_ready, t * ngr + ngr)
                pe.wait_ge(x_done, t + 1)
                b = t // TB
                for k in range(chunks):
                    mm = pe.matmul(o_ps[:, :], PT[:, k, :], N[:, b, k, :], start=(k == 0),
                                   stop=(k == chunks - 1 and out_row is None))
                if out_row is not None:
                    mm = pe.matmul(o_ps[:, :], core.ones[:, :], out_row, start=False, stop=True)
                mm.then_inc(o_ready, 1)

            front(0, first=True)
            with pe.Fori(1, NT) as t:
                front(t)
                back(t - 1)
            back(NT - 1)


def store_output(core, out):
    nc = core.nc
    with ExitStack() as stack:
        st = Stage(core, "out", stack)
        stored = st.sem("stored")
        block = stack.enter_context(nc.Block())

        @block.sync
        def _(sp):
            sp.dma_start(out.rearrange("b (n p) d -> p (b n) d", p=P), core.x[:, :, :]).then_inc(stored, 16)
            sp.wait_ge(stored, 16)


def layer0_xattn(core, A):
    nh, hd = 16, 64
    W = nh * SC
    with ExitStack() as stack:
        st = Stage(core, "L0x", stack)
        M = st.sb("M", [P, DC, B, W])
        n_dram = core.nc.dram_tensor("L0x_n_dram", (B, W, D), F32, kind="Internal").ap()
        cross_prep(core, "L0p", {k: A["L0_" + k] for k in ("wk", "wv", "wq", "wo")}, nh, hd, M, n_dram, False)
        N = st.sb("N", [P, B, -(-W // P), D])
        load_packed(core, "L0n", n_dram, N, W)
        row_stats(core, "L0s")
        cross_attend(core, "L0a", nh, M, N, hd ** -0.5, core.gates[:, 0, 0:1], guard=True)


def zero_tail(core, tag, tail):
    nc = core.nc
    with ExitStack() as stack:
        block = stack.enter_context(nc.Block())

        @block.vector
        def _(dve):
            dve.memset(tail, 0.0)


def load_packed(core, tag, n_dram, N, W):
    nc = core.nc
    full, rest = W // P, W % P
    zero_tail(core, tag + "z", N[:, :, full, :])
    with ExitStack() as stack:
        st = Stage(core, tag, stack)
        loaded = st.sem("loaded")
        block = stack.enter_context(nc.Block())

        @block.sync
        def _(sp):
            for b in range(B):
                sp.dma_start(N[:, b, 0:full, :], n_dram[b, 0:full * P, :].rearrange("(c p) o -> p c o", p=P)).then_inc(loaded, 16)
                sp.dma_start(N[0:rest, b, full, :], n_dram[b, full * P:W, :]).then_inc(loaded, 16)
            sp.wait_ge(loaded, 16 * B * 2)


def batch_norm_stats(core, tag, A, bn_scale, bn_bias):
    nc = core.nc
    with ExitStack() as stack:
        st = Stage(core, tag, stack)
        hn = [st.sb(f"hn{u}", [P, D]) for u in range(2)]
        stats = st.sb("stats", [P, DC, NT // 2, 6])
        mv = st.sb("mv", [P, DC, 2])
        gb = st.sb("gb", [P, 2, DC])
        ve = st.sb("ve", [P, DC])
        h_ps = [st.ps(f"h_ps{u}", [P, DC, 2, P]) for u in range(2)]
        loaded = st.sem("loaded")
        hn_ready = st.sem("hn_ready")
        ht_ready = st.sem("ht_ready")
        ht_used = st.sem("ht_used")
        var_ready, std_ready = st.sem("var_ready"), st.sem("std_ready")
        block = stack.enter_context(nc.Block())

        @block.sync
        def _(sp):
            sp.dma_start(gb[:, :, :], A["bn"]).then_inc(loaded, 16)

        @block.vector
        def _(dve):
            dve.sem_inc(ht_used, 1)
            with dve.Fori(0, NT // 2) as k:
                for u in range(2):
                    dve.wait_ge(ht_ready, 2 * k + u + 1)
                    normalise(dve, core, hn[u][:, :], 2 * k + u).then_inc(hn_ready, 1)
                dve.wait_ge(ht_ready, 2 * k + 4)
                for c in range(DC):
                    bn = dve.bn_stats(stats[:, c, k, :], h_ps[0][:, c, :, :])
                bn.then_inc(ht_used, 1)
            dve.drain()
            for c in range(DC):
                dve.bn_aggr(mv[:, c, :], stats[:, c, :, :])
            dve.drain()
            dve.tensor_scalar(ve[:, :], mv[:, :, 1], EPS, None, ALU.add).then_inc(var_ready, 1)
            dve.wait_ge(std_ready, 1)
            dve.reciprocal(ve[:, :], ve[:, :])
            dve.drain()
            dve.wait_ge(loaded, 16)
            dve.tensor_tensor(bn_scale, ve[:, :], gb[:, 0, :], ALU.mult)
            dve.drain()
            dve.tensor_tensor(ve[:, :], mv[:, :, 0], bn_scale, ALU.mult)
            dve.drain()
            dve.tensor_tensor(bn_bias, gb[:, 1, :], ve[:, :], ALU.subtract)

        @block.tensor
        def _(pe):
            pe.sem_inc(ht_ready, 2)
            with pe.Fori(0, NT // 2) as k:
                pe.wait_ge(ht_used, k + 1)
                for u in range(2):
                    pe.wait_ge(hn_ready, 2 * k + u + 1)
                    for c in range(DC):
                        mm = pe.transpose(h_ps[0][:, c, u, :], hn[u][:, c * P:(c + 1) * P], core.ident[:, :])
                    mm.then_inc(ht_ready, 1)

        @block.scalar
        def _(act):
            act.wait_ge(var_ready, 1)
            act.activation(ve[:, :], ve[:, :], ACT.Sqrt).then_inc(std_ready, 1)


def fold_keys(core, tag, A, groups, hd, nk, G):
    nc = core.nc
    with ExitStack() as stack:
        st = Stage(core, tag, stack)
        wq = st.sb("wq", [hd, groups, D])
        keys = st.sb("keys", [hd, groups, nk])
        g_ps = [st.ps(f"g_ps{u}", [P, DC, nk]) for u in range(2)]
        loaded, g_ready, g_done = st.sem("loaded"), st.sem("g_ready"), st.sem("g_done")
        block = stack.enter_context(nc.Block())

        @block.sync
        def _(sp):
            sp.dma_start(wq[:, :, :], A["wq"]).then_inc(loaded, 16)
            sp.dma_start(keys[:, :, :], A["keys"]).then_inc(loaded, 16)

        @block.tensor
        def _(pe):
            pe.wait_ge(loaded, 32)
            for g in range(groups):
                if g >= 2:
                    pe.wait_ge(g_done, g - 1)
                for c in range(DC):
                    mm = pe.matmul(g_ps[g % 2][:, c, :], wq[:, g, c * P:(c + 1) * P], keys[:, g, :], start=True, stop=True)
                mm.then_inc(g_ready, 1)

        @block.scalar
        def _(act):
            for g in range(groups):
                act.wait_ge(g_ready, g + 1)
                act.copy(G[:, :, g * nk:(g + 1) * nk], g_ps[g % 2][:, :, :]).then_inc(g_done, 1)


def product_key_experts(core, tag, table, nh, nk, G, gate, last_expert=None, bn=None, soft=False):
    nc = core.nc
    groups = 2 * nh
    K = 8
    NE = nh * K
    NC = NE // K
    RC = 4
    assert NC % RC == 0 and groups * nk == 1024
    with ExitStack() as stack:
        st = Stage(core, tag, stack)
        hn = [st.sb(f"hn{u}", [P, D]) for u in range(2)]
        hT = st.sb("hT", [P, DC, P])
        val = st.sb("val", [P, groups, K])
        pos = st.sb("pos", [P, groups, K], U32)
        posf = st.sb("posf", [P, groups, K])
        sums = st.sb("sums", [P, nh, K, K])
        top = [st.sb(f"top{u}", [P, nh, K]) for u in range(2)]
        pick = st.sb("pick", [P, nh, K], U32)
        half = st.sb("half", [P, 2, nh * K], U32)
        halff = st.sb("halff", [P, 2, nh * K])
        count = st.sb("count", [P, K])
        hot = st.sb("hot", [P, 2, nh * K, K])
        chosen = st.sb("chosen", [P, 2, nh * K])
        idx = [st.sb(f"idx{u}", [P, NE], U32) for u in range(2)]
        weigh = [st.sb(f"weigh{u}", [P, NE]) for u in range(2)]
        total = st.sb("total", [P, nh])
        ring = st.sb("ring", [P, RC * K, 2 * D])
        dot = st.sb("dot", [P, NE])
        mid = st.sb("mid", [P, NE])
        w = st.sb("w", [P, NE])
        diag = st.sb("diag", [P, 2, K, P])
        h_ps = st.ps("h_ps", [P, DC, P])
        s_ps = st.ps("s_ps", [P, 2, 512])
        o_ps = [st.ps(f"o_ps{u}", [P, D]) for u in range(2)]
        hn_ready = st.sem("hn_ready")
        ht_ready = st.sem("ht_ready")
        hT_ready = st.sem("hT_ready")
        s_ready = st.sem("s_ready")
        s_used = st.sem("s_used")
        top_ready = st.sem("top_ready")
        idx_ready = st.sem("idx_ready")
        weigh_ready = st.sem("weigh_ready")
        gathered = [st.sem(f"gathered{i}") for i in range(RC)]
        dots_ready = st.sem("dots_ready")
        act_done = st.sem("act_done")
        w_ready = st.sem("w_ready")
        diag_ready = st.sem("diag_ready")
        up_done = st.sem("up_done")
        x_done = st.sem("x_done")
        counted = st.sem("counted")
        pool_steps, dve_steps = st.sem("pool_steps"), st.sem("dve_steps")
        block = stack.enter_context(nc.Block())
        s2 = s_ps[:, :, :].rearrange("p a b -> p (a b)")

        def run(front, experts):
            def body(k, eng):
                front(2 * k + 1, 1)
                experts(2 * k, 0)
                front(2 * k + 2, 0)
                experts(2 * k + 1, 1)

            def go(eng):
                front(0, 0)
                with eng.Fori(0, NT // 2 - 1) as k:
                    body(k, eng)
                front(NT - 1, 1)
                experts(NT - 2, 0)
                experts(NT - 1, 1)
            return go

        @block.gpsimd
        def _(pool):
            pool.iota(count[:, :], [[1, K]], base=0, channel_multiplier=0,
                      allow_small_or_imprecise_dtypes=True).then_inc(counted, 1)

            def front(t, u):
                pass

            def experts(t, u):
                pool.wait_ge(idx_ready, t + 1)
                for c in range(NC):
                    pool.wait_ge(up_done, t * NC + c + 1)
                    pool.sem_inc(pool_steps, 1)
                    for i in range(K):
                        e = c * K + i
                        pool.indirect_dma_start(ring[:, (c % RC) * K + i, :], None, table,
                                                bass.IndirectOffsetOnAxis(ap=idx[u][:, e:e + 1], axis=0)
                                                ).then_inc(gathered[c % RC], 16)

            run(front, experts)(pool)

        @block.vector
        def _(dve):
            def front(t, u):
                normalise(dve, core, hn[u][:, :], t).then_inc(hn_ready, 1)
                dve.wait_ge(s_ready, t + 1)
                dve.sem_inc(dve_steps, 1)
                for g in range(groups):
                    dve.max(val[:, g, :], s2[:, g * nk:(g + 1) * nk])
                dve.drain()
                for g in range(groups):
                    dve.max_index(pos[:, g, :], val[:, g, :], s2[:, g * nk:(g + 1) * nk])
                dve.drain().then_inc(s_used, 1)
                dve.tensor_copy(posf[:, :, :], pos[:, :, :])
                dve.tensor_tensor(sums[:, :, :, :], val[:, 0:nh, :].unsqueeze(3).to_broadcast([P, nh, K, K]),
                                  val[:, nh:groups, :].unsqueeze(2).to_broadcast([P, nh, K, K]), ALU.add)
                dve.drain()
                for h in range(nh):
                    dve.max(top[u][:, h, :], sums[:, h, :, :])
                dve.drain()
                for h in range(nh):
                    dve.max_index(pick[:, h, :], top[u][:, h, :], sums[:, h, :, :].rearrange("p i j -> p (i j)"))
                dve.drain()
                if soft:
                    dve.tensor_tensor(weigh[u][:, :].rearrange("p (h k) -> p h k", k=K), top[u][:, :, :],
                                      top[u][:, :, 0:1].to_broadcast([P, nh, K]), ALU.subtract).then_inc(top_ready, 1)
                else:
                    dve.sem_inc(top_ready, 1)
                flat = pick[:, :, :].rearrange("p h k -> p (h k)")
                dve.tensor_scalar(half[:, 0, :], flat, 3, None, ALU.logical_shift_right)
                dve.tensor_scalar(half[:, 1, :], flat, K - 1, None, ALU.bitwise_and)
                dve.drain()
                dve.tensor_copy(halff[:, :, :], half[:, :, :])
                dve.drain()
                for p in range(2):
                    dve.tensor_tensor(hot[:, p, :, :], halff[:, p, :].unsqueeze(2).to_broadcast([P, nh * K, K]),
                                      count[:, :].unsqueeze(1).to_broadcast([P, nh * K, K]), ALU.is_equal)
                dve.drain()
                for p in range(2):
                    hot4 = hot[:, p, :, :].rearrange("p (h k) i -> p h k i", k=K)
                    dve.tensor_tensor(hot4, hot4, posf[:, p * nh:(p + 1) * nh, :].unsqueeze(2).to_broadcast([P, nh, K, K]),
                                      ALU.mult)
                dve.drain()
                dve.tensor_reduce(chosen[:, :, :], hot[:, :, :, :], AX.X, ALU.add)
                dve.drain()
                if last_expert is None:
                    dve.scalar_tensor_tensor(idx[u][:, :], chosen[:, 0, :], float(nk), chosen[:, 1, :],
                                             ALU.mult, ALU.add).then_inc(idx_ready, 1)
                else:
                    dve.scalar_tensor_tensor(chosen[:, 0, :], chosen[:, 0, :], float(nk), chosen[:, 1, :], ALU.mult, ALU.add)
                    dve.drain()
                    dve.tensor_scalar(idx[u][:, :], chosen[:, 0, :], float(last_expert), None, ALU.min).then_inc(idx_ready, 1)
                if soft:
                    dve.wait_ge(weigh_ready, t + 1)
                    w3 = weigh[u][:, :].rearrange("p (h k) -> p h k", k=K)
                    dve.tensor_reduce(total[:, :], w3, AX.X, ALU.add)
                    dve.drain()
                    dve.reciprocal(total[:, :], total[:, :])
                    dve.drain()
                    dve.tensor_tensor(w3, w3, total[:, :].unsqueeze(2).to_broadcast([P, nh, K]), ALU.mult)

            def weights(t, u, c):
                e = slice(c * K, (c + 1) * K)
                dve.wait_ge(act_done, t * NC + c + 1)
                dve.tensor_tensor(w[:, e], mid[:, e], weigh[u][:, e], ALU.mult).then_inc(w_ready, 1)

            def experts(t, u):
                for c in range(NC):
                    dve.wait_ge(gathered[c % RC], 16 * K * (t * (NC // RC) + c // RC + 1))
                    for i in range(K):
                        e = c * K + i
                        down = ring[:, (c % RC) * K + i, 0:D]
                        tr = dve.tensor_tensor_reduce(down, down, hn[u][:, :], 1.0, 0.0,
                                                      ALU.mult, ALU.add, dot[:, e:e + 1])
                    tr.then_inc(dots_ready, 1)
                    if c:
                        weights(t, u, c - 1)
                weights(t, u, NC - 1)
                dve.wait_ge(up_done, (t + 1) * NC + RC)
                dve.scalar_tensor_tensor(core.x[:, t, :], o_ps[u][:, :], gate, core.x[:, t, :],
                                         ALU.mult, ALU.add).then_inc(x_done, 1)

            dve.sem_inc(s_used, 1)
            dve.sem_inc(x_done, 2)
            dve.wait_ge(counted, 1)
            run(front, experts)(dve)

        @block.scalar
        def _(act):
            def front(t, u):
                act.wait_ge(ht_ready, t + 1)
                for c in range(DC):
                    if bn is None:
                        cp = act.copy(hT[:, c, :], h_ps[:, c, :])
                    else:
                        cp = act.activation(hT[:, c, :], h_ps[:, c, :], ACT.Identity, bias=bn[1][:, c:c + 1],
                                            scale=bn[0][:, c:c + 1])
                cp.then_inc(hT_ready, 1)
                act.wait_ge(top_ready, t + 1)
                if soft:
                    act.activation(weigh[u][:, :], weigh[u][:, :], ACT.Exp).then_inc(weigh_ready, 1)
                else:
                    act.activation(weigh[u][:, :], top[u][:, :, :].rearrange("p h k -> p (h k)"), ACT.Sigmoid).then_inc(weigh_ready, 1)

            def spread(t, u, c):
                act.wait_ge(w_ready, t * NC + c + 1)
                act.wait_ge(up_done, t * NC + c + RC - 1)
                for i in range(K):
                    e = c * K + i
                    cp = act.mul(diag[:, c % 2, i, :], core.ident[:, :], w[:, e:e + 1])
                cp.then_inc(diag_ready, 1)

            def experts(t, u):
                for c in range(NC):
                    e = slice(c * K, (c + 1) * K)
                    act.wait_ge(dots_ready, t * NC + c + 1)
                    act.activation(mid[:, e], dot[:, e], ACT.Silu if soft else ACT.Gelu).then_inc(act_done, 1)
                    if c:
                        spread(t, u, c - 1)
                spread(t, u, NC - 1)

            run(front, experts)(act)

        @block.tensor
        def _(pe):
            def front(t, u):
                pe.wait_ge(hn_ready, t + 1)
                for c in range(DC):
                    mm = pe.transpose(h_ps[:, c, :], hn[u][:, c * P:(c + 1) * P], core.ident[:, :])
                mm.then_inc(ht_ready, 1)
                pe.wait_ge(hT_ready, t + 1)
                pe.wait_ge(s_used, t + 1)
                for n in range(2):
                    for c in range(DC):
                        mm = pe.matmul(s_ps[:, n, :], hT[:, c, :], G[:, c, n * 512:(n + 1) * 512], start=(c == 0), stop=(c == DC - 1))
                mm.then_inc(s_ready, 1)

            def experts(t, u):
                pe.wait_ge(x_done, t + 1)
                for c in range(NC):
                    pe.wait_ge(diag_ready, t * NC + c + 1)
                    for i in range(K):
                        mm = pe.matmul(o_ps[u][:, :], diag[:, c % 2, i, :], ring[:, (c % RC) * K + i, D:2 * D],
                                       start=(c == 0 and i == 0), stop=(c == NC - 1 and i == K - 1))
                    mm.then_inc(up_done, 1)

            pe.sem_inc(up_done, RC)
            run(front, experts)(pe)


def layer0_ffn(core, A):
    nh, nk = 8, 64
    with ExitStack() as stack:
        st = Stage(core, "L0f", stack)
        G = st.sb("G", [P, DC, 2 * nh * nk])
        bn_scale = st.sb("bn_scale", [P, DC])
        bn_bias = st.sb("bn_bias", [P, DC])
        row_stats(core, "L0t")
        batch_norm_stats(core, "L0b", {"bn": A["L0_bn"]}, bn_scale[:, :], bn_bias[:, :])
        fold_keys(core, "L0g", {"wq": A["L0_pq"], "keys": A["L0_keys"]}, 2 * nh, 128, nk, G)
        product_key_experts(core, "L0e", A["L0_table"], nh, nk, G, core.gates[:, 1, 0:1], bn=(bn_scale, bn_bias))


def context_norm(core, tag, A, cxT, mask_row):
    nc = core.nc
    with ExitStack() as stack:
        st = Stage(core, tag, stack)
        ctx = st.sb("ctx", [SC, B, D])
        gb = st.sb("gb", [P, 2, DC])
        mask = st.sb("mask", [1, CT], U8)
        stats = st.sb("stats", [SC, B, 6])
        mv = st.sb("mv", [SC, B, 2])
        std = st.sb("std", [SC, B])
        c_ps = [st.ps(f"c_ps{u}", [P, DC, SC]) for u in range(2)]
        loaded = st.sem("loaded")
        var_ready, std_ready = st.sem("var_ready"), st.sem("std_ready")
        hn_ready, ht_ready, done = st.sem("hn_ready"), st.sem("ht_ready"), st.sem("done")
        block = stack.enter_context(nc.Block())

        @block.sync
        def _(sp):
            sp.dma_start(ctx[:, :, :], A["ctx"]).then_inc(loaded, 16)
            sp.dma_start(gb[:, :, :], A["ln_x"]).then_inc(loaded, 16)
            sp.dma_start(mask[:, :], A["mask"]).then_inc(loaded, 16)

        @block.vector
        def _(dve):
            dve.wait_ge(loaded, 48)
            dve.tensor_copy(mask_row, mask[:, :])
            for b in range(B):
                dve.bn_stats(stats[:, b, :], ctx[:, b, :])
            dve.drain()
            dve.tensor_scalar(mask_row, mask_row, 1.0, -MASKED, ALU.subtract, ALU.mult)
            for b in range(B):
                dve.bn_aggr(mv[:, b, :], stats[:, b, :])
            dve.drain()
            dve.tensor_scalar(std[:, :], mv[:, :, 1], EPS, None, ALU.add).then_inc(var_ready, 1)
            dve.wait_ge(std_ready, 1)
            dve.reciprocal(std[:, :], std[:, :])
            dve.drain()
            for b in range(B):
                dve.tensor_scalar(ctx[:, b, :], ctx[:, b, :], mv[:, b, 0:1], std[:, b:b + 1], ALU.subtract,
                                  ALU.mult).then_inc(hn_ready, 1)

        @block.scalar
        def _(act):
            act.wait_ge(var_ready, 1)
            act.activation(std[:, :], std[:, :], ACT.Sqrt).then_inc(std_ready, 1)
            for b in range(B):
                act.wait_ge(ht_ready, b + 1)
                for c in range(DC):
                    cp = act.activation(cxT[:, c, b * SC:(b + 1) * SC], c_ps[b % 2][:, c, :], ACT.Identity,
                                        bias=gb[:, 1, c:c + 1], scale=gb[:, 0, c:c + 1])
                cp.then_inc(done, 1)

        @block.tensor
        def _(pe):
            for b in range(B):
                pe.wait_ge(hn_ready, b + 1)
                if b >= 2:
                    pe.wait_ge(done, b - 1)
                for c in range(DC):
                    mm = pe.transpose(c_ps[b % 2][:, c, :], ctx[:, b, c * P:(c + 1) * P], core.ident[0:SC, 0:SC])
                mm.then_inc(ht_ready, 1)


def counts(sizes):
    out = [0]
    for n in sizes:
        out.append(out[-1] + n)
    return out[:-1], out[-1]


def long_attention(core, tag, A, y, heads, hd, slot, scale, affine=None, cxT=None, mask_row=None, causal=False,
                   biased=False):
    nc = core.nc
    NG = 16 // heads
    VW = heads * hd
    OC = NG * VW // P
    KX = SC if cxT is not None else 0
    KT = S + KX
    ktiles = [(a, min(a + P, KT)) for a in range(0, KT, P)]
    key_cuts = [(a, min(a + 512, KT)) for a in range(0, KT, 512)]
    vper = 512 // VW
    vgroups = [ktiles[a:a + vper] for a in range(0, len(ktiles), vper)]
    projections = [("q", c) for c in ((0, 512), (512, 1024))] + [("k", c) for c in key_cuts] + \
                  [("v", g) for g in vgroups]
    NJ = len(projections)
    NJA, NJV = (NJ + 1) // 2, NJ // 2
    units = [(j, i) for j in range(heads) for i in range(TB)]
    UN = len(units)

    def tiles_of(i):
        return ktiles[:i + 1] if causal else ktiles

    def tgroups(i):
        n = len(tiles_of(i))
        return [range(a, min(a + 4, n)) for a in range(0, n, 4)]

    t_at, t_all = counts([len(tgroups(i)) for _, i in units])
    a_at, a_all = counts([(len(tgroups(i)) + 1) // 2 for _, i in units])
    v_at, v_all = counts([len(tgroups(i)) // 2 for _, i in units])
    ogroups = [range(a, min(a + 4, OC)) for a in range(0, OC, 4)]
    ahead = 1 if KX else 2
    s_banks = 5 if KX else 4
    s_at = (0, 3 * 512 - KX if KX else 2 * 512)

    def place(u, a):
        if u == 0 or not KX:
            return a
        return a + KX if a < S else a - S

    with ExitStack() as stack:
        st = Stage(core, tag, stack)
        hn = [st.sb(f"hn{u}", [P, D]) for u in range(2)]
        kvT = st.sb("kvT", [P, DC, KT])
        wq = st.sb("wq", [P, DC, P])
        wk = st.sb("wk", [P, DC, P])
        wv = st.sb("wv", [P, DC, VW])
        wo = st.sb("wo", [P, OC, D])
        qT = st.sb("qT", [P, heads, S])
        kT = st.sb("kT", [P, KT])
        V = st.sb("V", [P, len(ktiles), VW])
        E = [st.sb(f"E{u}", [P, KT]) for u in range(2)]
        nmax = st.sb("nmax", [P, 2])
        l = st.sb("l", [P, UN])
        rl = st.sb("rl", [P, UN])
        PT = st.sb("PT", [P, len(ktiles), P])
        O = st.sb("O", [P, TB, NG * VW])
        if biased:
            qk_bias = st.sb("qk_bias", [P, 2, NG])
            v_bias = st.sb("v_bias", [1, NG, VW])
            o_bias = st.sb("o_bias", [1, D])
        if causal:
            cmask = st.sb("cmask", [P, P])
        s_ps = st.ps("s_ps", [P, 512 * s_banks])
        t_ps = [st.ps(f"t_ps{i}", [P, 512]) for i in range(2)]
        misc_ps = [st.ps(f"misc_ps{i}", [P, 512]) for i in range(8 - s_banks - 2)]
        o_ps = [misc_ps[u % len(misc_ps)][:, u * hd:(u + 1) * hd] for u in range(2)]
        t_ps.append(misc_ps[0][:, 128:256])
        y_ps = misc_ps[0][:, 256:512]
        consts = st.sem("consts")
        w_loaded = st.sem("w_loaded")
        hn_ready = st.sem("hn_ready")
        ht_ready = st.sem("ht_ready")
        hT_ready = st.sem("hT_ready")
        cx_ready = st.sem("cx_ready")
        pj_ready = st.sem("pj_ready")
        pj_act = st.sem("pj_act")
        pj_dve = st.sem("pj_dve")
        s_ready = st.sem("s_ready")
        max_ready = st.sem("max_ready")
        e_ready = st.sem("e_ready")
        t_ready = st.sem("t_ready")
        tc_act = st.sem("tc_act")
        tc_dve = st.sem("tc_dve")
        o_ready = st.sem("o_ready")
        o_done = st.sem("o_done")
        ot_ready = st.sem("ot_ready")
        oT_ready = st.sem("oT_ready")
        y_ready = st.sem("y_ready")
        y_done = st.sem("y_done")
        zeroed = st.sem("zeroed")
        masked = st.sem("masked")
        pe_steps = st.sem("pe_steps")
        OT = PT
        assert OC <= len(ktiles)
        block = stack.enter_context(nc.Block())

        @block.sync
        def _(sp):
            n_const = 1
            sp.dma_start(wo[:, :, :], A["wo"].rearrange("(c p) o -> p c o", p=P)).then_inc(consts, 16)
            if biased:
                sp.dma_start(qk_bias[:, :, :], A["qk_bias"]).then_inc(consts, 16)
                sp.dma_start(v_bias[:, :, :], A["v_bias"]).then_inc(consts, 16)
                sp.dma_start(o_bias[:, :], A["o_bias"]).then_inc(consts, 16)
                n_const = 4
            sp.wait_ge(consts, 16 * n_const)

            def weights(n, g, first=False):
                if not first:
                    sp.wait_ge(pj_ready, n * NJ)
                for w, name in ((wq, "wq"), (wk, "wk"), (wv, "wv")):
                    sp.dma_start(w[:, :, :], A[name][:, g, :].rearrange("(c p) e -> p c e", p=P)).then_inc(w_loaded, 16)

            weights(0, 0, first=True)
            with sp.Fori(1, B * NG) as n:
                weights(n, n % NG)

        @block.gpsimd
        def _(pool):
            pool.memset(qT[:, :, :], 0.0).then_inc(zeroed, 1)
            if causal:
                pool.memset(cmask[:, :], 0.0)
                pool.drain()
                pool.affine_select(cmask[:, :], cmask[:, :], [[-1, P]], ALU.is_ge, MASKED, base=0,
                                   channel_multiplier=1).then_inc(masked, 1)

        @block.tensor
        def _(pe):
            pe.wait_ge(consts, 16 * (4 if biased else 1))
            if causal:
                pe.wait_ge(masked, 1)

            def scores(b, n, m):
                j, i = units[m]
                u = m % 2
                kn = tiles_of(i)[-1][1]
                for a, z in key_cuts:
                    z = min(z, kn, S)
                    if a >= z:
                        continue
                    diag = causal and z == kn
                    at = s_at[u] + place(u, a)
                    mm = pe.matmul(s_ps[:, at:at + z - a], qT[:, j, i * P:(i + 1) * P], kT[:, a:z], start=True, stop=not diag)
                    if diag:
                        mm = pe.matmul(s_ps[:, at + z - a - P:at + z - a], core.ident[:, :], cmask[:, :], start=False, stop=True)
                if not KX:
                    mm.then_inc(s_ready, 1)

            def context_scores(b, n, m):
                j, i = units[m]
                at = s_at[m % 2] + place(m % 2, S)
                pe.matmul(s_ps[:, at:at + KX], qT[:, j, i * P:(i + 1) * P], kT[:, S:KT], start=True, stop=False)
                pe.matmul(s_ps[:, at:at + KX], core.ones[:, :], mask_row[:, bass.ds(b * SC, SC)], start=False,
                          stop=True).then_inc(s_ready, 1)

            def turn(n, m):
                j, i = units[m]
                pe.wait_ge(e_ready, n * UN + m + 1)
                ks = tiles_of(i)
                for x, g in enumerate(tgroups(i)):
                    if x == 2:
                        pe.wait_ge(o_done, n * UN + m + 2)
                    for k in g:
                        a, z = ks[k]
                        at = place(m % 2, a)
                        mm = pe.transpose(t_ps[x][0:z - a, (k - g[0]) * P:(k - g[0] + 1) * P], E[m % 2][:, at:at + z - a], core.ident[:, :])
                    mm.then_inc(t_ready, 1)

            def values(n, m):
                j, i = units[m]
                ks = tiles_of(i)
                pe.wait_ge(tc_act, n * a_all + a_at[m] + (len(tgroups(i)) + 1) // 2)
                if len(tgroups(i)) > 1:
                    pe.wait_ge(tc_dve, n * v_all + v_at[m] + len(tgroups(i)) // 2)
                pe.wait_ge(o_done, n * UN + m + 1)
                for k, (a, z) in enumerate(ks):
                    mm = pe.matmul(o_ps[m % 2], PT[0:z - a, k, :], V[0:z - a, k, j * hd:(j + 1) * hd],
                                   start=(k == 0), stop=(k == len(ks) - 1))
                mm.then_inc(o_ready, 1)

            with pe.Fori(0, B) as b:
                for i in range(TB):
                    pe.wait_ge(hn_ready, b * TB + i + 1)
                    if i >= 2:
                        pe.wait_ge(hT_ready, b * TB + i - 1)
                    for c in range(DC):
                        mm = pe.transpose(t_ps[i % 2][:, c * P:(c + 1) * P], hn[i % 2][:, c * P:(c + 1) * P], core.ident[:, :])
                    mm.then_inc(ht_ready, 1)
                pe.wait_ge(hT_ready, (b + 1) * TB)
                if KX:
                    pe.wait_ge(cx_ready, b + 1)
                pe.sem_inc(pe_steps, 1)
                with pe.Fori(0, NG) as g:
                    n = b * NG + g
                    pe.wait_ge(w_loaded, (n + 1) * 48)
                    for x, (kind, what) in enumerate(projections):
                        if x >= 2:
                            if x % 2:
                                pe.wait_ge(pj_dve, n * NJV + x // 2)
                            else:
                                pe.wait_ge(pj_act, n * NJA + x // 2)
                        ps = t_ps[x % 2]
                        if kind in "qk":
                            a, z = what
                            w = wq if kind == "q" else wk
                            for c in range(DC):
                                mm = pe.matmul(ps[:, 0:z - a], w[:, c, :], kvT[:, c, a:z], start=(c == 0), stop=(c == DC - 1))
                        else:
                            for v, (a, z) in enumerate(what):
                                out = ps[0:z - a, v * VW:(v + 1) * VW]
                                for c in range(DC):
                                    mm = pe.matmul(out, kvT[:, c, a:z], wv[:, c, :], start=(c == 0), stop=(c == DC - 1 and not biased))
                                if biased:
                                    mm = pe.matmul(out, core.ones[:, 0:z - a], v_bias[:, g, :], start=False, stop=True)
                        mm.then_inc(pj_ready, 1)
                    pe.wait_ge(pj_act, (n + 1) * NJA)
                    pe.wait_ge(pj_dve, (n + 1) * NJV)
                    scores(b, n, 0)
                    if KX:
                        context_scores(b, n, 0)
                    scores(b, n, 1)
                    for m in range(UN):
                        turn(n, m)
                        if KX and m + 1 < UN:
                            context_scores(b, n, m + 1)
                        if m + 2 < UN:
                            scores(b, n, m + 2)
                        values(n, m)
                pe.wait_ge(o_done, (b + 1) * NG * UN + 2)
                for i in range(TB):
                    for x, g in enumerate(ogroups):
                        for k in g:
                            mm = pe.transpose(t_ps[x][:, (k - g[0]) * P:(k - g[0] + 1) * P], O[:, i, k * P:(k + 1) * P], core.ident[:, :])
                        mm.then_inc(ot_ready, 1)
                    pe.wait_ge(oT_ready, (b * TB + i + 1) * len(ogroups))
                    pe.wait_ge(y_done, b * TB + i + 1)
                    for k in range(OC):
                        mm = pe.matmul(y_ps, OT[:, k, :], wo[:, k, :], start=(k == 0), stop=(k == OC - 1 and not biased))
                    if biased:
                        mm = pe.matmul(y_ps, core.ones[:, :], o_bias[:, :], start=False, stop=True)
                    mm.then_inc(y_ready, 1)

        @block.vector
        def _(dve):
            dve.sem_inc(o_done, 2)
            dve.sem_inc(y_done, 1)
            dve.wait_ge(zeroed, 1)

            def largest(n, m):
                u = m % 2
                dve.wait_ge(s_ready, n * UN + m + 1)
                dve.tensor_reduce(nmax[:, u:u + 1], s_ps[:, s_at[u]:s_at[u] + tiles_of(units[m][1])[-1][1]], AX.X, ALU.max,
                                  negate=True).then_inc(max_ready, 1)

            def finish(n, g, m):
                j, i = units[m]
                if len(tgroups(i)) == 1:
                    dve.drain()
                dve.wait_ge(o_ready, n * UN + m + 1)
                dve.tensor_scalar(O[:, i, bass.ds(g * VW + j * hd, hd)], o_ps[m % 2], rl[:, m:m + 1], None,
                                  ALU.mult).then_inc(o_done, 1)

            with dve.Fori(0, B) as b:
                if KX:
                    dve.tensor_copy(kvT[:, :, S:KT], cxT[:, :, bass.ds(b * SC, SC)]).then_inc(cx_ready, 1)
                for i in range(TB):
                    if i >= 2:
                        dve.wait_ge(ht_ready, b * TB + i - 1)
                    normalise(dve, core, hn[i % 2][:, :], b * TB + i).then_inc(hn_ready, 1)
                with dve.Fori(0, NG) as g:
                    n = b * NG + g
                    for x, (kind, what) in enumerate(projections):
                        if x % 2 == 0:
                            continue
                        dve.wait_ge(pj_ready, n * NJ + x + 1)
                        ps = t_ps[x % 2]
                        if kind == "q":
                            a, z = what
                            for j in range(heads):
                                r = slice(j * slot, (j + 1) * slot)
                                if biased:
                                    ins = dve.tensor_scalar(qT[r, j, a:z], ps[r, 0:z - a], qk_bias[r, 0, bass.ds(g, 1)], scale, ALU.add, ALU.mult)
                                else:
                                    ins = dve.tensor_scalar(qT[r, j, a:z], ps[r, 0:z - a], scale, None, ALU.mult)
                        elif kind == "k":
                            a, z = what
                            if biased:
                                ins = dve.tensor_scalar(kT[:, a:z], ps[:, 0:z - a], qk_bias[:, 1, bass.ds(g, 1)], None, ALU.add)
                            else:
                                ins = dve.tensor_copy(kT[:, a:z], ps[:, 0:z - a])
                        else:
                            rows = what[0][1] - what[0][0]
                            k = what[0][0] // P
                            ins = dve.tensor_copy(V[0:rows, k:k + len(what), :],
                                                  ps[0:rows, 0:len(what) * VW].rearrange("p (k v) -> p k v", v=VW))
                        ins.then_inc(pj_dve, 1)
                    for m in range(ahead):
                        largest(n, m)
                    for m in range(UN):
                        if m:
                            finish(n, g, m - 1)
                        i = units[m][1]
                        if len(tgroups(i)) == 1:
                            dve.wait_ge(e_ready, n * UN + m + 1)
                            dve.reciprocal(rl[:, m:m + 1], l[:, m:m + 1])
                        for x, gr in enumerate(tgroups(i)):
                            if x % 2:
                                dve.wait_ge(t_ready, n * t_all + t_at[m] + x + 1)
                                if x == 1:
                                    dve.reciprocal(rl[:, m:m + 1], l[:, m:m + 1])
                                dve.tensor_copy(PT[:, gr[0]:gr[-1] + 1, :],
                                                t_ps[x][:, 0:len(gr) * P].rearrange("p (k q) -> p k q", q=P)).then_inc(tc_dve, 1)
                        if m + ahead < UN:
                            largest(n, m + ahead)
                    dve.drain()
                    finish(n, g, UN - 1)
                for i in range(TB):
                    dve.wait_ge(y_ready, b * TB + i + 1)
                    dve.tensor_copy(y[:, bass.ds(b * TB + i, 1), :], y_ps.unsqueeze(1)).then_inc(y_done, 1)

        @block.scalar
        def _(act):
            act.wait_ge(zeroed, 1)

            def exponentials(n, m):
                u = m % 2
                kn = tiles_of(units[m][1])[-1][1]
                act.wait_ge(max_ready, n * UN + m + 1)
                act.activation(E[u][:, 0:kn], s_ps[:, s_at[u]:s_at[u] + kn], ACT.Exp, bias=nmax[:, u:u + 1],
                               accum_out=l[:, m:m + 1]).then_inc(e_ready, 1)

            with act.Fori(0, B) as b:
                for i in range(TB):
                    act.wait_ge(ht_ready, b * TB + i + 1)
                    for c in range(DC):
                        out, ps = kvT[:, c, i * P:(i + 1) * P], t_ps[i % 2][:, c * P:(c + 1) * P]
                        if affine is None:
                            cp = act.copy(out, ps)
                        else:
                            cp = act.activation(out, ps, ACT.Identity, bias=affine[:, 1, c:c + 1], scale=affine[:, 0, c:c + 1])
                    cp.then_inc(hT_ready, 1)
                with act.Fori(0, NG) as g:
                    n = b * NG + g
                    for x, (kind, what) in enumerate(projections):
                        if x % 2:
                            continue
                        act.wait_ge(pj_ready, n * NJ + x + 1)
                        ps = t_ps[x % 2]
                        if kind == "q":
                            a, z = what
                            for j in range(heads):
                                r = slice(j * slot, (j + 1) * slot)
                                if biased:
                                    act.activation(qT[r, j, a:z], ps[r, 0:z - a], ACT.Identity, bias=qk_bias[r, 0, bass.ds(g, 1)])
                                else:
                                    ins = act.mul(qT[r, j, a:z], ps[r, 0:z - a], scale)
                            if biased:
                                act.drain()
                                ins = act.mul(qT[:, :, a:z], qT[:, :, a:z], scale)
                        elif kind == "k":
                            a, z = what
                            if biased:
                                ins = act.activation(kT[:, a:z], ps[:, 0:z - a], ACT.Identity, bias=qk_bias[:, 1, bass.ds(g, 1)])
                            else:
                                ins = act.copy(kT[:, a:z], ps[:, 0:z - a])
                        else:
                            rows = what[0][1] - what[0][0]
                            k = what[0][0] // P
                            ins = act.copy(V[0:rows, k:k + len(what), :],
                                           ps[0:rows, 0:len(what) * VW].rearrange("p (k v) -> p k v", v=VW))
                        ins.then_inc(pj_act, 1)
                    for m in range(ahead):
                        exponentials(n, m)
                    for m in range(UN):
                        i = units[m][1]
                        ks = tiles_of(i)
                        for x, gr in enumerate(tgroups(i)):
                            if x % 2 == 0:
                                rows = ks[gr[0]][1] - ks[gr[0]][0]
                                act.wait_ge(t_ready, n * t_all + t_at[m] + x + 1)
                                act.copy(PT[0:rows, gr[0]:gr[-1] + 1, :],
                                         t_ps[x][0:rows, 0:len(gr) * P].rearrange("p (k q) -> p k q", q=P)).then_inc(tc_act, 1)
                        if m + ahead < UN:
                            if len(tgroups(i)) % 2 == 0:
                                act.wait_ge(t_ready, n * t_all + t_at[m] + len(tgroups(i)))
                            exponentials(n, m + ahead)
                for i in range(TB):
                    for x, gr in enumerate(ogroups):
                        act.wait_ge(ot_ready, (b * TB + i) * len(ogroups) + x + 1)
                        act.copy(OT[:, gr[0]:gr[-1] + 1, :],
                                 t_ps[x][:, 0:len(gr) * P].rearrange("p (k q) -> p k q", q=P)).then_inc(oT_ready, 1)


def add_normed(core, tag, A, y, gate):
    nc = core.nc
    with ExitStack() as stack:
        st = Stage(core, tag, stack)
        rows = st.sb("rows", [P, 2, D])
        stats = st.sb("stats", [P, NT, 6])
        mv = st.sb("mv", [P, NT, 2])
        rstd = st.sb("rstd", [P, NT])
        loaded, var_ready, std_ready = st.sem("loaded"), st.sem("var_ready"), st.sem("std_ready")
        scaled, shifted = st.sem("scaled"), st.sem("shifted")
        block = stack.enter_context(nc.Block())

        @block.sync
        def _(sp):
            sp.dma_start(rows[:, :, :], A["ln_o"]).then_inc(loaded, 16)

        @block.vector
        def _(dve):
            with dve.Fori(0, NT) as t:
                dve.bn_stats(stats[:, t, :], y[:, t, :])
            dve.drain()
            for t in range(NT):
                dve.bn_aggr(mv[:, t, :], stats[:, t, :])
            dve.drain()
            dve.tensor_scalar(rstd[:, :], mv[:, :, 1], EPS, None, ALU.add).then_inc(var_ready, 1)
            dve.wait_ge(std_ready, 1)
            dve.reciprocal(rstd[:, :], rstd[:, :])
            dve.drain()
            dve.wait_ge(loaded, 16)
            dve.tensor_scalar(rows[:, :, :], rows[:, :, :], gate, None, ALU.mult)
            dve.drain()
            with dve.Fori(0, NT) as t:
                dve.tensor_scalar(y[:, t, :], y[:, t, :], mv[:, t, 0:1], rstd[:, bass.ds(t, 1)], ALU.subtract, ALU.mult)
                dve.tensor_tensor(core.x[:, t, :], core.x[:, t, :], rows[:, 1, :], ALU.add)
                dve.drain()
                dve.tensor_tensor(y[:, t, :], y[:, t, :], rows[:, 0, :], ALU.mult)
                dve.drain()
                dve.tensor_tensor(core.x[:, t, :], core.x[:, t, :], y[:, t, :], ALU.add)

        @block.scalar
        def _(act):
            act.wait_ge(var_ready, 1)
            act.activation(rstd[:, :], rstd[:, :], ACT.Sqrt).then_inc(std_ready, 1)


def layer1_xattn(core, A):
    nc = core.nc
    with ExitStack() as stack:
        st = Stage(core, "L1x", stack)
        y = st.sb("y", [P, NT, D])
        cxT = st.sb("cxT", [P, DC, CT])
        mask_row = st.sb("mask_row", [1, CT])
        affine = st.sb("affine", [P, 2, DC])
        loaded = st.sem("loaded")
        with ExitStack() as inner:
            block = inner.enter_context(nc.Block())

            @block.sync
            def _(sp):
                sp.dma_start(affine[:, :, :], A["L1_ln_l"]).then_inc(loaded, 16)
                sp.wait_ge(loaded, 16)
        context_norm(core, "L1c", {"ctx": A["ctx"], "ln_x": A["L1_ln_x"], "mask": A["mask"]}, cxT, mask_row[:, :])
        row_stats(core, "L1s", twice=True)
        long_attention(core, "L1a", {k: A["L1_" + k] for k in ("wq", "wk", "wv", "wo")}, y, 2, 64, 64, 64 ** -0.5,
                       affine=affine, cxT=cxT, mask_row=mask_row)
        add_normed(core, "L1n", {"ln_o": A["L1_ln_o"]}, y, core.gates[:, 0, 1:2])


def transpose_normed(core, tag, hT):
    nc = core.nc
    with ExitStack() as stack:
        st = Stage(core, tag, stack)
        hn = [st.sb(f"hn{u}", [P, D]) for u in range(2)]
        h_ps = [st.ps(f"h_ps{u}", [P, DC, P]) for u in range(2)]
        hn_ready = st.sem("hn_ready")
        ht_ready = st.sem("ht_ready")
        hT_done = st.sem("hT_done")
        block = stack.enter_context(nc.Block())

        @block.vector
        def _(dve):
            with dve.Fori(0, NT // 2) as k:
                for u in range(2):
                    dve.wait_ge(ht_ready, 2 * k + u + 1)
                    normalise(dve, core, hn[u][:, :], 2 * k + u).then_inc(hn_ready, 1)

        @block.tensor
        def _(pe):
            pe.sem_inc(ht_ready, 2)
            with pe.Fori(0, NT // 2) as k:
                for u in range(2):
                    pe.wait_ge(hn_ready, 2 * k + u + 1)
                    pe.wait_ge(hT_done, 2 * k + u + 1)
                    for c in range(DC):
                        mm = pe.transpose(h_ps[u][:, c, :], hn[u][:, c * P:(c + 1) * P], core.ident[:, :])
                    mm.then_inc(ht_ready, 1)

        @block.scalar
        def _(act):
            act.sem_inc(hT_done, 2)
            with act.Fori(0, NT // 2) as k:
                for u in range(2):
                    act.wait_ge(ht_ready, 2 * k + u + 3)
                    act.copy(hT[:, :, bass.ds((2 * k + u) * P, P)], h_ps[u][:, :, :]).then_inc(hT_done, 1)


E8, F = 8, 1024
FC = F // P
NB = B * S // 512


def task_gates(core, tag, A, hT, gv):
    nc = core.nc
    with ExitStack() as stack:
        st = Stage(core, tag, stack)
        w1 = st.sb("w1", [P, DC, D])
        b1 = st.sb("b1", [P, DC])
        w2 = st.sb("w2", [P, DC, E8])
        b2 = st.sb("b2", [P, E8])
        acc = st.sb("acc", [P, DC, NB])
        mh = st.sb("mh", [P, DC * B])
        spread = st.sb("spread", [P, DC * B, P])
        a_ps = [st.ps(f"a_ps{u}", [P, 512]) for u in range(2)]
        g_ps = st.ps("g_ps", [P, B, E8])
        loaded = st.sem("loaded")
        a_ready, a_done = st.sem("a_ready"), st.sem("a_done")
        spread_ready, g_ready = st.sem("spread_ready"), st.sem("g_ready")
        block = stack.enter_context(nc.Block())

        @block.sync
        def _(sp):
            sp.dma_start(w1[:, :, :], A["w1"].rearrange("(c p) o -> p c o", p=P)).then_inc(loaded, 16)
            sp.dma_start(b1[:, :], A["b1"]).then_inc(loaded, 16)
            sp.dma_start(w2[:, :, :], A["w2"].rearrange("(c p) e -> p c e", p=P)).then_inc(loaded, 16)
            sp.dma_start(b2[:, :], A["b2"]).then_inc(loaded, 16)

        @block.tensor
        def _(pe):
            pe.wait_ge(loaded, 64)
            for n in range(NB * DC):
                q, o = n // DC, n % DC
                if n >= 2:
                    pe.wait_ge(a_done, n - 1)
                for c in range(DC):
                    mm = pe.matmul(a_ps[n % 2][:, :], w1[:, c, o * P:(o + 1) * P], hT[:, c, q * 512:(q + 1) * 512],
                                   start=(c == 0), stop=(c == DC - 1))
                mm.then_inc(a_ready, 1)
            pe.wait_ge(spread_ready, 1)
            for b in range(B):
                for o in range(DC):
                    mm = pe.matmul(g_ps[:, b, :], spread[:, o * B + b, :], w2[:, o, :], start=(o == 0), stop=(o == DC - 1))
            mm.then_inc(g_ready, 1)

        @block.scalar
        def _(act):
            act.wait_ge(loaded, 64)
            for n in range(NB * DC):
                q, o = n // DC, n % DC
                act.wait_ge(a_ready, n + 1)
                act.activation(a_ps[n % 2][:, :], a_ps[n % 2][:, :], ACT.Relu, bias=b1[:, o:o + 1],
                               accum_out=acc[:, o, q:q + 1]).then_inc(a_done, 1)

        @block.vector
        def _(dve):
            dve.wait_ge(a_done, NB * DC)
            dve.tensor_reduce(mh[:, :], acc[:, :, :].rearrange("p o (b q) -> p (o b) q", b=B), AX.X, ALU.add)
            dve.drain()
            dve.tensor_scalar(mh[:, :], mh[:, :], 1.0 / S, None, ALU.mult)
            dve.drain()
            dve.tensor_copy(spread[:, :, :], mh[:, :].unsqueeze(2).to_broadcast([P, DC * B, P])).then_inc(spread_ready, 1)
            dve.wait_ge(g_ready, 1)
            dve.wait_ge(loaded, 64)
            dve.tensor_tensor(gv, g_ps[:, :, :], b2[:, :].unsqueeze(1).to_broadcast([P, B, E8]), ALU.add)


def merge_tasks(core, tag, A, gv, Wm, b1m, b2m):
    nc = core.nc
    W = DC * F + FC * D
    with ExitStack() as stack:
        st = Stage(core, tag, stack)
        base = st.sb("base", [P, W])
        task = [st.sb(f"task{u}", [P, W]) for u in range(2)]
        b1 = st.sb("b1", [P, E8 + 1, FC])
        b2 = st.sb("b2", [1, E8 + 1, D])
        loaded = st.sem("loaded")
        task_loaded = [st.sem(f"task_loaded{u}") for u in range(2)]
        merged = st.sem("merged")
        block = stack.enter_context(nc.Block())

        @block.sync
        def _(sp):
            sp.dma_start(base[:, :], A["w"][0]).then_inc(loaded, 16)
            sp.dma_start(b1[:, :, :], A["b1"]).then_inc(loaded, 16)
            sp.dma_start(b2[:, :, :], A["b2"]).then_inc(loaded, 16)
            for e in range(E8):
                if e >= 2:
                    sp.wait_ge(merged, e - 1)
                sp.dma_start(task[e % 2][:, :], A["w"][1 + e]).then_inc(task_loaded[e % 2], 16)

        @block.vector
        def _(dve):
            dve.wait_ge(loaded, 48)
            for e in range(E8):
                dve.wait_ge(task_loaded[e % 2], 16 * (e // 2 + 1))
                for b in range(B):
                    g = gv[:, b, e:e + 1]
                    dve.scalar_tensor_tensor(b1m[:, b, :], b1[:, 1 + e, :], g, b1m[:, b, :] if e else b1[:, 0, :], ALU.mult, ALU.add)
                    dve.scalar_tensor_tensor(b2m[:, b, :], b2[:, 1 + e, :], gv[0:1, b, e:e + 1],
                                             b2m[:, b, :] if e else b2[:, 0, :], ALU.mult, ALU.add)
                    ins = dve.scalar_tensor_tensor(Wm[:, b, :], task[e % 2][:, :], g, Wm[:, b, :] if e else base[:, :],
                                                   ALU.mult, ALU.add)
                ins.then_inc(merged, 1)
                dve.drain()


def batch_ffn(core, tag, hT, Wm, b1m, b2m, gate):
    nc = core.nc
    with ExitStack() as stack:
        st = Stage(core, tag, stack)
        uT = st.sb("uT", [P, FC, 512])
        u_ps = [st.ps(f"u_ps{i}", [P, 512]) for i in range(3)]
        o_ps = [st.ps(f"o_ps{i}", [P, D]) for i in range(2)]
        u_ready = st.sem("u_ready")
        u_done = st.sem("u_done")
        o_ready = st.sem("o_ready")
        x_done = st.sem("x_done")
        block = stack.enter_context(nc.Block())

        @block.tensor
        def _(pe):
            for b in range(B):
                w1 = Wm[:, b, 0:DC * F].rearrange("p (c f) -> p c f", c=DC)
                w2 = Wm[:, b, DC * F:].rearrange("p (k o) -> p k o", k=FC)
                with pe.Fori(0, 2) as q:
                    n = q + 2 * b
                    for k in range(FC):
                        if k >= 3:
                            pe.wait_ge(u_done, n * FC + k - 2)
                        for c in range(DC):
                            mm = pe.matmul(u_ps[k % 3][:, :], w1[:, c, k * P:(k + 1) * P], hT[:, c, bass.ds(n * 512, 512)],
                                           start=(c == 0), stop=(c == DC - 1))
                        mm.then_inc(u_ready, 1)
                    pe.wait_ge(u_done, (n + 1) * FC)
                    for i in range(4):
                        pe.wait_ge(x_done, n * 4 + i + 1)
                        for k in range(FC):
                            pe.matmul(o_ps[i % 2][:, :], uT[:, k, i * P:(i + 1) * P], w2[:, k, :], start=(k == 0), stop=False)
                        pe.matmul(o_ps[i % 2][:, :], core.ones[:, :], b2m[:, b, :], start=False, stop=True).then_inc(o_ready, 1)

        @block.scalar
        def _(act):
            for b in range(B):
                with act.Fori(0, 2) as q:
                    n = q + 2 * b
                    for k in range(FC):
                        act.wait_ge(u_ready, n * FC + k + 1)
                        act.activation(uT[:, k, :], u_ps[k % 3][:, :], ACT.Gelu_apprx_tanh,
                                       bias=b1m[:, b, k:k + 1]).then_inc(u_done, 1)

        @block.vector
        def _(dve):
            dve.sem_inc(x_done, 2)
            with dve.Fori(0, NT // 2) as k:
                for i in range(2):
                    t = 2 * k + i
                    dve.wait_ge(o_ready, t + 1)
                    dve.scalar_tensor_tensor(core.x[:, t, :], o_ps[i][:, :], gate, core.x[:, t, :],
                                             ALU.mult, ALU.add).then_inc(x_done, 1)


def layer1_ffn(core, A):
    with ExitStack() as stack:
        st = Stage(core, "L1f", stack)
        hT = st.sb("hT", [P, DC, B * S])
        gv = st.sb("gv", [P, B, E8])
        Wm = st.sb("Wm", [P, B, DC * F + FC * D])
        b1m = st.sb("b1m", [P, B, FC])
        b2m = st.sb("b2m", [1, B, D])
        row_stats(core, "L1t")
        transpose_normed(core, "L1h", hT)
        task_gates(core, "L1g", {k: A["L1_g" + k] for k in ("w1", "b1", "w2", "b2")}, hT, gv[:, :, :])
        merge_tasks(core, "L1m", {"w": A["L1_tasks"], "b1": A["L1_tb1"], "b2": A["L1_tb2"]}, gv, Wm, b1m, b2m)
        batch_ffn(core, "L1f", hT, Wm, b1m, b2m, core.gates[:, 1, 1:2])


def single_head_prep(core, tag, A, M, N, cM):
    nc = core.nc
    with ExitStack() as stack:
        st = Stage(core, tag, stack)
        wk = st.sb("wk", [P, DC, D])
        wq = st.sb("wq", [P, DC, D])
        wv = st.sb("wv", [P, DC, D])
        bqk = st.sb("bqk", [P, 2, DC])
        bv = st.sb("bv", [1, D])
        kT = st.sb("kT", [P, DC, CT])
        k_ps = st.ps("k_ps", [P, DC, 512])
        m_ps = st.ps("m_ps", [P, DC, 512])
        c_ps = st.ps("c_ps", [1, CT])
        v_ps = st.ps("v_ps", [SC, B, D])
        loaded, k_ready, kT_ready = st.sem("loaded"), st.sem("k_ready"), st.sem("kT_ready")
        v_ready, m_ready = st.sem("v_ready"), st.sem("m_ready")
        block = stack.enter_context(nc.Block())

        @block.sync
        def _(sp):
            for w, name in ((wk, "wk"), (wq, "wq"), (wv, "wv")):
                sp.dma_start(w[:, :, :], A[name].rearrange("(c p) e -> p c e", p=P)).then_inc(loaded, 16)
            sp.dma_start(bqk[:, :, :], A["bqk"]).then_inc(loaded, 16)
            sp.dma_start(bv[:, :], A["bv"]).then_inc(loaded, 16)

        @block.tensor
        def _(pe):
            pe.wait_ge(loaded, 80)
            for e in range(DC):
                for c in range(DC):
                    mm = pe.matmul(k_ps[:, e, 0:CT], wk[:, c, e * P:(e + 1) * P], core.ctxT[:, c, :], start=(c == 0), stop=(c == DC - 1))
            mm.then_inc(k_ready, 1)
            for b in range(B):
                for c in range(DC):
                    pe.matmul(v_ps[:, b, :], core.ctxT[:, c, b * SC:(b + 1) * SC], wv[:, c, :], start=(c == 0), stop=False)
                mm = pe.matmul(v_ps[:, b, :], core.ones[:, 0:SC], bv[:, :], start=False, stop=True)
            mm.then_inc(v_ready, 1)
            pe.wait_ge(kT_ready, 1)
            for c in range(DC):
                for e in range(DC):
                    pe.matmul(m_ps[:, c, 0:CT], wq[:, e, c * P:(c + 1) * P], kT[:, e, :], start=(e == 0), stop=(e == DC - 1))
            for e in range(DC):
                mm = pe.matmul(c_ps[:, :], bqk[:, 0, e:e + 1], kT[:, e, :], start=(e == 0), stop=(e == DC - 1))
            mm.then_inc(m_ready, 1)

        @block.scalar
        def _(act):
            act.wait_ge(k_ready, 1)
            for e in range(DC):
                cp = act.activation(kT[:, e, :], k_ps[:, e, 0:CT], ACT.Identity, bias=bqk[:, 1, e:e + 1])
            cp.then_inc(kT_ready, 1)
            act.wait_ge(m_ready, 1)
            for c in range(DC):
                act.copy(M[:, c, :, :], m_ps[:, c, 0:CT].rearrange("p (b j) -> p b j", b=B))

        @block.vector
        def _(dve):
            dve.wait_ge(v_ready, 1)
            dve.tensor_copy(N[0:SC, :, 0, :], v_ps[:, :, :])
            dve.wait_ge(m_ready, 1)
            dve.tensor_copy(cM[:, :, :], c_ps[:, :].rearrange("p (b j) -> p b j", b=B))


def layer2_xattn(core, A):
    with ExitStack() as stack:
        st = Stage(core, "L2x", stack)
        M = st.sb("M", [P, DC, B, SC])
        N = st.sb("N", [P, B, 1, D])
        cM = st.sb("cM", [1, B, SC])
        zero_tail(core, "L2z", N[:, :, :, :])
        single_head_prep(core, "L2p", {k: A["L2_" + k] for k in ("wk", "wq", "wv", "bqk", "bv")}, M, N, cM)
        row_stats(core, "L2s")
        cross_attend(core, "L2a", 1, M, N, D ** -0.5, core.gates[:, 0, 2:3], cM=cM)


def swiglu(core, tag, A, hT, gate):
    nc = core.nc
    with ExitStack() as stack:
        st = Stage(core, tag, stack)
        wg = st.sb("wg", [P, DC, F])
        wu = st.sb("wu", [P, DC, F])
        wd = st.sb("wd", [P, FC, D])
        sg = st.sb("sg", [P, 2, 512])
        aT = st.sb("aT", [P, FC, 512])
        g_ps = [st.ps(f"g_ps{i}", [P, 512]) for i in range(2)]
        u_ps = [st.ps(f"u_ps{i}", [P, 512]) for i in range(2)]
        o_ps = [st.ps(f"o_ps{i}", [P, D]) for i in range(2)]
        loaded = st.sem("loaded")
        gu_ready = st.sem("gu_ready")
        sg_ready = st.sem("sg_ready")
        a_done = st.sem("a_done")
        o_ready = st.sem("o_ready")
        x_done = st.sem("x_done")
        block = stack.enter_context(nc.Block())

        @block.sync
        def _(sp):
            sp.dma_start(wg[:, :, :], A["wg"].rearrange("(c p) e -> p c e", p=P)).then_inc(loaded, 16)
            sp.dma_start(wu[:, :, :], A["wu"].rearrange("(c p) e -> p c e", p=P)).then_inc(loaded, 16)
            sp.dma_start(wd[:, :, :], A["wd"].rearrange("(c p) e -> p c e", p=P)).then_inc(loaded, 16)

        @block.tensor
        def _(pe):
            pe.wait_ge(loaded, 48)
            with pe.Fori(0, NB) as n:
                for k in range(FC):
                    pe.wait_ge(a_done, n * FC + k + 1)
                    for w, ps in ((wg, g_ps), (wu, u_ps)):
                        for c in range(DC):
                            mm = pe.matmul(ps[k % 2][:, :], w[:, c, k * P:(k + 1) * P], hT[:, c, bass.ds(n * 512, 512)],
                                           start=(c == 0), stop=(c == DC - 1))
                    mm.then_inc(gu_ready, 1)
                pe.wait_ge(a_done, (n + 1) * FC + 2)
                for i in range(4):
                    pe.wait_ge(x_done, n * 4 + i + 1)
                    for k in range(FC):
                        mm = pe.matmul(o_ps[i % 2][:, :], aT[:, k, i * P:(i + 1) * P], wd[:, k, :], start=(k == 0), stop=(k == FC - 1))
                    mm.then_inc(o_ready, 1)

        @block.scalar
        def _(act):
            with act.Fori(0, NB) as n:
                for k in range(FC):
                    act.wait_ge(gu_ready, n * FC + k + 1)
                    act.wait_ge(a_done, n * FC + k + 1)
                    act.activation(sg[:, k % 2, :], g_ps[k % 2][:, :], ACT.Silu).then_inc(sg_ready, 1)

        @block.vector
        def _(dve):
            dve.sem_inc(a_done, 2)
            dve.sem_inc(x_done, 2)
            with dve.Fori(0, NB) as n:
                for k in range(FC):
                    dve.wait_ge(sg_ready, n * FC + k + 1)
                    dve.tensor_tensor(aT[:, k, :], u_ps[k % 2][:, :], sg[:, k % 2, :], ALU.mult).then_inc(a_done, 1)
                for i in range(4):
                    t = n * 4 + i
                    dve.wait_ge(o_ready, t + 1)
                    dve.scalar_tensor_tensor(core.x[:, t, :], o_ps[i % 2][:, :], gate, core.x[:, t, :],
                                             ALU.mult, ALU.add).then_inc(x_done, 1)


def layer2_ffn(core, A):
    nh, nk = 4, 128
    with ExitStack() as stack:
        st = Stage(core, "L2f", stack)
        hT = st.sb("hT", [P, DC, B * S])
        row_stats(core, "L2t")
        transpose_normed(core, "L2h", hT)
        with ExitStack() as inner:
            G = inner.enter_context(core.nc.sbuf_tensor("L2f_G", [P, DC, 2 * nh * nk], F32))
            fold_keys(core, "L2g", {"wq": A["L2_pq"], "keys": A["L2_keys"]}, 2 * nh, 64, nk, G)
            product_key_experts(core, "L2e", A["L2_table"], nh, nk, G, core.gates[:, 1, 2:3], last_expert=4095, soft=True)
        swiglu(core, "L2m", {k: A["L2_" + k] for k in ("wg", "wu", "wd")}, hT, core.gates[:, 1, 2:3])


def layer3_xattn(core, A):
    nh, hd = 16, 16
    W = nh * SC
    with ExitStack() as stack:
        st = Stage(core, "L3x", stack)
        y = st.sb("y", [P, NT, D])
        row_stats(core, "L3s")
        long_attention(core, "L3a", {k: A["L3s_" + k] for k in ("wq", "wk", "wv", "wo", "qk_bias", "v_bias", "o_bias")}, y,
                       4, 16, 32, hd ** -0.5, causal=True, biased=True)
        M = st.sb("M", [P, DC, B, W])
        n_dram = core.nc.dram_tensor("L3x_n_dram", (B, W, D), F32, kind="Internal").ap()
        cM = st.sb("cM", [1, B, W])
        out_row = st.sb("out_row", [1, D])
        loaded = st.sem("loaded")
        with ExitStack() as inner:
            block = inner.enter_context(core.nc.Block())

            @block.sync
            def _(sp):
                sp.dma_start(out_row[:, :], A["L3c_bo"]).then_inc(loaded, 16)
                sp.wait_ge(loaded, 16)
        cross_prep(core, "L3p", {k: A["L3c_" + k] for k in ("wk", "wv", "wq", "wo", "bias")}, nh, hd, M, n_dram, True, cM=cM)
        N = st.sb("N", [P, B, -(-W // P), D])
        load_packed(core, "L3n", n_dram, N, W)
        cross_attend(core, "L3c", nh, M, N, hd ** -0.5, core.gates[:, 0, 3:4], src=y, cM=cM, out_row=out_row[:, :])


def ternary_weights(core, tag, A, q, s_w):
    nc = core.nc
    W = DC * F
    with ExitStack() as stack:
        st = Stage(core, tag, stack)
        w = st.sb("w", [P, 3, W])
        ones = st.sb("ones", [P, P])
        mag = st.sb("mag", [P, 3])
        inv = st.sb("inv", [P, 3])
        s_ps = st.ps("s_ps", [P, 3])
        loaded, mag_ready, sum_ready = st.sem("loaded"), st.sem("mag_ready"), st.sem("sum_ready")
        block = stack.enter_context(nc.Block())

        @block.sync
        def _(sp):
            sp.dma_start(w[:, :, :], A["w"]).then_inc(loaded, 16)

        @block.vector
        def _(dve):
            dve.memset(ones[:, :], 1.0)
            dve.wait_ge(loaded, 16)
            dve.tensor_reduce(mag[:, :], w[:, :, :], AX.X, ALU.add, apply_absolute_value=True)
            dve.drain().then_inc(mag_ready, 1)
            dve.wait_ge(sum_ready, 1)
            dve.tensor_scalar(s_w, s_ps[:, :], 1.0 / (D * F), 1e-5, ALU.mult, ALU.max)
            dve.drain()
            dve.reciprocal(inv[:, :], s_w)
            dve.drain()
            for i in range(3):
                dve.tensor_scalar(w[:, i, :], w[:, i, :], inv[:, i:i + 1], ROUND, ALU.mult, ALU.add)
            dve.drain()
            dve.tensor_scalar(w[:, :, :], w[:, :, :], ROUND, 1.0, ALU.subtract, ALU.min)
            dve.drain()
            dve.tensor_scalar(q, w[:, :, :], -1.0, None, ALU.max)

        @block.tensor
        def _(pe):
            pe.wait_ge(mag_ready, 1)
            pe.matmul(s_ps[:, :], ones[:, :], mag[:, :], start=True, stop=True).then_inc(sum_ready, 1)


def bit_ffn(core, tag, A, q, s_w, gate):
    nc = core.nc
    wg = q[:, 0, :].rearrange("p (c f) -> p c f", c=DC)
    wu = q[:, 1, :].rearrange("p (c f) -> p c f", c=DC)
    wd = q[:, 2, :].rearrange("p (k o) -> p k o", k=FC)
    with ExitStack() as stack:
        st = Stage(core, tag, stack)
        identb = st.sb("identb", [P, P], BF16)
        hn = st.sb("hn", [P, D])
        hq = st.sb("hq", [P, D], BF16)
        hqT = st.sb("hqT", [P, DC, P], BF16)
        sg = st.sb("sg", [P, F])
        a = st.sb("a", [P, F])
        aq = st.sb("aq", [P, F], BF16)
        aqT = st.sb("aqT", [P, FC, P], BF16)
        top = st.sb("top", [P, 2])
        to_int = st.sb("to_int", [P, 2])
        g_scale = st.sb("g_scale", [P, NT])
        u_scale = st.sb("u_scale", [P, NT])
        o_scale = st.sb("o_scale", [P, 1])
        h_ps = st.ps("h_ps", [P, DC, P], BF16)
        g_ps = st.ps("g_ps", [P, F])
        u_ps = st.ps("u_ps", [P, F])
        t_ps = st.ps("t_ps", [P, FC, P], BF16)
        o_ps = st.ps("o_ps", [P, D])
        ident_ready = st.sem("ident_ready")
        hq_ready = st.sem("hq_ready")
        ht_ready = st.sem("ht_ready")
        hT_ready = st.sem("hT_ready")
        gu_ready = st.sem("gu_ready")
        sg_ready = st.sem("sg_ready")
        aq_ready = st.sem("aq_ready")
        at_ready = st.sem("at_ready")
        aT_ready = st.sem("aT_ready")
        o_ready = st.sem("o_ready")
        x_done = st.sem("x_done")
        block = stack.enter_context(nc.Block())

        @block.vector
        def _(dve):
            def rounded(out, tmp, i):
                dve.tensor_scalar(tmp, tmp, to_int[:, i:i + 1], 127.0, ALU.mult, ALU.min)
                dve.drain()
                dve.tensor_scalar(tmp, tmp, -128.0, ROUND, ALU.max, ALU.add)
                dve.drain()
                return dve.tensor_scalar(out, tmp, ROUND, None, ALU.subtract)

            def scales(x, i):
                dve.tensor_reduce(top[:, i:i + 1], x, AX.X, ALU.max, apply_absolute_value=True)
                dve.drain()
                dve.tensor_scalar(top[:, i:i + 1], top[:, i:i + 1], 1e-5, None, ALU.max)
                dve.drain()
                dve.reciprocal(to_int[:, i:i + 1], top[:, i:i + 1])
                dve.tensor_scalar(top[:, i:i + 1], top[:, i:i + 1], 1.0 / 127.0, None, ALU.mult)
                dve.drain()
                dve.tensor_scalar(to_int[:, i:i + 1], to_int[:, i:i + 1], 127.0, None, ALU.mult)

            def front(t, first=False):
                dve.drain()
                normalise(dve, core, hn[:, :], t)
                dve.drain()
                scales(hn[:, :], 0)
                dve.tensor_scalar(g_scale[:, bass.ds(t, 1)], top[:, 0:1], s_w[:, 0:1], None, ALU.mult)
                dve.tensor_scalar(u_scale[:, bass.ds(t, 1)], top[:, 0:1], s_w[:, 1:2], None, ALU.mult)
                dve.drain()
                if not first:
                    dve.wait_ge(ht_ready, t)
                rounded(hq[:, :], hn[:, :], 0).then_inc(hq_ready, 1)

            def back(t):
                dve.drain()
                dve.wait_ge(sg_ready, t + 1)
                dve.scalar_tensor_tensor(a[:, :], u_ps[:, :], u_scale[:, bass.ds(t, 1)], sg[:, :], ALU.mult, ALU.mult)
                dve.drain()
                scales(a[:, :], 1)
                dve.tensor_scalar(o_scale[:, :], top[:, 1:2], s_w[:, 2:3], None, ALU.mult)
                dve.drain()
                dve.tensor_scalar(o_scale[:, :], o_scale[:, :], gate, None, ALU.mult)
                rounded(aq[:, :], a[:, :], 1).then_inc(aq_ready, 1)
                dve.wait_ge(o_ready, t + 1)
                dve.scalar_tensor_tensor(core.x[:, t, :], o_ps[:, :], o_scale[:, 0:1], core.x[:, t, :],
                                         ALU.mult, ALU.add).then_inc(x_done, 1)

            dve.sem_inc(x_done, 1)
            dve.tensor_copy(identb[:, :], core.ident[:, :]).then_inc(ident_ready, 1)
            front(0, first=True)
            with dve.Fori(0, NT - 1) as t:
                front(t + 1)
                back(t)
            back(NT - 1)

        @block.scalar
        def _(act):
            def front(t):
                act.wait_ge(ht_ready, t + 1)
                act.copy(hqT[:, :, :], h_ps[:, :, :]).then_inc(hT_ready, 1)

            def turn(t):
                act.wait_ge(at_ready, t + 1)
                act.copy(aqT[:, :, :], t_ps[:, :, :]).then_inc(aT_ready, 1)

            def silu(t):
                act.wait_ge(gu_ready, t + 1)
                act.activation(sg[:, :], g_ps[:, :], ACT.Silu, scale=g_scale[:, bass.ds(t, 1)]).then_inc(sg_ready, 1)

            front(0)
            silu(0)
            with act.Fori(0, NT - 1) as t:
                front(t + 1)
                turn(t)
                silu(t + 1)
            turn(NT - 1)

        @block.tensor
        def _(pe):
            def front(t):
                pe.wait_ge(hq_ready, t + 1)
                for c in range(DC):
                    mm = pe.transpose(h_ps[:, c, :], hq[:, c * P:(c + 1) * P], identb[:, :])
                mm.then_inc(ht_ready, 1)

            def products(t):
                pe.wait_ge(hT_ready, t + 1)
                for w, ps in ((wg, g_ps), (wu, u_ps)):
                    for n in range(2):
                        for c in range(DC):
                            mm = pe.matmul(ps[:, n * 512:(n + 1) * 512], hqT[:, c, :], w[:, c, n * 512:(n + 1) * 512],
                                           start=(c == 0), stop=(c == DC - 1))
                mm.then_inc(gu_ready, 1)

            def turn(t):
                pe.wait_ge(aq_ready, t + 1)
                for k in range(FC):
                    mm = pe.transpose(t_ps[:, k, :], aq[:, k * P:(k + 1) * P], identb[:, :])
                mm.then_inc(at_ready, 1)

            def output(t):
                pe.wait_ge(aT_ready, t + 1)
                pe.wait_ge(x_done, t + 1)
                for k in range(FC):
                    mm = pe.matmul(o_ps[:, :], aqT[:, k, :], wd[:, k, :], start=(k == 0), stop=(k == FC - 1))
                mm.then_inc(o_ready, 1)

            pe.wait_ge(ident_ready, 1)
            front(0)
            products(0)
            with pe.Fori(0, NT - 1) as t:
                front(t + 1)
                turn(t)
                products(t + 1)
                output(t)
            turn(NT - 1)
            output(NT - 1)


def layer3_ffn(core, A):
    with ExitStack() as stack:
        st = Stage(core, "L3f", stack)
        q = st.sb("q", [P, 3, DC * F], BF16)
        s_w = st.sb("s_w", [P, 3])
        ternary_weights(core, "L3w", {"w": A["L3_w"]}, q[:, :, :], s_w[:, :])
        row_stats(core, "L3t")
        bit_ffn(core, "L3b", A, q, s_w, core.gates[:, 1, 3:4])


def build(nc, A, out, stages):
    with ExitStack() as stack:
        core = Core(nc, stack)
        load_inputs(core, A)
        for s in stages:
            s(core, A)
            core.end_layer()
        store_output(core, out)


def layout(i):
    f = np.float32
    a = {}
    a["x"] = i["x"]
    a["ident"] = np.eye(P, dtype=f)
    a["ctxT"] = i["ctx_1024"].reshape(CT, D).T
    a["gates"] = np.broadcast_to(np.stack([i["g_xattn"], i["g_ffn"]]), (P, 2, 4))
    kv = i["L0_xattn_Wkv"].reshape(64, 2, 16, D)
    a["L0_wk"] = kv[:, 0].transpose(2, 1, 0).reshape(D, 1024)
    a["L0_wv"] = kv[:, 1].transpose(2, 1, 0).reshape(D, 1024)
    a["L0_wq"] = i["L0_xattn_Wq"].reshape(64, 16, D)
    a["L0_wo"] = i["L0_xattn_W0"].reshape(D, 16, 64).transpose(2, 1, 0)
    a["L0_bn"] = np.stack([i["L0_ffn_bn_gamma"], i["L0_ffn_bn_beta"]]).reshape(2, DC, P).transpose(2, 0, 1)
    a["L0_pq"] = i["L0_ffn_w_q"].reshape(16, 128, D).transpose(1, 0, 2)
    a["L0_keys"] = i["L0_ffn_keys_p"].transpose(3, 2, 0, 1).reshape(128, 16, 64)
    a["L0_table"] = np.concatenate([i["L0_ffn_down"], i["L0_ffn_up"]], axis=1)
    a["ctx"] = i["ctx_1024"].transpose(1, 0, 2)
    a["mask"] = i["mask_BxS2_bk0"].reshape(1, CT)
    for n in ("ln_x", "ln_l"):
        a["L1_" + n] = np.stack([i[f"L1_xattn_{n}_g"], i[f"L1_xattn_{n}_b"]]).reshape(2, DC, P).transpose(2, 0, 1)
    a["L1_ln_o"] = np.broadcast_to(np.stack([i["L1_xattn_ln_o_g"], i["L1_xattn_ln_o_b"]]), (P, 2, D))
    a["L1_wq"] = i["L1_xattn_Wq"].reshape(D, 8, P)
    a["L1_wk"] = i["L1_xattn_Wkv"][:, 0:1024].reshape(D, 8, P)
    a["L1_wv"] = i["L1_xattn_Wkv"][:, 1024:2048].reshape(D, 8, P)
    a["L1_wo"] = i["L1_xattn_Wout"]

    def chunked(w):
        return w.reshape(-1, P, w.shape[-1]).transpose(1, 0, 2).reshape(P, -1)

    a["L1_gw1"] = i["L1_ffn_gate_w1"].T
    a["L1_gb1"] = i["L1_ffn_gate_b1"].reshape(DC, P).T
    a["L1_gw2"] = i["L1_ffn_gate_w2"].T
    a["L1_gb2"] = np.broadcast_to(i["L1_ffn_gate_b2"], (P, E8))
    w1 = np.concatenate([i["L1_ffn_W1"][None], i["L1_ffn_TW1"]])
    w2 = np.concatenate([i["L1_ffn_W2"][None], i["L1_ffn_TW2"]])
    a["L1_tasks"] = np.stack([np.concatenate([chunked(u.T), chunked(v.T)], axis=1) for u, v in zip(w1, w2)])
    a["L1_tb1"] = np.concatenate([i["L1_ffn_b1"][None], i["L1_ffn_Tb1"]]).reshape(E8 + 1, FC, P).transpose(2, 0, 1)
    a["L1_tb2"] = np.concatenate([i["L1_ffn_b2"][None], i["L1_ffn_Tb2"]])[None]
    a["L2_wk"], a["L2_wv"], a["L2_wq"] = i["L2_xattn_Wk"], i["L2_xattn_Wv"], i["L2_xattn_Wq"].T
    a["L2_bqk"] = np.stack([i["L2_xattn_bq"], i["L2_xattn_bk"]]).reshape(2, DC, P).transpose(2, 0, 1)
    a["L2_bv"] = i["L2_xattn_bv"][None]
    a["L2_pq"] = i["L2_ffn_Wq"].reshape(8, 64, D).transpose(1, 0, 2)
    a["L2_keys"] = i["L2_ffn_keys"].transpose(3, 2, 0, 1).reshape(64, 8, 128)
    a["L2_table"] = np.concatenate([i["L2_ffn_down_embed"], i["L2_ffn_up_embed"]], axis=1)
    a["L2_wg"], a["L2_wu"], a["L2_wd"] = i["L2_ffn_Wg"].T, i["L2_ffn_Wu"].T, i["L2_ffn_Wd"].T
    for n in ("q", "k"):
        w = np.zeros((D, 4, 4, 32), f)
        w[:, :, :, 0:16] = i[f"L3_xattn_W{n}1"].transpose(1, 0, 2).reshape(D, 4, 4, 16)
        a["L3s_w" + n] = w.reshape(D, 4, P)
    bias = np.zeros((2, 4, 4, 32), f)
    bias[0, :, :, 0:16] = i["L3_xattn_bq1"].reshape(4, 4, 16)
    bias[1, :, :, 0:16] = i["L3_xattn_bk1"].reshape(4, 4, 16)
    a["L3s_qk_bias"] = bias.reshape(2, 4, P).transpose(2, 0, 1)
    a["L3s_wv"] = i["L3_xattn_Wv1"].transpose(1, 0, 2).reshape(D, 4, 64)
    a["L3s_v_bias"] = i["L3_xattn_bv1"].reshape(1, 4, 64)
    a["L3s_wo"] = i["L3_xattn_Wo1"]
    a["L3s_o_bias"] = i["L3_xattn_bo1"][None]
    a["L3c_wk"] = i["L3_xattn_Wk2"].transpose(1, 0, 2).reshape(D, D)
    a["L3c_wv"] = i["L3_xattn_Wv2"].transpose(1, 0, 2).reshape(D, D)
    a["L3c_wq"] = i["L3_xattn_Wq2"].transpose(2, 0, 1)
    a["L3c_wo"] = i["L3_xattn_Wo2"].reshape(16, 16, D).transpose(1, 0, 2)
    a["L3c_bias"] = np.stack([i["L3_xattn_bq2"], i["L3_xattn_bk2"], i["L3_xattn_bv2"]]).transpose(2, 0, 1)
    a["L3c_bo"] = i["L3_xattn_bo2"][None]
    a["L3_w"] = np.stack([chunked(i["L3_ffn_" + n].T) for n in ("w_gate", "w_up", "w_down")], axis=1)
    return a


ALL = [layer0_xattn, layer0_ffn, layer1_xattn, layer1_ffn, layer2_xattn, layer2_ffn, layer3_xattn, layer3_ffn]


def kernel(**inputs):
    import concourse.bacc as _bacc
    from concourse.bass_utils import run_bass_kernel_spmd as _run

    nc = _bacc.Bacc("TRN2", target_bir_lowering=False, num_devices=1)
    arrays = {"in_" + k: np.ascontiguousarray(v) for k, v in layout({k: np.asarray(v) for k, v in inputs.items()}).items()}
    aps = {k[3:]: nc.dram_tensor(k, v.shape, mybir.dt.from_np(v.dtype), kind="ExternalInput").ap() for k, v in arrays.items()}
    out = nc.dram_tensor("out_x", (B, S, D), F32, kind="ExternalOutput").ap()
    build(nc, aps, out, ALL)
    r = _run(nc, [arrays], core_ids=[0])
    return r.results[0]["out_x"]
```

```python
from contextlib import ExitStack

import numpy as np

import concourse.bass as bass
from concourse import mybir

F32 = mybir.dt.float32
BF16 = mybir.dt.bfloat16
U32 = mybir.dt.uint32
I32 = mybir.dt.int32
U8 = mybir.dt.uint8
ALU = mybir.AluOpType
ACT = mybir.ActivationFunctionType
AX = mybir.AxisListType

P = 128
B, S, D = 4, 1024, 256
NT = B * S // P
TB = S // P
DC = D // P
SC = 77
CT = B * SC
EPS = 1e-5
MASKED = -1e30
ROUND = 1.5 * 2.0 ** 23


class Core:

    def __init__(self, nc, stack, out):
        self.nc = nc
        self.out = out
        self.stack = stack
        self.x = stack.enter_context(nc.sbuf_tensor("x_res", [P, NT, D], F32))
        self.mean = stack.enter_context(nc.sbuf_tensor("row_mean", [P, NT], F32))
        self.rstd = stack.enter_context(nc.sbuf_tensor("row_rstd", [P, NT], F32))
        self.ident = stack.enter_context(nc.sbuf_tensor("ident", [P, P], F32))
        self.ones = stack.enter_context(nc.sbuf_tensor("ones_row", [1, P], F32))
        self.ctxT = stack.enter_context(nc.sbuf_tensor("ctxT", [P, DC, CT], F32))
        self.gates = stack.enter_context(nc.sbuf_tensor("gates", [P, 2, 4], F32))

        self.sems = []
        self.x_loaded = self.sem("x_loaded")

    def sem(self, name):
        self.sems.append(self.nc.alloc_semaphore(name=name))
        return self.sems[-1]

    def end_layer(self):
        self.nc.clear_and_free_semaphores(self.sems)
        self.nc.all_engine_barrier()
        self.sems = []


class Stage:

    def __init__(self, core, tag, stack):
        self.core, self.tag, self.stack = core, tag, stack

    def sb(self, name, shape, dt=F32):
        return self.stack.enter_context(self.core.nc.sbuf_tensor(f"{self.tag}_{name}", shape, dt))

    def ps(self, name, shape, dt=F32):
        return self.stack.enter_context(self.core.nc.psum_tensor(f"{self.tag}_{name}", shape, dt))

    def sem(self, name):
        return self.core.sem(f"{self.tag}_{name}")


def load_inputs(core, A):
    nc = core.nc
    with ExitStack() as stack:
        st = Stage(core, "in", stack)
        loaded, ready = st.sem("loaded"), st.sem("ready")
        block = stack.enter_context(nc.Block())

        @block.sync
        def _(sp):
            sp.dma_start(core.ident[:, :], A["ident"]).then_inc(loaded, 16)
            sp.dma_start(core.ctxT[:, :, :], A["ctxT"].rearrange("(c p) t -> p c t", p=P)).then_inc(loaded, 16)
            sp.dma_start(core.gates[:, :, :], A["gates"]).then_inc(loaded, 16)
            sp.wait_ge(loaded, 48)

        @block.vector
        def _(dve):
            dve.memset(core.ones[:, :], 1.0)

        @block.scalar
        def _(act):
            act.wait_ge(loaded, 48)
            act.activation(core.gates[:, :, :], core.gates[:, :, :], ACT.Tanh).then_inc(ready, 1)
            act.wait_ge(ready, 1)


def load_x(sp, core, A):
    sp.dma_start(core.x[:, :, :], A["x"].rearrange("b (n p) d -> p (b n) d", p=P)).then_inc(core.x_loaded, 16)


def row_stats(core, tag, twice=False, load=None, x_arrives=False):
    nc = core.nc
    with ExitStack() as stack:
        st = Stage(core, tag, stack)
        stats = st.sb("stats", [P, NT, 6])
        var = st.sb("var", [P, NT])
        tmp = st.sb("tmp", [P, NT])
        std = st.sb("std", [P, NT])
        var_ready, std_ready = st.sem("var_ready"), st.sem("std_ready")
        loaded = st.sem("loaded")
        block = stack.enter_context(nc.Block())

        if load:
            @block.sync
            def _(sp):
                sp.wait_ge(loaded, load(sp, loaded))

        @block.vector
        def _(dve):
            if x_arrives:
                dve.wait_ge(core.x_loaded, 16)
            with dve.Fori(0, NT // 8) as k:
                for i in range(8):
                    dve.bn_stats(stats[:, 8 * k + i, :], core.x[:, 8 * k + i, :])
            dve.drain()
            dve.tensor_tensor(core.mean[:, :], stats[:, :, 1], stats[:, :, 4], ALU.add)
            dve.tensor_tensor(tmp[:, :], stats[:, :, 1], stats[:, :, 4], ALU.subtract)
            dve.tensor_tensor(var[:, :], stats[:, :, 2], stats[:, :, 5], ALU.add)
            dve.drain()
            dve.tensor_scalar(core.mean[:, :], core.mean[:, :], 0.5, None, ALU.mult)
            dve.tensor_tensor(tmp[:, :], tmp[:, :], tmp[:, :], ALU.mult)
            dve.tensor_scalar(var[:, :], var[:, :], 1.0 / D, None, ALU.mult)
            dve.drain()
            dve.tensor_scalar(tmp[:, :], tmp[:, :], 0.25, None, ALU.mult)
            dve.drain()
            dve.tensor_tensor(var[:, :], var[:, :], tmp[:, :], ALU.add)
            dve.drain()
            dve.tensor_scalar(tmp[:, :], var[:, :], EPS, None, ALU.add).then_inc(var_ready, 1)
            dve.wait_ge(std_ready, 1)
            dve.reciprocal(core.rstd[:, :], std[:, :])
            if twice:
                dve.drain()
                dve.tensor_tensor(tmp[:, :], core.rstd[:, :], core.rstd[:, :], ALU.mult)
                dve.drain()
                dve.tensor_tensor(tmp[:, :], tmp[:, :], var[:, :], ALU.mult)
                dve.drain()
                dve.tensor_scalar(tmp[:, :], tmp[:, :], EPS, None, ALU.add).then_inc(var_ready, 1)
                dve.wait_ge(std_ready, 2)
                dve.reciprocal(tmp[:, :], std[:, :])
                dve.drain()
                dve.tensor_tensor(core.rstd[:, :], core.rstd[:, :], tmp[:, :], ALU.mult)

        @block.scalar
        def _(act):
            act.wait_ge(var_ready, 1)
            act.activation(std[:, :], tmp[:, :], ACT.Sqrt).then_inc(std_ready, 1)
            if twice:
                act.wait_ge(var_ready, 2)
                act.activation(std[:, :], tmp[:, :], ACT.Sqrt).then_inc(std_ready, 1)


def normalise(dve, core, out, t):
    return dve.tensor_scalar(out, core.x[:, t, :], core.mean[:, bass.ds(t, 1)], core.rstd[:, bass.ds(t, 1)],
                             ALU.subtract, ALU.mult)


def cross_prep(core, tag, A, nh, hd, M, n_dram, biased, cM=None, load=None):
    nc = core.nc
    with ExitStack() as stack:
        st = Stage(core, tag, stack)
        wk = st.sb("wk", [P, DC, nh * hd])
        wv = st.sb("wv", [P, DC, nh * hd])
        wq = st.sb("wq", [hd, nh, D])
        wo = st.sb("wo", [hd, nh, D])
        kT = st.sb("kT", [hd, CT])
        vT = st.sb("vT", [hd, CT])
        Nst = st.sb("Nst", [SC, B, D])
        bias = st.sb("bias", [hd, 3, nh])
        k_ps = st.ps("k_ps", [hd, CT])
        v_ps = st.ps("v_ps", [hd, CT])
        m_ps = st.ps("m_ps", [P, DC, 512])
        n_ps = st.ps("n_ps", [SC, B, D])
        c_ps = st.ps("c_ps", [1, CT])
        if biased:
            c_row = st.sb("c_row", [1, CT])
        loaded = st.sem("loaded")
        kv_ready = st.sem("kv_ready")
        kT_ready = st.sem("kT_ready")
        vT_ready = st.sem("vT_ready")
        mn_ready = st.sem("mn_ready")
        m_done = st.sem("m_done")
        n_done = st.sem("n_done")
        n_stored = st.sem("n_stored")
        cleared = st.sem("cleared")
        nload = 4 + biased
        block = stack.enter_context(nc.Block())

        @block.sync
        def _(sp):
            sp.dma_start(wk[:, :, :], A["wk"].rearrange("(c p) e -> p c e", p=P)).then_inc(loaded, 16)
            sp.dma_start(wv[:, :, :], A["wv"].rearrange("(c p) e -> p c e", p=P)).then_inc(loaded, 16)
            sp.dma_start(wq[:, :, :], A["wq"]).then_inc(loaded, 16)
            sp.dma_start(wo[:, :, :], A["wo"]).then_inc(loaded, 16)
            if biased:
                sp.dma_start(bias[:, :, :], A["bias"]).then_inc(loaded, 16)
            if load:
                load(sp)
            for h in range(nh):
                sp.wait_ge(n_done, h + 1)
                sp.dma_start(n_dram[:, h * SC:(h + 1) * SC, :].rearrange("b j o -> j b o"), Nst[:, :, :]).then_inc(n_stored, 16)
            sp.wait_ge(n_stored, 16 * nh)

        @block.tensor
        def _(pe):
            pe.wait_ge(loaded, 16 * nload)
            for h in range(nh):
                e = slice(h * hd, (h + 1) * hd)
                if h:
                    pe.wait_ge(kT_ready, h)
                    pe.wait_ge(vT_ready, h)
                for w, ps in ((wk, k_ps), (wv, v_ps)):
                    for c in range(DC):
                        mm = pe.matmul(ps[:, :], w[:, c, e], core.ctxT[:, c, :], start=(c == 0), stop=(c == DC - 1))
                mm.then_inc(kv_ready, 1)
                pe.wait_ge(kT_ready, h + 1)
                pe.wait_ge(vT_ready, h + 1)
                if h:
                    pe.wait_ge(m_done, h)
                    pe.wait_ge(n_done, h)
                for c in range(DC):
                    pe.matmul(m_ps[:, c, 0:CT], wq[:, h, c * P:(c + 1) * P], kT[:, :], start=True, stop=True)
                if biased:
                    pe.matmul(c_ps[:, :], bias[:, 0, h:h + 1], kT[:, :], start=True, stop=True)
                for b in range(B):
                    mm = pe.matmul(n_ps[:, b, :], vT[:, b * SC:(b + 1) * SC], wo[:, h, :], start=True, stop=True)
                mm.then_inc(mn_ready, 1)

        @block.scalar
        def _(act):
            for h in range(nh):
                act.wait_ge(kv_ready, h + 1)
                if h:
                    act.wait_ge(mn_ready, h)
                if biased:
                    act.activation(kT[:, :], k_ps[:, :], ACT.Identity, bias=bias[:, 1, h:h + 1]).then_inc(kT_ready, 1)
                else:
                    act.copy(kT[:, :], k_ps[:, :]).then_inc(kT_ready, 1)
                act.wait_ge(mn_ready, h + 1)
                for c in range(DC):
                    cp = act.copy(M[:, c, :, h * SC:(h + 1) * SC], m_ps[:, c, 0:CT].rearrange("p (b j) -> p b j", b=B))
                cp.then_inc(m_done, 1)

        if biased:
            @block.gpsimd
            def _(pool):
                pool.memset(cM[:, :, :], 0.0).then_inc(cleared, 1)

        @block.vector
        def _(dve):
            if biased:
                dve.wait_ge(cleared, 1)
            for h in range(nh):
                dve.wait_ge(kv_ready, h + 1)
                if h:
                    dve.wait_ge(mn_ready, h)
                if biased:
                    dve.tensor_scalar(vT[:, :], v_ps[:, :], bias[:, 2, h:h + 1], None, ALU.add).then_inc(vT_ready, 1)
                else:
                    dve.tensor_copy(vT[:, :], v_ps[:, :]).then_inc(vT_ready, 1)
                dve.wait_ge(mn_ready, h + 1)
                if h:
                    dve.wait_ge(n_stored, 16 * h)
                if biased:
                    dve.tensor_copy(c_row[:, :], c_ps[:, :])
                dve.tensor_copy(Nst[:, :, :], n_ps[:, :, :]).then_inc(n_done, 1)
                if biased:
                    row = c_row[:, :].rearrange("p (b j) -> p b j", b=B)
                    dve.drain()
                    for i in range(3):
                        part = cM[32 * i:32 * i + 1, :, h * SC:(h + 1) * SC]
                        dve.tensor_copy(part, row)
                        if i < 2:
                            dve.drain()
                            dve.tensor_tensor(row, row, part, ALU.subtract)
                            dve.drain()


def cross_attend(core, tag, nh, M, N, scale, gate, src=None, cM=None, cM_ones=None, out_row=None,
                 guard=False):
    nc = core.nc
    W = nh * SC
    chunks = -(-W // P)
    groups = [list(range(k, min(k + 4, chunks))) for k in range(0, chunks, 4)]
    ngr = len(groups)
    cuts = [(a, min(a + 512, W)) for a in range(0, W, 512)]
    with ExitStack() as stack:
        st = Stage(core, tag, stack)
        hn = st.sb("hn", [P, D])
        hT = st.sb("hT", [P, DC, P])
        E = st.sb("E", [P, nh, SC])
        Pn = st.sb("Pn", [P, chunks * P])
        PT = st.sb("PT", [P, chunks, P])
        mx = st.sb("mx", [P, nh])
        l = st.sb("l", [P, nh])
        h_ps = st.ps("h_ps", [P, DC, P])
        s_ps = st.ps("s_ps", [P, 512 * len(cuts)])
        pt_ps = [st.ps(f"pt_ps{i}", [P, 4, P]) for i in range(ngr)]
        o_ps = st.ps("o_ps", [P, D])
        hn_ready = st.sem("hn_ready")
        ht_ready = st.sem("ht_ready")
        hT_ready = st.sem("hT_ready")
        s_ready = st.sem("s_ready")
        e_ready = st.sem("e_ready")
        exp_done = st.sem("exp_done")
        p_ready = st.sem("p_ready")
        pt_ready = st.sem("pt_ready")
        pT_ready = st.sem("pT_ready")
        o_ready = st.sem("o_ready")
        x_done = st.sem("x_done")
        block = stack.enter_context(nc.Block())
        s3 = s_ps[:, 0:W].rearrange("p (h j) -> p h j", h=nh)
        p3 = Pn[:, 0:W].rearrange("p (h j) -> p h j", h=nh)

        @block.vector
        def _(dve):
            def rows(t, first=False):
                if not first:
                    dve.wait_ge(ht_ready, t)
                if src is None:
                    normalise(dve, core, hn[:, :], t).then_inc(hn_ready, 1)
                else:
                    dve.tensor_copy(hn[:, :], src[:, t, :]).then_inc(hn_ready, 1)

            def front(t, first=False, last=False):
                if not last:
                    rows(t + 1)
                dve.wait_ge(s_ready, t + 1)
                dve.tensor_reduce(mx[:, :], s3, AX.X, ALU.max)
                dve.drain()
                dve.tensor_tensor(E[:, :, :], s3, mx[:, :].unsqueeze(2).to_broadcast([P, nh, SC]),
                                  ALU.subtract).then_inc(e_ready, 1)
                dve.wait_ge(exp_done, t + 1)
                dve.tensor_reduce(l[:, :], E[:, :, :], AX.X, ALU.add)
                dve.drain()
                dve.reciprocal(l[:, :], l[:, :])
                dve.drain()
                if not first:
                    dve.wait_ge(pt_ready, t * ngr)
                if guard:
                    dve.tensor_scalar(l[:, :], l[:, :], 0.0, None, ALU.max)
                    dve.drain()
                    dve.scalar_tensor_tensor(p3, E[:, :, :], 0.0, l[:, :].unsqueeze(2).to_broadcast([P, nh, SC]),
                                             ALU.max, ALU.mult).then_inc(p_ready, 1)
                else:
                    dve.tensor_tensor(p3, E[:, :, :], l[:, :].unsqueeze(2).to_broadcast([P, nh, SC]),
                                      ALU.mult).then_inc(p_ready, 1)

            def back(t):
                dve.wait_ge(o_ready, t + 1)
                dve.scalar_tensor_tensor(core.x[:, t, :], o_ps[:, :], gate, core.x[:, t, :],
                                         ALU.mult, ALU.add).then_inc(x_done, 1)

            dve.sem_inc(x_done, 1)
            if W % P:
                dve.memset(Pn[:, W:chunks * P], 0.0)
            rows(0, first=True)
            front(0, first=True)
            with dve.Fori(1, NT - 1) as t:
                front(t)
                back(t - 1)
            front(NT - 1, last=True)
            back(NT - 2)
            back(NT - 1)

        @block.scalar
        def _(act):
            def rows(t, first=False):
                act.wait_ge(ht_ready, t + 1)
                if not first:
                    act.wait_ge(s_ready, t)
                act.copy(hT[:, :, :], h_ps[:, :, :]).then_inc(hT_ready, 1)

            def front(t):
                act.wait_ge(e_ready, t + 1)
                act.activation(E[:, :, :], E[:, :, :], ACT.Exp, scale=scale).then_inc(exp_done, 1)

            def back(t):
                for g, ks in enumerate(groups):
                    act.wait_ge(pt_ready, t * ngr + g + 1)
                    act.copy(PT[:, ks[0]:ks[-1] + 1, :], pt_ps[g][:, 0:len(ks), :]).then_inc(pT_ready, 1)

            rows(0, first=True)
            rows(1)
            front(0)
            with act.Fori(1, NT - 1) as t:
                back(t - 1)
                rows(t + 1)
                front(t)
            back(NT - 2)
            front(NT - 1)
            back(NT - 1)

        @block.tensor
        def _(pe):
            def rows(t):
                pe.wait_ge(hn_ready, t + 1)
                for c in range(DC):
                    mm = pe.transpose(h_ps[:, c, :], hn[:, c * P:(c + 1) * P], core.ident[:, :])
                mm.then_inc(ht_ready, 1)

            def front(t, first=False):
                pe.wait_ge(hT_ready, t + 1)
                if not first:
                    pe.wait_ge(e_ready, t)
                b = t // TB
                for a, z in cuts:
                    for c in range(DC):
                        mm = pe.matmul(s_ps[:, a:z], hT[:, c, :], M[:, c, b, a:z], start=(c == 0),
                                       stop=(c == DC - 1 and cM is None))
                    if cM is not None:
                        ones = core.ones[:, :] if cM_ones is None else cM_ones
                        mm = pe.matmul(s_ps[:, a:z], ones, cM[:, b, a:z], start=False, stop=True)
                mm.then_inc(s_ready, 1)

            def turn(t):
                pe.wait_ge(p_ready, t + 1)
                for g, ks in enumerate(groups):
                    for i, k in enumerate(ks):
                        mm = pe.transpose(pt_ps[g][:, i, :], Pn[:, k * P:(k + 1) * P], core.ident[:, :])
                    mm.then_inc(pt_ready, 1)

            def back(t):
                pe.wait_ge(pT_ready, t * ngr + ngr)
                pe.wait_ge(x_done, t + 1)
                b = t // TB
                for k in range(chunks):
                    mm = pe.matmul(o_ps[:, :], PT[:, k, :], N[:, b, k, :], start=(k == 0),
                                   stop=(k == chunks - 1 and out_row is None))
                if out_row is not None:
                    mm = pe.matmul(o_ps[:, :], core.ones[:, :], out_row, start=False, stop=True)
                mm.then_inc(o_ready, 1)

            rows(0)
            front(0, first=True)
            rows(1)
            with pe.Fori(1, NT - 1) as t:
                front(t)
                turn(t - 1)
                rows(t + 1)
                back(t - 1)
            front(NT - 1)
            turn(NT - 2)
            back(NT - 2)
            turn(NT - 1)
            back(NT - 1)


def layer0_xattn(core, A):
    nh, hd = 16, 64
    W = nh * SC
    with ExitStack() as stack:
        st = Stage(core, "L0x", stack)
        M = st.sb("M", [P, DC, B, W])
        n_dram = core.nc.dram_tensor("L0x_n_dram", (B, W, D), F32, kind="Internal").ap()
        cross_prep(core, "L0p", {k: A["L0_" + k] for k in ("wk", "wv", "wq", "wo")}, nh, hd, M, n_dram, False,
                   load=lambda sp: load_x(sp, core, A))
        N = st.sb("N", [P, B, -(-W // P), D])
        zero_tail(core, "L0n", N[:, :, W // P, :])
        row_stats(core, "L0s", load=lambda sp, loaded: load_packed(sp, loaded, n_dram, N, W), x_arrives=True)
        cross_attend(core, "L0a", nh, M, N, hd ** -0.5, core.gates[:, 0, 0:1], guard=True)


def zero_tail(core, tag, tail):
    nc = core.nc
    with ExitStack() as stack:
        block = stack.enter_context(nc.Block())

        @block.vector
        def _(dve):
            dve.memset(tail, 0.0)


def load_packed(sp, loaded, n_dram, N, W):
    full, rest = W // P, W % P
    for b in range(B):
        sp.dma_start(N[:, b, 0:full, :], n_dram[b, 0:full * P, :].rearrange("(c p) o -> p c o", p=P)).then_inc(loaded, 16)
        sp.dma_start(N[0:rest, b, full, :], n_dram[b, full * P:W, :]).then_inc(loaded, 16)
    return 16 * B * 2


def batch_norm_stats(core, tag, A, bn_scale, bn_bias):
    nc = core.nc
    with ExitStack() as stack:
        st = Stage(core, tag, stack)
        hn = [st.sb(f"hn{u}", [P, D]) for u in range(2)]
        stats = st.sb("stats", [P, DC, NT // 2, 6])
        mv = st.sb("mv", [P, DC, 2])
        gb = st.sb("gb", [P, 2, DC])
        ve = st.sb("ve", [P, DC])
        h_ps = [st.ps(f"h_ps{u}", [P, DC, 2, P]) for u in range(2)]
        loaded = st.sem("loaded")
        hn_ready = st.sem("hn_ready")
        ht_ready = st.sem("ht_ready")
        ht_used = st.sem("ht_used")
        var_ready, std_ready = st.sem("var_ready"), st.sem("std_ready")
        block = stack.enter_context(nc.Block())

        @block.sync
        def _(sp):
            sp.dma_start(gb[:, :, :], A["bn"]).then_inc(loaded, 16)

        @block.vector
        def _(dve):
            def rows(k):
                for u in range(2):
                    dve.wait_ge(ht_ready, 2 * k + u + 1)
                    normalise(dve, core, hn[u][:, :], 2 * k + u).then_inc(hn_ready, 1)

            def pair(k, w):
                dve.wait_ge(ht_ready, 2 * k + 4)
                for c in range(DC):
                    bn = dve.bn_stats(stats[:, c, k, :], h_ps[w][:, c, :, :])
                bn.then_inc(ht_used, 1)

            dve.sem_inc(ht_used, 2)
            rows(0)
            with dve.Fori(0, NT // 4 - 1) as k:
                rows(2 * k + 1)
                pair(2 * k, 0)
                rows(2 * k + 2)
                pair(2 * k + 1, 1)
            rows(NT // 2 - 1)
            pair(NT // 2 - 2, 0)
            pair(NT // 2 - 1, 1)
            dve.drain()
            for c in range(DC):
                dve.bn_aggr(mv[:, c, :], stats[:, c, :, :])
            dve.drain()
            dve.tensor_scalar(ve[:, :], mv[:, :, 1], EPS, None, ALU.add).then_inc(var_ready, 1)
            dve.wait_ge(std_ready, 1)
            dve.reciprocal(ve[:, :], ve[:, :])
            dve.drain()
            dve.wait_ge(loaded, 16)
            dve.tensor_tensor(bn_scale, ve[:, :], gb[:, 0, :], ALU.mult)
            dve.drain()
            dve.tensor_tensor(ve[:, :], mv[:, :, 0], bn_scale, ALU.mult)
            dve.drain()
            dve.tensor_tensor(bn_bias, gb[:, 1, :], ve[:, :], ALU.subtract)

        @block.tensor
        def _(pe):
            pe.sem_inc(ht_ready, 2)
            with pe.Fori(0, NT // 4) as k:
                for w in range(2):
                    pe.wait_ge(ht_used, 2 * k + w + 1)
                    for u in range(2):
                        pe.wait_ge(hn_ready, 2 * (2 * k + w) + u + 1)
                        for c in range(DC):
                            mm = pe.transpose(h_ps[w][:, c, u, :], hn[u][:, c * P:(c + 1) * P], core.ident[:, :])
                        mm.then_inc(ht_ready, 1)

        @block.scalar
        def _(act):
            act.wait_ge(var_ready, 1)
            act.activation(ve[:, :], ve[:, :], ACT.Sqrt).then_inc(std_ready, 1)


def fold_keys(core, tag, A, groups, hd, nk, G):
    nc = core.nc
    with ExitStack() as stack:
        st = Stage(core, tag, stack)
        wq = st.sb("wq", [hd, groups, D])
        keys = st.sb("keys", [hd, groups, nk])
        g_ps = [st.ps(f"g_ps{u}", [P, DC, nk]) for u in range(2)]
        loaded, g_ready, g_done = st.sem("loaded"), st.sem("g_ready"), st.sem("g_done")
        block = stack.enter_context(nc.Block())

        @block.sync
        def _(sp):
            sp.dma_start(wq[:, :, :], A["wq"]).then_inc(loaded, 16)
            sp.dma_start(keys[:, :, :], A["keys"]).then_inc(loaded, 16)

        @block.tensor
        def _(pe):
            pe.wait_ge(loaded, 32)
            for g in range(groups):
                if g >= 2:
                    pe.wait_ge(g_done, g - 1)
                for c in range(DC):
                    mm = pe.matmul(g_ps[g % 2][:, c, :], wq[:, g, c * P:(c + 1) * P], keys[:, g, :], start=True, stop=True)
                mm.then_inc(g_ready, 1)

        @block.scalar
        def _(act):
            for g in range(groups):
                act.wait_ge(g_ready, g + 1)
                act.copy(G[:, :, g * nk:(g + 1) * nk], g_ps[g % 2][:, :, :]).then_inc(g_done, 1)


def product_key_experts(core, tag, table, nh, nk, G, gate, last_expert=None, bn=None, soft=False, mlp=None):
    nc = core.nc
    groups = 2 * nh
    K = 8
    NE = nh * K
    NC = NE // K
    RC = 4
    assert NC % RC == 0 and groups * nk == 1024
    with ExitStack() as stack:
        st = Stage(core, tag, stack)
        hq = st.sb("hq", [P, D])
        hn = [st.sb(f"hn{u}", [P, D]) for u in range(2)]
        hT = st.sb("hT", [P, DC, P])
        val = st.sb("val", [P, groups, K])
        pos = st.sb("pos", [P, groups, K], U32)
        posf = st.sb("posf", [P, groups, K])
        sums = st.sb("sums", [P, nh, K, K])
        top = [st.sb(f"top{u}", [P, nh, K]) for u in range(2)]
        pick = st.sb("pick", [P, nh, K], U32)
        half = st.sb("half", [P, 2, nh * K], U32)
        halff = st.sb("halff", [P, 2, nh * K])
        count = st.sb("count", [P, K])
        hot = st.sb("hot", [P, 2, nh * K, K])
        chosen = st.sb("chosen", [P, 2, nh * K])
        idx = [st.sb(f"idx{u}", [P, NE], U32) for u in range(2)]
        weigh = [st.sb(f"weigh{u}", [P, NE]) for u in range(2)]
        total = st.sb("total", [P, nh])
        ring = st.sb("ring", [P, RC * K, 2 * D])
        dot = st.sb("dot", [P, NE])
        mid = st.sb("mid", [P, NE])
        w = st.sb("w", [P, NE])
        diag = st.sb("diag", [P, 2, K, P])
        h_ps = st.ps("h_ps", [P, DC, P])
        s_ps = st.ps("s_ps", [P, 2, 512])
        o_ps = [st.ps(f"o_ps{u}", [P, D]) for u in range(2)]
        if mlp:
            HC = FC // 2
            wg = st.sb("wg", [P, DC, F])
            wu = st.sb("wu", [P, DC, F])
            wd = st.sb("wd", [P, FC, D])
            sg = st.sb("sg", [P, HC, P])
            aT = [st.sb(f"aT{u}", [P, FC, P]) for u in range(2)]
            g_ps = st.ps("g_ps", [P, HC, P])
            u_ps = st.ps("u_ps", [P, HC, P])
            mlp_loaded = st.sem("mlp_loaded")
            gu_ready = st.sem("gu_ready")
            sg_ready = st.sem("sg_ready")
            a_done = st.sem("a_done")
        hq_ready = st.sem("hq_ready")
        ht_ready = st.sem("ht_ready")
        hT_ready = st.sem("hT_ready")
        s_ready = st.sem("s_ready")
        s_used = st.sem("s_used")
        top_ready = st.sem("top_ready")
        idx_ready = st.sem("idx_ready")
        weigh_ready = st.sem("weigh_ready")
        gathered = [st.sem(f"gathered{i}") for i in range(RC)]
        dots_ready = st.sem("dots_ready")
        act_done = st.sem("act_done")
        w_ready = st.sem("w_ready")
        diag_ready = st.sem("diag_ready")
        up_done = st.sem("up_done")
        x_done = st.sem("x_done")
        counted = st.sem("counted")
        pool_steps, dve_steps = st.sem("pool_steps"), st.sem("dve_steps")
        block = stack.enter_context(nc.Block())
        s2 = s_ps[:, :, :].rearrange("p a b -> p (a b)")

        def run(eng, experts):
            experts(0, 0, first=True)
            with eng.Fori(0, NT // 2 - 2) as k:
                experts(2 * k + 1, 1)
                experts(2 * k + 2, 0)
            experts(NT - 3, 1)
            experts(NT - 2, 0, left=1)
            experts(NT - 1, 1, left=0)

        if mlp:
            @block.sync
            def _(sp):
                sp.dma_start(wg[:, :, :], mlp["wg"].rearrange("(c p) e -> p c e", p=P)).then_inc(mlp_loaded, 16)
                sp.dma_start(wu[:, :, :], mlp["wu"].rearrange("(c p) e -> p c e", p=P)).then_inc(mlp_loaded, 16)
                sp.dma_start(wd[:, :, :], mlp["wd"].rearrange("(c p) e -> p c e", p=P)).then_inc(mlp_loaded, 16)

        @block.gpsimd
        def _(pool):
            pool.iota(count[:, :], [[1, K]], base=0, channel_multiplier=0,
                      allow_small_or_imprecise_dtypes=True).then_inc(counted, 1)

            def experts(t, u, first=False, left=2):
                pool.wait_ge(idx_ready, t + 1)
                for c in range(NC):
                    pool.wait_ge(up_done, t * NC + c + 1)
                    pool.sem_inc(pool_steps, 1)
                    for i in range(K):
                        e = c * K + i
                        pool.indirect_dma_start(ring[:, (c % RC) * K + i, :], None, table,
                                                bass.IndirectOffsetOnAxis(ap=idx[u][:, e:e + 1], axis=0)
                                                ).then_inc(gathered[c % RC], 16)

            run(pool, experts)

        @block.vector
        def _(dve):
            def search(t, first=False):
                if not first:
                    dve.wait_ge(ht_ready, t)
                normalise(dve, core, hq[:, :], t).then_inc(hq_ready, 1)

            def best_keys(t, u):
                normalise(dve, core, hn[u][:, :], t)
                dve.wait_ge(s_ready, t + 1)
                dve.sem_inc(dve_steps, 1)
                for g in range(groups):
                    dve.max(val[:, g, :], s2[:, g * nk:(g + 1) * nk])
                dve.drain()
                for g in range(groups):
                    dve.max_index(pos[:, g, :], val[:, g, :], s2[:, g * nk:(g + 1) * nk])
                dve.drain().then_inc(s_used, 1)

            def best_sums(t, u):
                dve.tensor_copy(posf[:, :, :], pos[:, :, :])
                dve.tensor_tensor(sums[:, :, :, :], val[:, 0:nh, :].unsqueeze(3).to_broadcast([P, nh, K, K]),
                                  val[:, nh:groups, :].unsqueeze(2).to_broadcast([P, nh, K, K]), ALU.add)
                dve.drain()
                for h in range(nh):
                    dve.max(top[u][:, h, :], sums[:, h, :, :])
                dve.drain()
                for h in range(nh):
                    dve.max_index(pick[:, h, :], top[u][:, h, :], sums[:, h, :, :].rearrange("p i j -> p (i j)"))
                dve.drain()
                if soft:
                    dve.tensor_tensor(weigh[u][:, :].rearrange("p (h k) -> p h k", k=K), top[u][:, :, :],
                                      top[u][:, :, 0:1].to_broadcast([P, nh, K]), ALU.subtract).then_inc(top_ready, 1)
                else:
                    dve.sem_inc(top_ready, 1)

            def choice(t, u):
                flat = pick[:, :, :].rearrange("p h k -> p (h k)")
                dve.tensor_scalar(half[:, 0, :], flat, 3, None, ALU.logical_shift_right)
                dve.tensor_scalar(half[:, 1, :], flat, K - 1, None, ALU.bitwise_and)
                dve.drain()
                dve.tensor_copy(halff[:, :, :], half[:, :, :])
                dve.drain()
                for p in range(2):
                    dve.tensor_tensor(hot[:, p, :, :], halff[:, p, :].unsqueeze(2).to_broadcast([P, nh * K, K]),
                                      count[:, :].unsqueeze(1).to_broadcast([P, nh * K, K]), ALU.is_equal)
                dve.drain()
                for p in range(2):
                    hot4 = hot[:, p, :, :].rearrange("p (h k) i -> p h k i", k=K)
                    dve.tensor_tensor(hot4, hot4, posf[:, p * nh:(p + 1) * nh, :].unsqueeze(2).to_broadcast([P, nh, K, K]),
                                      ALU.mult)
                dve.drain()
                dve.tensor_reduce(chosen[:, :, :], hot[:, :, :, :], AX.X, ALU.add)
                dve.drain()
                if last_expert is None:
                    dve.scalar_tensor_tensor(idx[u][:, :], chosen[:, 0, :], float(nk), chosen[:, 1, :],
                                             ALU.mult, ALU.add).then_inc(idx_ready, 1)
                else:
                    dve.scalar_tensor_tensor(chosen[:, 0, :], chosen[:, 0, :], float(nk), chosen[:, 1, :], ALU.mult, ALU.add)
                    dve.drain()
                    dve.tensor_scalar(idx[u][:, :], chosen[:, 0, :], float(last_expert), None, ALU.min).then_inc(idx_ready, 1)

            def shares(t, u):
                if soft:
                    dve.wait_ge(weigh_ready, t + 1)
                    w3 = weigh[u][:, :].rearrange("p (h k) -> p h k", k=K)
                    dve.tensor_reduce(total[:, :], w3, AX.X, ALU.add)
                    dve.drain()
                    dve.reciprocal(total[:, :], total[:, :])
                    dve.drain()
                    dve.tensor_tensor(w3, w3, total[:, :].unsqueeze(2).to_broadcast([P, nh, K]), ALU.mult)

            def update(t, u):
                dve.wait_ge(up_done, (t + 1) * NC + RC)
                dve.scalar_tensor_tensor(core.x[:, t, :], o_ps[u][:, :], gate, core.x[:, t, :],
                                         ALU.mult, ALU.add).then_inc(x_done, 1)

            def weights(t, u, c):
                e = slice(c * K, (c + 1) * K)
                dve.wait_ge(act_done, t * NC + c + 1)
                dve.tensor_tensor(w[:, e], mid[:, e], weigh[u][:, e], ALU.mult).then_inc(w_ready, 1)

            def experts(t, u, first=False, left=2):
                for c in range(NC):
                    dve.wait_ge(gathered[c % RC], 16 * K * (t * (NC // RC) + c // RC + 1))
                    for i in range(K):
                        e = c * K + i
                        down = ring[:, (c % RC) * K + i, 0:D]
                        tr = dve.tensor_tensor_reduce(down, down, hn[u][:, :], 1.0, 0.0,
                                                      ALU.mult, ALU.add, dot[:, e:e + 1])
                    tr.then_inc(dots_ready, 1)
                    if c:
                        weights(t, u, c - 1)
                    if c == 1 and not first:
                        update(t - 1, 1 - u)
                    if left:
                        if c < 4:
                            (best_keys, best_sums, choice, shares)[c](t + 1, 1 - u)
                        if mlp and c >= NC - 2:
                            hidden(t + 1, 1 - u, c - (NC - 2))
                    if c == NC - 2 and left > 1:
                        search(t + 2)
                weights(t, u, NC - 1)

            def hidden(t, u, half):
                dve.wait_ge(sg_ready, 2 * t + half + 1)
                dve.tensor_tensor(aT[u][:, half * HC:(half + 1) * HC, :], u_ps[:, :, :], sg[:, :, :],
                                  ALU.mult).then_inc(a_done, 1)

            dve.sem_inc(s_used, 1)
            dve.sem_inc(x_done, 2)
            if mlp:
                dve.sem_inc(a_done, 1)
            dve.wait_ge(counted, 1)
            search(0, first=True)
            for piece in (best_keys, best_sums, choice, shares):
                piece(0, 0)
            if mlp:
                hidden(0, 0, 0)
                hidden(0, 0, 1)
            search(1)
            run(dve, experts)
            update(NT - 1, 1)

        @block.scalar
        def _(act):
            def search(t):
                act.wait_ge(ht_ready, t + 1)
                for c in range(DC):
                    if bn is None:
                        cp = act.copy(hT[:, c, :], h_ps[:, c, :])
                    else:
                        cp = act.activation(hT[:, c, :], h_ps[:, c, :], ACT.Identity, bias=bn[1][:, c:c + 1],
                                            scale=bn[0][:, c:c + 1])
                cp.then_inc(hT_ready, 1)

            def score_weights(t, u):
                act.wait_ge(top_ready, t + 1)
                if soft:
                    act.activation(weigh[u][:, :], weigh[u][:, :], ACT.Exp).then_inc(weigh_ready, 1)
                else:
                    act.activation(weigh[u][:, :], top[u][:, :, :].rearrange("p h k -> p (h k)"), ACT.Sigmoid).then_inc(weigh_ready, 1)

            def spread(t, u, c):
                act.wait_ge(w_ready, t * NC + c + 1)
                act.wait_ge(up_done, t * NC + c + RC - 1)
                for i in range(K):
                    e = c * K + i
                    cp = act.mul(diag[:, c % 2, i, :], core.ident[:, :], w[:, e:e + 1])
                cp.then_inc(diag_ready, 1)

            def experts(t, u, first=False, left=2):
                for c in range(NC):
                    e = slice(c * K, (c + 1) * K)
                    act.wait_ge(dots_ready, t * NC + c + 1)
                    act.activation(mid[:, e], dot[:, e], ACT.Silu if soft else ACT.Gelu).then_inc(act_done, 1)
                    if c:
                        spread(t, u, c - 1)
                    if left:
                        if c == 2:
                            score_weights(t + 1, 1 - u)
                        if mlp and c >= NC - 2:
                            hidden(t + 1, 1 - u, c - (NC - 2))
                    if c == NC - 1 and left > 1:
                        search(t + 2)
                spread(t, u, NC - 1)

            def hidden(t, u, half):
                act.wait_ge(gu_ready, 2 * t + half + 1)
                act.activation(sg[:, :, :], g_ps[:, :, :], ACT.Silu).then_inc(sg_ready, 1)

            search(0)
            score_weights(0, 0)
            if mlp:
                hidden(0, 0, 0)
                hidden(0, 0, 1)
            search(1)
            run(act, experts)

        @block.tensor
        def _(pe):
            def search(t):
                pe.wait_ge(hq_ready, t + 1)
                for c in range(DC):
                    mm = pe.transpose(h_ps[:, c, :], hq[:, c * P:(c + 1) * P], core.ident[:, :])
                mm.then_inc(ht_ready, 1)
                pe.wait_ge(hT_ready, t + 1)
                pe.wait_ge(s_used, t + 1)
                for n in range(2):
                    for c in range(DC):
                        mm = pe.matmul(s_ps[:, n, :], hT[:, c, :], G[:, c, n * 512:(n + 1) * 512], start=(c == 0), stop=(c == DC - 1))
                mm.then_inc(s_ready, 1)

            def experts(t, u, first=False, left=2):
                pe.wait_ge(x_done, t + 1)
                for c in range(NC):
                    pe.wait_ge(diag_ready, t * NC + c + 1)
                    for i in range(K):
                        mm = pe.matmul(o_ps[u][:, :], diag[:, c % 2, i, :], ring[:, (c % RC) * K + i, D:2 * D],
                                       start=(c == 0 and i == 0), stop=(c == NC - 1 and i == K - 1))
                    mm.then_inc(up_done, 1)
                    if c == 0 and mlp:
                        pe.wait_ge(a_done, 2 * t + 3)
                        for k in range(FC):
                            pe.matmul(o_ps[u][:, :], aT[u][:, k, :], wd[:, k, :], start=False, stop=False)
                    if mlp and left and c < 2:
                        hidden(t + 1, 1 - u, c)
                    if c == NC - 2 and left > 1:
                        search(t + 2)

            def hidden(t, u, half):
                pe.wait_ge(a_done, 2 * t + half + 1)
                for w, ps in ((wg, g_ps), (wu, u_ps)):
                    for k in range(HC):
                        for c in range(DC):
                            f = (half * HC + k) * P
                            mm = pe.matmul(ps[:, k, :], w[:, c, f:f + P], hT[:, c, :], start=(c == 0), stop=(c == DC - 1))
                mm.then_inc(gu_ready, 1)

            pe.sem_inc(up_done, RC)
            search(0)
            if mlp:
                pe.wait_ge(mlp_loaded, 48)
                hidden(0, 0, 0)
                hidden(0, 0, 1)
            search(1)
            run(pe, experts)


def layer0_ffn(core, A):
    nh, nk = 8, 64
    with ExitStack() as stack:
        st = Stage(core, "L0f", stack)
        G = st.sb("G", [P, DC, 2 * nh * nk])
        bn_scale = st.sb("bn_scale", [P, DC])
        bn_bias = st.sb("bn_bias", [P, DC])
        row_stats(core, "L0t")
        batch_norm_stats(core, "L0b", {"bn": A["L0_bn"]}, bn_scale[:, :], bn_bias[:, :])
        fold_keys(core, "L0g", {"wq": A["L0_pq"], "keys": A["L0_keys"]}, 2 * nh, 128, nk, G)
        product_key_experts(core, "L0e", A["L0_table"], nh, nk, G, core.gates[:, 1, 0:1], bn=(bn_scale, bn_bias))


def context_norm(core, tag, A, cxT, mask_row):
    nc = core.nc
    with ExitStack() as stack:
        st = Stage(core, tag, stack)
        ctx = st.sb("ctx", [SC, B, D])
        gb = st.sb("gb", [P, 2, DC])
        mask = st.sb("mask", [1, CT], U8)
        stats = st.sb("stats", [SC, B, 6])
        mv = st.sb("mv", [SC, B, 2])
        std = st.sb("std", [SC, B])
        c_ps = [st.ps(f"c_ps{u}", [P, DC, SC]) for u in range(2)]
        loaded = st.sem("loaded")
        var_ready, std_ready = st.sem("var_ready"), st.sem("std_ready")
        hn_ready, ht_ready, done = st.sem("hn_ready"), st.sem("ht_ready"), st.sem("done")
        block = stack.enter_context(nc.Block())

        @block.sync
        def _(sp):
            sp.dma_start(ctx[:, :, :], A["ctx"]).then_inc(loaded, 16)
            sp.dma_start(gb[:, :, :], A["ln_x"]).then_inc(loaded, 16)
            sp.dma_start(mask[:, :], A["mask"]).then_inc(loaded, 16)

        @block.vector
        def _(dve):
            dve.wait_ge(loaded, 48)
            dve.tensor_copy(mask_row, mask[:, :])
            for b in range(B):
                dve.bn_stats(stats[:, b, :], ctx[:, b, :])
            dve.drain()
            dve.tensor_scalar(mask_row, mask_row, 1.0, -MASKED, ALU.subtract, ALU.mult)
            for b in range(B):
                dve.bn_aggr(mv[:, b, :], stats[:, b, :])
            dve.drain()
            dve.tensor_scalar(std[:, :], mv[:, :, 1], EPS, None, ALU.add).then_inc(var_ready, 1)
            dve.wait_ge(std_ready, 1)
            dve.reciprocal(std[:, :], std[:, :])
            dve.drain()
            for b in range(B):
                dve.tensor_scalar(ctx[:, b, :], ctx[:, b, :], mv[:, b, 0:1], std[:, b:b + 1], ALU.subtract,
                                  ALU.mult).then_inc(hn_ready, 1)

        @block.scalar
        def _(act):
            act.wait_ge(var_ready, 1)
            act.activation(std[:, :], std[:, :], ACT.Sqrt).then_inc(std_ready, 1)
            for b in range(B):
                act.wait_ge(ht_ready, b + 1)
                for c in range(DC):
                    cp = act.activation(cxT[:, c, b * SC:(b + 1) * SC], c_ps[b % 2][:, c, :], ACT.Identity,
                                        bias=gb[:, 1, c:c + 1], scale=gb[:, 0, c:c + 1])
                cp.then_inc(done, 1)

        @block.tensor
        def _(pe):
            for b in range(B):
                pe.wait_ge(hn_ready, b + 1)
                if b >= 2:
                    pe.wait_ge(done, b - 1)
                for c in range(DC):
                    mm = pe.transpose(c_ps[b % 2][:, c, :], ctx[:, b, c * P:(c + 1) * P], core.ident[0:SC, 0:SC])
                mm.then_inc(ht_ready, 1)


def counts(sizes):
    out = [0]
    for n in sizes:
        out.append(out[-1] + n)
    return out[:-1], out[-1]


def long_attention(core, tag, A, y, heads, hd, slot, scale, affine=None, cxT=None, mask_row=None, causal=False,
                   biased=False):
    nc = core.nc
    NG = 16 // heads
    VW = heads * hd
    OC = NG * VW // P
    KX = SC if cxT is not None else 0
    KT = S + KX
    ktiles = [(a, min(a + P, KT)) for a in range(0, KT, P)]
    key_cuts = [(a, min(a + 512, KT)) for a in range(0, KT, 512)]
    vper = min(512 // VW, 4)
    vgroups = [ktiles[a:a + vper] for a in range(0, len(ktiles), vper)]
    projections = [("q", c) for c in ((0, 512), (512, 1024))] + [("k", c) for c in key_cuts] + \
                  [("v", g) for g in vgroups]
    NJ = len(projections)
    NJA, NJV = (NJ + 1) // 2, NJ // 2
    NQK = 2 + len(key_cuts)
    early, rest = range(NQK + 1), range(NQK + 1, NJ)
    units = [(j, i) for j in range(heads) for i in range(TB)]
    UN = len(units)

    def tiles_of(i):
        return ktiles[:i + 1] if causal else ktiles

    def tgroups(i):
        n = len(tiles_of(i))
        return [range(a, min(a + 4, n)) for a in range(0, n, 4)]

    t_at, t_all = counts([len(tgroups(i)) for _, i in units])
    a_at, a_all = counts([(len(tgroups(i)) + 1) // 2 for _, i in units])
    v_at, v_all = counts([len(tgroups(i)) // 2 for _, i in units])
    ogroups = [range(a, min(a + 4, OC)) for a in range(0, OC, 4)]
    ahead = 1 if KX else 2
    late = 0 if KX else 1
    s_banks = 5 if KX else 4
    s_at = (0, 3 * 512 - KX if KX else 2 * 512)

    def place(u, a):
        if u == 0 or not KX:
            return a
        return a + KX if a < S else a - S

    with ExitStack() as stack:
        st = Stage(core, tag, stack)
        hn = [st.sb(f"hn{u}", [P, D]) for u in range(2)]
        kvT = st.sb("kvT", [P, DC, KT])
        wq = st.sb("wq", [P, DC, P])
        wk = st.sb("wk", [P, DC, P])
        wv = st.sb("wv", [P, DC, VW])
        wo = st.sb("wo", [P, OC, D])
        qT = st.sb("qT", [P, heads, S])
        kT = st.sb("kT", [P, KT])
        V = st.sb("V", [P, len(ktiles), VW])
        E = [st.sb(f"E{u}", [P, KT]) for u in range(2)]
        nmax = st.sb("nmax", [P, 2])
        l = st.sb("l", [P, UN])
        rl = st.sb("rl", [P, UN])
        PT = [st.sb(f"PT{u}", [P, len(ktiles), P]) for u in range(2)]
        O = st.sb("O", [P, TB, NG * VW])
        if biased:
            qk_bias = st.sb("qk_bias", [P, 2, NG])
            q_bias = st.sb("q_bias", [P, NG])
            v_bias = st.sb("v_bias", [1, NG, VW])
            o_bias = st.sb("o_bias", [1, D])
        if causal:
            cmask = st.sb("cmask", [P, P], BF16)
            identb = st.sb("identb", [P, P], BF16)
        if KX:
            onesb = st.sb("onesb", [1, P], BF16)
        s_ps = st.ps("s_ps", [P, 512 * s_banks])
        t_ps = [st.ps(f"t_ps{i}", [P, 512]) for i in range(2)]
        misc_ps = [st.ps(f"misc_ps{i}", [P, 512]) for i in range(8 - s_banks - 2)]
        o_ps = [misc_ps[u % len(misc_ps)][:, u * hd:(u + 1) * hd] for u in range(2)]
        t_ps.append(misc_ps[0][:, 128:256])
        y_ps = misc_ps[0][:, 256:512]
        consts = st.sem("consts")
        w_loaded = st.sem("w_loaded")
        hn_ready = st.sem("hn_ready")
        ht_ready = st.sem("ht_ready")
        hT_ready = st.sem("hT_ready")
        cx_ready = st.sem("cx_ready")
        pj_ready = st.sem("pj_ready")
        pj_act = st.sem("pj_act")
        pj_dve = st.sem("pj_dve")
        s_ready = st.sem("s_ready")
        max_ready = st.sem("max_ready")
        e_ready = st.sem("e_ready")
        t_ready = st.sem("t_ready")
        tc_act = st.sem("tc_act")
        tc_dve = st.sem("tc_dve")
        o_ready = st.sem("o_ready")
        o_done = st.sem("o_done")
        ot_ready = st.sem("ot_ready")
        oT_ready = st.sem("oT_ready")
        y_ready = st.sem("y_ready")
        y_done = st.sem("y_done")
        zeroed = st.sem("zeroed")
        masked = st.sem("masked")
        pe_steps = st.sem("pe_steps")
        OT = PT
        assert OC <= len(ktiles)
        block = stack.enter_context(nc.Block())

        @block.sync
        def _(sp):
            n_const = 1
            sp.dma_start(wo[:, :, :], A["wo"].rearrange("(c p) o -> p c o", p=P)).then_inc(consts, 16)
            if biased:
                sp.dma_start(qk_bias[:, :, :], A["qk_bias"]).then_inc(consts, 16)
                sp.dma_start(v_bias[:, :, :], A["v_bias"]).then_inc(consts, 16)
                sp.dma_start(o_bias[:, :], A["o_bias"]).then_inc(consts, 16)
                n_const = 4
            sp.wait_ge(consts, 16 * n_const)

            def weights(n, g, first=False):
                if not first:
                    sp.wait_ge(pj_ready, n * NJ)
                for w, name in ((wq, "wq"), (wk, "wk"), (wv, "wv")):
                    sp.dma_start(w[:, :, :], A[name][:, g, :].rearrange("(c p) e -> p c e", p=P)).then_inc(w_loaded, 16)

            weights(0, 0, first=True)
            with sp.Fori(1, B * NG) as n:
                weights(n, n % NG)

        @block.gpsimd
        def _(pool):
            pool.memset(qT[:, :, :], 0.0).then_inc(zeroed, 1)
            if KX:
                pool.memset(onesb[:, :], 1.0).then_inc(masked, 1)
            if causal:
                pool.memset(cmask[:, :], 0.0)
                pool.tensor_copy(identb[:, :], core.ident[:, :])
                pool.drain()
                pool.affine_select(cmask[:, :], cmask[:, :], [[-1, P]], ALU.is_ge, MASKED, base=0,
                                   channel_multiplier=1).then_inc(masked, 1)

        @block.tensor
        def _(pe):
            pe.wait_ge(consts, 16 * (4 if biased else 1))
            if causal or KX:
                pe.wait_ge(masked, 1)

            def scores(b, n, m):
                j, i = units[m]
                u = m % 2
                kn = tiles_of(i)[-1][1]
                for a, z in key_cuts:
                    z = min(z, kn, S)
                    if a >= z:
                        continue
                    diag = causal and z == kn
                    at = s_at[u] + place(u, a)
                    mm = pe.matmul(s_ps[:, at:at + z - a], qT[:, j, i * P:(i + 1) * P], kT[:, a:z], start=True, stop=not diag)
                    if diag:
                        mm = pe.matmul(s_ps[:, at + z - a - P:at + z - a], identb[:, :], cmask[:, :], start=False, stop=True)
                if not KX:
                    mm.then_inc(s_ready, 1)

            def context_scores(b, n, m):
                j, i = units[m]
                at = s_at[m % 2] + place(m % 2, S)
                pe.matmul(s_ps[:, at:at + KX], qT[:, j, i * P:(i + 1) * P], kT[:, S:KT], start=True, stop=False)
                pe.matmul(s_ps[:, at:at + KX], onesb[:, :], mask_row[:, bass.ds(b * SC, SC)], start=False,
                          stop=True).then_inc(s_ready, 1)

            def turn(n, m):
                j, i = units[m]
                pe.wait_ge(e_ready, n * UN + m + 1)
                if late and m:
                    copied(n, m - 1)
                ks = tiles_of(i)
                for x, g in enumerate(tgroups(i)):
                    if x == 2:
                        pe.wait_ge(o_done, n * UN + m + 2)
                    for k in g:
                        a, z = ks[k]
                        at = place(m % 2, a)
                        mm = pe.transpose(t_ps[x][0:z - a, (k - g[0]) * P:(k - g[0] + 1) * P], E[m % 2][:, at:at + z - a], core.ident[:, :])
                    mm.then_inc(t_ready, 1)

            def copied(n, m):
                i = units[m][1]
                pe.wait_ge(tc_act, n * a_all + a_at[m] + (len(tgroups(i)) + 1) // 2)
                if len(tgroups(i)) > 1:
                    pe.wait_ge(tc_dve, n * v_all + v_at[m] + len(tgroups(i)) // 2)

            def values(n, m):
                j, i = units[m]
                ks = tiles_of(i)
                copied(n, m)
                pe.wait_ge(o_done, n * UN + m + 1)
                for k, (a, z) in enumerate(ks):
                    mm = pe.matmul(o_ps[m % 2], PT[m % 2][0:z - a, k, :], V[0:z - a, k, j * hd:(j + 1) * hd],
                                   start=(k == 0), stop=(k == len(ks) - 1))
                mm.then_inc(o_ready, 1)

            def project(n, g, x):
                kind, what = projections[x]
                if x >= 2:
                    if x % 2:
                        pe.wait_ge(pj_dve, n * NJV + x // 2)
                    else:
                        pe.wait_ge(pj_act, n * NJA + x // 2)
                ps = t_ps[x % 2]
                if kind in "qk":
                    a, z = what
                    w = wq if kind == "q" else wk
                    for c in range(DC):
                        mm = pe.matmul(ps[:, 0:z - a], w[:, c, :], kvT[:, c, a:z], start=(c == 0), stop=(c == DC - 1))
                else:
                    for v, (a, z) in enumerate(what):
                        out = ps[0:z - a, v * VW:(v + 1) * VW]
                        for c in range(DC):
                            mm = pe.matmul(out, kvT[:, c, a:z], wv[:, c, :], start=(c == 0), stop=(c == DC - 1 and not biased))
                        if biased:
                            mm = pe.matmul(out, core.ones[:, 0:z - a], v_bias[:, g, :], start=False, stop=True)
                mm.then_inc(pj_ready, 1)

            with pe.Fori(0, B) as b:
                for i in range(TB):
                    pe.wait_ge(hn_ready, b * TB + i + 1)
                    if i >= 2:
                        pe.wait_ge(hT_ready, b * TB + i - 1)
                    for c in range(DC):
                        mm = pe.transpose(t_ps[i % 2][:, c * P:(c + 1) * P], hn[i % 2][:, c * P:(c + 1) * P], core.ident[:, :])
                    mm.then_inc(ht_ready, 1)
                pe.wait_ge(hT_ready, (b + 1) * TB)
                if KX:
                    pe.wait_ge(cx_ready, b + 1)
                pe.sem_inc(pe_steps, 1)
                with pe.Fori(0, NG) as g:
                    n = b * NG + g
                    pe.wait_ge(w_loaded, (n + 1) * 48)
                    for x in early:
                        project(n, g, x)
                    pe.wait_ge(pj_act, n * NJA + (NQK + 1) // 2)
                    pe.wait_ge(pj_dve, n * NJV + NQK // 2)
                    scores(b, n, 0)
                    if KX:
                        context_scores(b, n, 0)
                    scores(b, n, 1)
                    for x in rest:
                        project(n, g, x)
                    pe.wait_ge(pj_act, (n + 1) * NJA)
                    pe.wait_ge(pj_dve, (n + 1) * NJV)
                    for m in range(UN):
                        turn(n, m)
                        if KX and m + 1 < UN:
                            context_scores(b, n, m + 1)
                        if m + 2 < UN:
                            scores(b, n, m + 2)
                        if m >= late:
                            values(n, m - late)
                    if late:
                        values(n, UN - 1)
                pe.wait_ge(o_done, (b + 1) * NG * UN + 2)
                for i in range(TB + 1):
                    if i:
                        pe.wait_ge(oT_ready, (b * TB + i) * len(ogroups))
                    if i < TB:
                        for x, g in enumerate(ogroups):
                            for k in g:
                                mm = pe.transpose(t_ps[x][:, (k - g[0]) * P:(k - g[0] + 1) * P], O[:, i, k * P:(k + 1) * P], core.ident[:, :])
                            mm.then_inc(ot_ready, 1)
                    if not i:
                        continue
                    pe.wait_ge(y_done, b * TB + i)
                    for k in range(OC):
                        mm = pe.matmul(y_ps, OT[(i - 1) % 2][:, k, :], wo[:, k, :], start=(k == 0), stop=(k == OC - 1 and not biased))
                    if biased:
                        mm = pe.matmul(y_ps, core.ones[:, :], o_bias[:, :], start=False, stop=True)
                    mm.then_inc(y_ready, 1)

        @block.vector
        def _(dve):
            dve.sem_inc(o_done, 2)
            dve.sem_inc(y_done, 1)
            dve.wait_ge(zeroed, 1)

            def largest(n, m):
                u = m % 2
                dve.wait_ge(s_ready, n * UN + m + 1)
                dve.tensor_reduce(nmax[:, u:u + 1], s_ps[:, s_at[u]:s_at[u] + tiles_of(units[m][1])[-1][1]], AX.X, ALU.max,
                                  negate=True).then_inc(max_ready, 1)

            def finish(n, g, m):
                j, i = units[m]
                if len(tgroups(i)) == 1:
                    dve.drain()
                dve.wait_ge(o_ready, n * UN + m + 1)
                dve.tensor_scalar(O[:, i, bass.ds(g * VW + j * hd, hd)], o_ps[m % 2], rl[:, m:m + 1], None,
                                  ALU.mult).then_inc(o_done, 1)

            def copy_projected(n, g, x):
                kind, what = projections[x]
                dve.wait_ge(pj_ready, n * NJ + x + 1)
                ps = t_ps[x % 2]
                if kind == "q":
                    a, z = what
                    for j in range(heads):
                        r = slice(j * slot, (j + 1) * slot)
                        if biased:
                            ins = dve.tensor_scalar(qT[r, j, a:z], ps[r, 0:z - a], qk_bias[r, 0, bass.ds(g, 1)], scale, ALU.add, ALU.mult)
                        else:
                            ins = dve.tensor_scalar(qT[r, j, a:z], ps[r, 0:z - a], scale, None, ALU.mult)
                elif kind == "k":
                    a, z = what
                    if biased:
                        ins = dve.tensor_scalar(kT[:, a:z], ps[:, 0:z - a], qk_bias[:, 1, bass.ds(g, 1)], None, ALU.add)
                    else:
                        ins = dve.tensor_copy(kT[:, a:z], ps[:, 0:z - a])
                else:
                    rows = what[0][1] - what[0][0]
                    k = what[0][0] // P
                    ins = dve.tensor_copy(V[0:rows, k:k + len(what), :],
                                          ps[0:rows, 0:len(what) * VW].rearrange("p (k v) -> p k v", v=VW))
                ins.then_inc(pj_dve, 1)

            with dve.Fori(0, B) as b:
                if KX:
                    dve.tensor_copy(kvT[:, :, S:KT], cxT[:, :, bass.ds(b * SC, SC)]).then_inc(cx_ready, 1)
                for i in range(TB):
                    if i >= 2:
                        dve.wait_ge(ht_ready, b * TB + i - 1)
                    normalise(dve, core, hn[i % 2][:, :], b * TB + i).then_inc(hn_ready, 1)
                with dve.Fori(0, NG) as g:
                    n = b * NG + g
                    for x in early[1::2]:
                        copy_projected(n, g, x)
                    for m in range(ahead):
                        largest(n, m)
                    for x in rest:
                        if x % 2 == 1:
                            copy_projected(n, g, x)
                    for m in range(UN):
                        if m > late:
                            finish(n, g, m - 1 - late)
                        i = units[m][1]
                        if len(tgroups(i)) == 1:
                            dve.wait_ge(e_ready, n * UN + m + 1)
                            dve.reciprocal(rl[:, m:m + 1], l[:, m:m + 1])
                        for x, gr in enumerate(tgroups(i)):
                            if x % 2:
                                dve.wait_ge(t_ready, n * t_all + t_at[m] + x + 1)
                                if x == 1:
                                    dve.reciprocal(rl[:, m:m + 1], l[:, m:m + 1])
                                dve.tensor_copy(PT[m % 2][:, gr[0]:gr[-1] + 1, :],
                                                t_ps[x][:, 0:len(gr) * P].rearrange("p (k q) -> p k q", q=P)).then_inc(tc_dve, 1)
                        if m + ahead < UN:
                            largest(n, m + ahead)
                    dve.drain()
                    for m in range(UN - 1 - late, UN):
                        finish(n, g, m)
                for i in range(TB):
                    dve.wait_ge(y_ready, b * TB + i + 1)
                    dve.tensor_copy(y[:, bass.ds(b * TB + i, 1), :], y_ps.unsqueeze(1)).then_inc(y_done, 1)

        @block.scalar
        def _(act):
            act.wait_ge(zeroed, 1)
            if biased:
                act.wait_ge(consts, 64)
                act.mul(q_bias[:, :], qk_bias[:, 0, :], scale)
                act.drain()

            def exponentials(n, m):
                u = m % 2
                kn = tiles_of(units[m][1])[-1][1]
                act.wait_ge(max_ready, n * UN + m + 1)
                act.activation(E[u][:, 0:kn], s_ps[:, s_at[u]:s_at[u] + kn], ACT.Exp, bias=nmax[:, u:u + 1],
                               accum_out=l[:, m:m + 1]).then_inc(e_ready, 1)

            def copy_projected(n, g, x):
                kind, what = projections[x]
                act.wait_ge(pj_ready, n * NJ + x + 1)
                ps = t_ps[x % 2]
                if kind == "q":
                    a, z = what
                    for j in range(heads):
                        r = slice(j * slot, (j + 1) * slot)
                        if biased:
                            ins = act.activation(qT[r, j, a:z], ps[r, 0:z - a], ACT.Identity, bias=q_bias[r, bass.ds(g, 1)],
                                                 scale=scale)
                        else:
                            ins = act.mul(qT[r, j, a:z], ps[r, 0:z - a], scale)
                elif kind == "k":
                    a, z = what
                    if biased:
                        ins = act.activation(kT[:, a:z], ps[:, 0:z - a], ACT.Identity, bias=qk_bias[:, 1, bass.ds(g, 1)])
                    else:
                        ins = act.copy(kT[:, a:z], ps[:, 0:z - a])
                else:
                    rows = what[0][1] - what[0][0]
                    k = what[0][0] // P
                    ins = act.copy(V[0:rows, k:k + len(what), :],
                                   ps[0:rows, 0:len(what) * VW].rearrange("p (k v) -> p k v", v=VW))
                ins.then_inc(pj_act, 1)

            with act.Fori(0, B) as b:
                for i in range(TB):
                    act.wait_ge(ht_ready, b * TB + i + 1)
                    for c in range(DC):
                        out, ps = kvT[:, c, i * P:(i + 1) * P], t_ps[i % 2][:, c * P:(c + 1) * P]
                        if affine is None:
                            cp = act.copy(out, ps)
                        else:
                            cp = act.activation(out, ps, ACT.Identity, bias=affine[:, 1, c:c + 1], scale=affine[:, 0, c:c + 1])
                    cp.then_inc(hT_ready, 1)
                with act.Fori(0, NG) as g:
                    n = b * NG + g
                    for x in early[0::2]:
                        copy_projected(n, g, x)
                    for m in range(ahead):
                        exponentials(n, m)
                    for x in rest:
                        if x % 2 == 0:
                            copy_projected(n, g, x)
                    for m in range(UN):
                        i = units[m][1]
                        ks = tiles_of(i)
                        for x, gr in enumerate(tgroups(i)):
                            if x % 2 == 0:
                                rows = ks[gr[0]][1] - ks[gr[0]][0]
                                act.wait_ge(t_ready, n * t_all + t_at[m] + x + 1)
                                act.copy(PT[m % 2][0:rows, gr[0]:gr[-1] + 1, :],
                                         t_ps[x][0:rows, 0:len(gr) * P].rearrange("p (k q) -> p k q", q=P)).then_inc(tc_act, 1)
                        if m + ahead < UN:
                            if len(tgroups(i)) % 2 == 0:
                                act.wait_ge(t_ready, n * t_all + t_at[m] + len(tgroups(i)))
                            exponentials(n, m + ahead)
                for i in range(TB):
                    for x, gr in enumerate(ogroups):
                        act.wait_ge(ot_ready, (b * TB + i) * len(ogroups) + x + 1)
                        act.copy(OT[i % 2][:, gr[0]:gr[-1] + 1, :],
                                 t_ps[x][:, 0:len(gr) * P].rearrange("p (k q) -> p k q", q=P)).then_inc(oT_ready, 1)


def add_normed(core, tag, A, y, gate):
    nc = core.nc
    with ExitStack() as stack:
        st = Stage(core, tag, stack)
        rows = st.sb("rows", [P, 2, D])
        stats = st.sb("stats", [P, NT, 6])
        mv = st.sb("mv", [P, NT, 2])
        rstd = st.sb("rstd", [P, NT])
        shift = st.sb("shift", [P, NT])
        loaded, var_ready, std_ready = st.sem("loaded"), st.sem("var_ready"), st.sem("std_ready")
        rows_ready = st.sem("rows_ready")
        shift_ready = st.sem("shift_ready")
        normed = st.sem("normed")
        shifted = st.sem("shifted")
        block = stack.enter_context(nc.Block())

        @block.sync
        def _(sp):
            sp.dma_start(rows[:, :, :], A["ln_o"]).then_inc(loaded, 16)

        @block.vector
        def _(dve):
            with dve.Fori(0, NT // 8) as k:
                for i in range(8):
                    dve.bn_stats(stats[:, 8 * k + i, :], y[:, 8 * k + i, :])
            dve.drain()
            for t in range(NT):
                dve.bn_aggr(mv[:, t, :], stats[:, t, :])
            dve.drain()
            dve.tensor_scalar(rstd[:, :], mv[:, :, 1], EPS, None, ALU.add).then_inc(var_ready, 1)
            dve.wait_ge(std_ready, 1)
            dve.reciprocal(rstd[:, :], rstd[:, :])
            dve.drain()
            dve.wait_ge(loaded, 16)
            dve.scalar_tensor_tensor(shift[:, :], mv[:, :, 0], -1.0, rstd[:, :], ALU.mult, ALU.mult).then_inc(shift_ready, 1)
            dve.tensor_scalar(rows[:, :, :], rows[:, :, :], gate, None, ALU.mult).then_inc(rows_ready, 1)
            dve.drain()
            with dve.Fori(0, NT // 4) as k:
                for i in range(4):
                    t = 4 * k + i
                    dve.wait_ge(normed, t + 1)
                    dve.tensor_tensor(y[:, t, :], y[:, t, :], rows[:, 0, :], ALU.mult)
                dve.drain()
                for i in range(4):
                    t = 4 * k + i
                    dve.wait_ge(shifted, t + 1)
                    dve.tensor_tensor(core.x[:, t, :], core.x[:, t, :], y[:, t, :], ALU.add)

        @block.gpsimd
        def _(pool):
            pool.wait_ge(rows_ready, 1)
            with pool.Fori(0, NT // 4) as k:
                for i in range(4):
                    t = 4 * k + i
                    pool.tensor_tensor(core.x[:, t, :], core.x[:, t, :], rows[:, 1, :], ALU.add).then_inc(shifted, 1)

        @block.scalar
        def _(act):
            act.wait_ge(var_ready, 1)
            act.activation(rstd[:, :], rstd[:, :], ACT.Sqrt).then_inc(std_ready, 1)
            act.wait_ge(shift_ready, 1)
            with act.Fori(0, NT // 4) as k:
                for i in range(4):
                    t = 4 * k + i
                    act.activation(y[:, t, :], y[:, t, :], ACT.Identity, bias=shift[:, bass.ds(t, 1)],
                                   scale=rstd[:, bass.ds(t, 1)]).then_inc(normed, 1)


def layer1_xattn(core, A):
    nc = core.nc
    with ExitStack() as stack:
        st = Stage(core, "L1x", stack)
        y = st.sb("y", [P, NT, D])
        cxT = st.sb("cxT", [P, DC, CT])
        mask_row = st.sb("mask_row", [1, CT], BF16)
        affine = st.sb("affine", [P, 2, DC])
        loaded = st.sem("loaded")
        with ExitStack() as inner:
            block = inner.enter_context(nc.Block())

            @block.sync
            def _(sp):
                sp.dma_start(affine[:, :, :], A["L1_ln_l"]).then_inc(loaded, 16)
                sp.wait_ge(loaded, 16)
        context_norm(core, "L1c", {"ctx": A["ctx"], "ln_x": A["L1_ln_x"], "mask": A["mask"]}, cxT, mask_row[:, :])
        row_stats(core, "L1s", twice=True)
        long_attention(core, "L1a", {k: A["L1_" + k] for k in ("wq", "wk", "wv", "wo")}, y, 2, 64, 64, 64 ** -0.5,
                       affine=affine, cxT=cxT, mask_row=mask_row)
        add_normed(core, "L1n", {"ln_o": A["L1_ln_o"]}, y, core.gates[:, 0, 1:2])


def transpose_normed(core, tag, hT):
    nc = core.nc
    with ExitStack() as stack:
        st = Stage(core, tag, stack)
        hn = [st.sb(f"hn{u}", [P, D]) for u in range(2)]
        h_ps = [st.ps(f"h_ps{u}", [P, DC, P]) for u in range(2)]
        hn_ready = st.sem("hn_ready")
        ht_ready = st.sem("ht_ready")
        hT_done = st.sem("hT_done")
        block = stack.enter_context(nc.Block())

        @block.vector
        def _(dve):
            with dve.Fori(0, NT // 2) as k:
                for u in range(2):
                    dve.wait_ge(ht_ready, 2 * k + u + 1)
                    normalise(dve, core, hn[u][:, :], 2 * k + u).then_inc(hn_ready, 1)

        @block.tensor
        def _(pe):
            pe.sem_inc(ht_ready, 2)
            with pe.Fori(0, NT // 2) as k:
                for u in range(2):
                    pe.wait_ge(hn_ready, 2 * k + u + 1)
                    pe.wait_ge(hT_done, 2 * k + u + 1)
                    for c in range(DC):
                        mm = pe.transpose(h_ps[u][:, c, :], hn[u][:, c * P:(c + 1) * P], core.ident[:, :])
                    mm.then_inc(ht_ready, 1)

        @block.scalar
        def _(act):
            act.sem_inc(hT_done, 2)
            with act.Fori(0, NT // 2) as k:
                for u in range(2):
                    act.wait_ge(ht_ready, 2 * k + u + 3)
                    act.copy(hT[:, :, bass.ds((2 * k + u) * P, P)], h_ps[u][:, :, :]).then_inc(hT_done, 1)


E8, F = 8, 1024
FC = F // P
NB = B * S // 512


def task_gates(core, tag, A, hT, gv, prefetch):
    nc = core.nc
    with ExitStack() as stack:
        st = Stage(core, tag, stack)
        w1 = st.sb("w1", [P, DC, D])
        b1 = st.sb("b1", [P, DC])
        w2 = st.sb("w2", [P, DC, E8])
        b2 = st.sb("b2", [P, E8])
        acc = st.sb("acc", [P, DC, NB])
        mh = st.sb("mh", [P, DC * B])
        spread = st.sb("spread", [P, DC * B, P])
        a_ps = [st.ps(f"a_ps{u}", [P, 512]) for u in range(2)]
        g_ps = st.ps("g_ps", [P, B, E8])
        loaded = st.sem("loaded")
        a_ready, a_done = st.sem("a_ready"), st.sem("a_done")
        spread_ready, g_ready = st.sem("spread_ready"), st.sem("g_ready")
        block = stack.enter_context(nc.Block())

        @block.sync
        def _(sp):
            sp.dma_start(w1[:, :, :], A["w1"].rearrange("(c p) o -> p c o", p=P)).then_inc(loaded, 16)
            sp.dma_start(b1[:, :], A["b1"]).then_inc(loaded, 16)
            sp.dma_start(w2[:, :, :], A["w2"].rearrange("(c p) e -> p c e", p=P)).then_inc(loaded, 16)
            sp.dma_start(b2[:, :], A["b2"]).then_inc(loaded, 16)
            prefetch(sp)

        @block.tensor
        def _(pe):
            pe.wait_ge(loaded, 64)
            for n in range(NB * DC):
                q, o = n // DC, n % DC
                if n >= 2:
                    pe.wait_ge(a_done, n - 1)
                for c in range(DC):
                    mm = pe.matmul(a_ps[n % 2][:, :], w1[:, c, o * P:(o + 1) * P], hT[:, c, q * 512:(q + 1) * 512],
                                   start=(c == 0), stop=(c == DC - 1))
                mm.then_inc(a_ready, 1)
            pe.wait_ge(spread_ready, 1)
            for b in range(B):
                for o in range(DC):
                    mm = pe.matmul(g_ps[:, b, :], spread[:, o * B + b, :], w2[:, o, :], start=(o == 0), stop=(o == DC - 1))
            mm.then_inc(g_ready, 1)

        @block.scalar
        def _(act):
            act.wait_ge(loaded, 64)
            for n in range(NB * DC):
                q, o = n // DC, n % DC
                act.wait_ge(a_ready, n + 1)
                act.activation(a_ps[n % 2][:, :], a_ps[n % 2][:, :], ACT.Relu, bias=b1[:, o:o + 1],
                               accum_out=acc[:, o, q:q + 1]).then_inc(a_done, 1)

        @block.vector
        def _(dve):
            dve.wait_ge(a_done, NB * DC)
            dve.tensor_reduce(mh[:, :], acc[:, :, :].rearrange("p o (b q) -> p (o b) q", b=B), AX.X, ALU.add)
            dve.drain()
            dve.tensor_scalar(mh[:, :], mh[:, :], 1.0 / S, None, ALU.mult)
            dve.drain()
            dve.tensor_copy(spread[:, :, :], mh[:, :].unsqueeze(2).to_broadcast([P, DC * B, P])).then_inc(spread_ready, 1)
            dve.wait_ge(g_ready, 1)
            dve.wait_ge(loaded, 64)
            dve.tensor_tensor(gv, g_ps[:, :, :], b2[:, :].unsqueeze(1).to_broadcast([P, B, E8]), ALU.add)


def task_buffers(st):
    W = DC * F + FC * D
    return (st.sb("base", [P, W]), [st.sb(f"task{u}", [P, W]) for u in range(2)], st.sem("loaded"),
            [st.sem(f"task_loaded{u}") for u in range(2)])


def load_task(sp, A, buffers, e):
    sp.dma_start(buffers[1][e % 2][:, :], A["w"][1 + e]).then_inc(buffers[3][e % 2], 16)


def merge_tasks(core, tag, A, buffers, gv, Wm, b1m, b2m):
    nc = core.nc
    W = DC * F + FC * D
    with ExitStack() as stack:
        st = Stage(core, tag, stack)
        base, task, loaded, task_loaded = buffers
        b1 = st.sb("b1", [P, E8 + 1, FC])
        b2 = st.sb("b2", [1, E8 + 1, D])
        PIECE = W // 4
        part = st.sb("part", [P, 2, PIECE])
        merged = st.sem("merged")
        part_ready = st.sem("part_ready")
        part_added = st.sem("part_added")
        bias_loaded = st.sem("bias_loaded")
        block = stack.enter_context(nc.Block())

        @block.sync
        def _(sp):
            sp.dma_start(b1[:, :, :], A["b1"]).then_inc(bias_loaded, 16)
            sp.dma_start(b2[:, :, :], A["b2"]).then_inc(bias_loaded, 16)
            for e in range(2, E8):
                sp.wait_ge(merged, e - 1)
                sp.wait_ge(part_ready, (e - 1) * 4)
                load_task(sp, A, buffers, e)

        @block.scalar
        def _(act):
            for e in range(E8):
                act.wait_ge(task_loaded[e % 2], 16 * (e // 2 + 1))
                for i in range(4):
                    n = 4 * e + i
                    if n >= 2:
                        act.wait_ge(part_added, n - 1)
                    act.mul(part[:, i % 2, :], task[e % 2][:, i * PIECE:(i + 1) * PIECE], gv[:, B - 1, e:e + 1]).then_inc(part_ready, 1)

        @block.gpsimd
        def _(pool):
            pool.wait_ge(loaded, 16)
            for e in range(E8):
                for i in range(4):
                    pool.wait_ge(part_ready, 4 * e + i + 1)
                    if e and i == 0:
                        pool.drain()
                    piece = slice(i * PIECE, (i + 1) * PIECE)
                    pool.tensor_tensor(Wm[:, B - 1, piece], Wm[:, B - 1, piece] if e else base[:, piece], part[:, i % 2, :],
                                       ALU.add).then_inc(part_added, 1)

        @block.vector
        def _(dve):
            dve.wait_ge(loaded, 16)
            dve.wait_ge(bias_loaded, 32)
            for e in range(E8):
                dve.wait_ge(task_loaded[e % 2], 16 * (e // 2 + 1))
                for b in range(B):
                    g = gv[:, b, e:e + 1]
                    dve.scalar_tensor_tensor(b1m[:, b, :], b1[:, 1 + e, :], g, b1m[:, b, :] if e else b1[:, 0, :], ALU.mult, ALU.add)
                    dve.scalar_tensor_tensor(b2m[:, b, :], b2[:, 1 + e, :], gv[0:1, b, e:e + 1],
                                             b2m[:, b, :] if e else b2[:, 0, :], ALU.mult, ALU.add)
                    if b == B - 1:
                        continue
                    ins = dve.scalar_tensor_tensor(Wm[:, b, :], task[e % 2][:, :], g, Wm[:, b, :] if e else base[:, :],
                                                   ALU.mult, ALU.add)
                ins.then_inc(merged, 1)
                dve.drain()


def batch_ffn(core, tag, hT, Wm, b1m, b2m, gate):
    nc = core.nc
    with ExitStack() as stack:
        st = Stage(core, tag, stack)
        uT = st.sb("uT", [P, FC, 512])
        u_ps = [st.ps(f"u_ps{i}", [P, 512]) for i in range(3)]
        o_ps = [st.ps(f"o_ps{i}", [P, D]) for i in range(2)]
        u_ready = st.sem("u_ready")
        u_done = st.sem("u_done")
        o_ready = st.sem("o_ready")
        x_done = st.sem("x_done")
        block = stack.enter_context(nc.Block())

        @block.tensor
        def _(pe):
            for b in range(B):
                w1 = Wm[:, b, 0:DC * F].rearrange("p (c f) -> p c f", c=DC)
                w2 = Wm[:, b, DC * F:].rearrange("p (k o) -> p k o", k=FC)
                with pe.Fori(0, 2) as q:
                    n = q + 2 * b
                    for k in range(FC):
                        if k >= 3:
                            pe.wait_ge(u_done, n * FC + k - 2)
                        for c in range(DC):
                            mm = pe.matmul(u_ps[k % 3][:, :], w1[:, c, k * P:(k + 1) * P], hT[:, c, bass.ds(n * 512, 512)],
                                           start=(c == 0), stop=(c == DC - 1))
                        mm.then_inc(u_ready, 1)
                    pe.wait_ge(u_done, (n + 1) * FC)
                    for i in range(4):
                        pe.wait_ge(x_done, n * 4 + i + 1)
                        for k in range(FC):
                            pe.matmul(o_ps[i % 2][:, :], uT[:, k, i * P:(i + 1) * P], w2[:, k, :], start=(k == 0), stop=False)
                        pe.matmul(o_ps[i % 2][:, :], core.ones[:, :], b2m[:, b, :], start=False, stop=True).then_inc(o_ready, 1)

        @block.scalar
        def _(act):
            for b in range(B):
                with act.Fori(0, 2) as q:
                    n = q + 2 * b
                    for k in range(FC):
                        act.wait_ge(u_ready, n * FC + k + 1)
                        act.activation(uT[:, k, :], u_ps[k % 3][:, :], ACT.Gelu_apprx_tanh,
                                       bias=b1m[:, b, k:k + 1]).then_inc(u_done, 1)

        @block.vector
        def _(dve):
            dve.sem_inc(x_done, 2)
            with dve.Fori(0, NT // 2) as k:
                for i in range(2):
                    t = 2 * k + i
                    dve.wait_ge(o_ready, t + 1)
                    dve.scalar_tensor_tensor(core.x[:, t, :], o_ps[i][:, :], gate, core.x[:, t, :],
                                             ALU.mult, ALU.add).then_inc(x_done, 1)


def layer1_ffn(core, A):
    with ExitStack() as stack:
        st = Stage(core, "L1f", stack)
        hT = st.sb("hT", [P, DC, B * S])
        gv = st.sb("gv", [P, B, E8])
        Wm = st.sb("Wm", [P, B, DC * F + FC * D])
        b1m = st.sb("b1m", [P, B, FC])
        b2m = st.sb("b2m", [1, B, D])
        row_stats(core, "L1t")
        transpose_normed(core, "L1h", hT)
        tasks = {"w": A["L1_tasks"], "b1": A["L1_tb1"], "b2": A["L1_tb2"]}
        with ExitStack() as inner:
            buffers = task_buffers(Stage(core, "L1m", inner))

            def prefetch(sp):
                sp.dma_start(buffers[0][:, :], tasks["w"][0]).then_inc(buffers[2], 16)
                load_task(sp, tasks, buffers, 0)
                load_task(sp, tasks, buffers, 1)

            task_gates(core, "L1g", {k: A["L1_g" + k] for k in ("w1", "b1", "w2", "b2")}, hT, gv[:, :, :], prefetch)
            merge_tasks(core, "L1m", tasks, buffers, gv, Wm, b1m, b2m)
        batch_ffn(core, "L1f", hT, Wm, b1m, b2m, core.gates[:, 1, 1:2])


def single_head_prep(core, tag, A, M, N, cM):
    nc = core.nc
    with ExitStack() as stack:
        st = Stage(core, tag, stack)
        wk = st.sb("wk", [P, DC, D])
        wq = st.sb("wq", [P, DC, D])
        wv = st.sb("wv", [P, DC, D])
        bqk = st.sb("bqk", [P, 2, DC])
        bv = st.sb("bv", [1, D])
        kT = st.sb("kT", [P, DC, CT])
        k_ps = st.ps("k_ps", [P, DC, 512])
        m_ps = st.ps("m_ps", [P, DC, 512])
        c_ps = st.ps("c_ps", [1, CT])
        v_ps = st.ps("v_ps", [SC, B, D])
        loaded, k_ready, kT_ready = st.sem("loaded"), st.sem("k_ready"), st.sem("kT_ready")
        v_ready, m_ready = st.sem("v_ready"), st.sem("m_ready")
        block = stack.enter_context(nc.Block())

        @block.sync
        def _(sp):
            for w, name in ((wk, "wk"), (wq, "wq"), (wv, "wv")):
                sp.dma_start(w[:, :, :], A[name].rearrange("(c p) e -> p c e", p=P)).then_inc(loaded, 16)
            sp.dma_start(bqk[:, :, :], A["bqk"]).then_inc(loaded, 16)
            sp.dma_start(bv[:, :], A["bv"]).then_inc(loaded, 16)

        @block.tensor
        def _(pe):
            pe.wait_ge(loaded, 80)
            for e in range(DC):
                for c in range(DC):
                    mm = pe.matmul(k_ps[:, e, 0:CT], wk[:, c, e * P:(e + 1) * P], core.ctxT[:, c, :], start=(c == 0), stop=(c == DC - 1))
            mm.then_inc(k_ready, 1)
            for b in range(B):
                for c in range(DC):
                    pe.matmul(v_ps[:, b, :], core.ctxT[:, c, b * SC:(b + 1) * SC], wv[:, c, :], start=(c == 0), stop=False)
                mm = pe.matmul(v_ps[:, b, :], core.ones[:, 0:SC], bv[:, :], start=False, stop=True)
            mm.then_inc(v_ready, 1)
            pe.wait_ge(kT_ready, 1)
            for c in range(DC):
                for e in range(DC):
                    pe.matmul(m_ps[:, c, 0:CT], wq[:, e, c * P:(c + 1) * P], kT[:, e, :], start=(e == 0), stop=(e == DC - 1))
            for e in range(DC):
                mm = pe.matmul(c_ps[:, :], bqk[:, 0, e:e + 1], kT[:, e, :], start=(e == 0), stop=(e == DC - 1))
            mm.then_inc(m_ready, 1)

        @block.scalar
        def _(act):
            act.wait_ge(k_ready, 1)
            for e in range(DC):
                cp = act.activation(kT[:, e, :], k_ps[:, e, 0:CT], ACT.Identity, bias=bqk[:, 1, e:e + 1])
            cp.then_inc(kT_ready, 1)
            act.wait_ge(m_ready, 1)
            for c in range(DC):
                act.copy(M[:, c, :, :], m_ps[:, c, 0:CT].rearrange("p (b j) -> p b j", b=B))

        @block.vector
        def _(dve):
            dve.wait_ge(v_ready, 1)
            dve.tensor_copy(N[0:SC, :, 0, :], v_ps[:, :, :])
            dve.wait_ge(m_ready, 1)
            dve.tensor_copy(cM[:, :, :], c_ps[:, :].rearrange("p (b j) -> p b j", b=B))


def layer2_xattn(core, A):
    with ExitStack() as stack:
        st = Stage(core, "L2x", stack)
        M = st.sb("M", [P, DC, B, SC])
        N = st.sb("N", [P, B, 1, D])
        cM = st.sb("cM", [1, B, SC])
        zero_tail(core, "L2z", N[:, :, :, :])
        single_head_prep(core, "L2p", {k: A["L2_" + k] for k in ("wk", "wq", "wv", "bqk", "bv")}, M, N, cM)
        row_stats(core, "L2s")
        cross_attend(core, "L2a", 1, M, N, D ** -0.5, core.gates[:, 0, 2:3], cM=cM)


def layer2_ffn(core, A):
    nh, nk = 4, 128
    with ExitStack() as stack:
        row_stats(core, "L2t")
        G = stack.enter_context(core.nc.sbuf_tensor("L2f_G", [P, DC, 2 * nh * nk], F32))
        fold_keys(core, "L2g", {"wq": A["L2_pq"], "keys": A["L2_keys"]}, 2 * nh, 64, nk, G)
        product_key_experts(core, "L2e", A["L2_table"], nh, nk, G, core.gates[:, 1, 2:3], last_expert=4095, soft=True,
                            mlp={k: A["L2_" + k] for k in ("wg", "wu", "wd")})


def layer3_xattn(core, A):
    nh, hd = 16, 16
    W = nh * SC
    with ExitStack() as stack:
        st = Stage(core, "L3x", stack)
        y = st.sb("y", [P, NT, D])
        row_stats(core, "L3s")
        long_attention(core, "L3a", {k: A["L3s_" + k] for k in ("wq", "wk", "wv", "wo", "qk_bias", "v_bias", "o_bias")}, y,
                       4, 16, 32, hd ** -0.5, causal=True, biased=True)
        M = st.sb("M", [P, DC, B, W])
        n_dram = core.nc.dram_tensor("L3x_n_dram", (B, W, D), F32, kind="Internal").ap()
        cM = st.sb("cM", [96, B, W], BF16)
        cM_ones = st.sb("cM_ones", [96, P], BF16)
        out_row = st.sb("out_row", [1, D])
        out_loaded, loaded = st.sem("out_loaded"), st.sem("loaded")
        cross_prep(core, "L3p", {k: A["L3c_" + k] for k in ("wk", "wv", "wq", "wo", "bias")}, nh, hd, M, n_dram, True, cM=cM)
        N = st.sb("N", [P, B, -(-W // P), D])
        zero_tail(core, "L3n", N[:, :, W // P, :])
        with ExitStack() as inner:
            block = inner.enter_context(core.nc.Block())

            @block.vector
            def _(dve):
                dve.memset(cM_ones[:, :], 1.0)

            @block.sync
            def _(sp):
                sp.dma_start(out_row[:, :], A["L3c_bo"]).then_inc(out_loaded, 16)
                sp.wait_ge(loaded, load_packed(sp, loaded, n_dram, N, W))
                sp.wait_ge(out_loaded, 16)

        cross_attend(core, "L3c", nh, M, N, hd ** -0.5, core.gates[:, 0, 3:4], src=y, cM=cM,
                     cM_ones=cM_ones[:, :], out_row=out_row[:, :])


def ternary_weights(core, tag, A, q, s_w):
    nc = core.nc
    W = DC * F
    with ExitStack() as stack:
        st = Stage(core, tag, stack)
        w = st.sb("w", [P, 3, W])
        ones = st.sb("ones", [P, P])
        mag = st.sb("mag", [P, 3])
        inv = st.sb("inv", [P, 3])
        s_ps = st.ps("s_ps", [P, 3])
        loaded, mag_ready, sum_ready = st.sem("loaded"), st.sem("mag_ready"), st.sem("sum_ready")
        block = stack.enter_context(nc.Block())

        @block.sync
        def _(sp):
            sp.dma_start(w[:, :, :], A["w"]).then_inc(loaded, 16)

        @block.vector
        def _(dve):
            dve.memset(ones[:, :], 1.0)
            dve.wait_ge(loaded, 16)
            dve.tensor_reduce(mag[:, :], w[:, :, :], AX.X, ALU.add, apply_absolute_value=True)
            dve.drain().then_inc(mag_ready, 1)
            dve.wait_ge(sum_ready, 1)
            dve.tensor_scalar(s_w, s_ps[:, :], 1.0 / (D * F), 1e-5, ALU.mult, ALU.max)
            dve.drain()
            dve.reciprocal(inv[:, :], s_w)
            dve.drain()
            for i in range(3):
                dve.tensor_scalar(w[:, i, :], w[:, i, :], inv[:, i:i + 1], ROUND, ALU.mult, ALU.add)
            dve.drain()
            dve.tensor_scalar(w[:, :, :], w[:, :, :], ROUND, 1.0, ALU.subtract, ALU.min)
            dve.drain()
            dve.tensor_scalar(q, w[:, :, :], -1.0, None, ALU.max)

        @block.tensor
        def _(pe):
            pe.wait_ge(mag_ready, 1)
            pe.matmul(s_ps[:, :], ones[:, :], mag[:, :], start=True, stop=True).then_inc(sum_ready, 1)


def bit_ffn(core, tag, A, q, s_w, gate, out):
    nc = core.nc
    wg = q[:, 0, :].rearrange("p (c f) -> p c f", c=DC)
    wu = q[:, 1, :].rearrange("p (c f) -> p c f", c=DC)
    wd = q[:, 2, :].rearrange("p (k o) -> p k o", k=FC)
    with ExitStack() as stack:
        st = Stage(core, tag, stack)
        identb = st.sb("identb", [P, P], BF16)
        hn = st.sb("hn", [P, D])
        hq = st.sb("hq", [P, D], BF16)
        hqT = st.sb("hqT", [P, DC, P], BF16)
        sg = st.sb("sg", [P, F])
        a = st.sb("a", [P, F])
        aq = st.sb("aq", [P, F], BF16)
        aqT = st.sb("aqT", [P, FC, P], BF16)
        top = st.sb("top", [P, 2])
        to_int = st.sb("to_int", [P, 2])
        g_scale = st.sb("g_scale", [P, NT])
        u_scale = st.sb("u_scale", [P, NT])
        o_scale = st.sb("o_scale", [P, NT])
        h_ps = st.ps("h_ps", [P, DC, P], BF16)
        g_ps = st.ps("g_ps", [P, F])
        u_ps = st.ps("u_ps", [P, F])
        t_ps = st.ps("t_ps", [P, FC, P], BF16)
        o_ps = st.ps("o_ps", [P, D])
        ident_ready = st.sem("ident_ready")
        hq_ready = st.sem("hq_ready")
        ht_ready = st.sem("ht_ready")
        hT_ready = st.sem("hT_ready")
        gu_ready = st.sem("gu_ready")
        sg_ready = st.sem("sg_ready")
        aq_ready = st.sem("aq_ready")
        at_ready = st.sem("at_ready")
        aT_ready = st.sem("aT_ready")
        o_ready = st.sem("o_ready")
        x_done = st.sem("x_done")
        stored = st.sem("stored")
        block = stack.enter_context(nc.Block())

        @block.sync
        def _(sp):
            rows = out.rearrange("b (n p) d -> p (b n) d", p=P)
            for k in range(NT // 8):
                tiles = slice(8 * k, 8 * k + 8)
                sp.wait_ge(x_done, 8 * k + 9)
                sp.dma_start(rows[:, tiles, :], core.x[:, tiles, :]).then_inc(stored, 16)
            sp.wait_ge(stored, 16 * (NT // 8))

        @block.vector
        def _(dve):
            def rounded(out, tmp, i):
                dve.tensor_scalar(tmp, tmp, to_int[:, i:i + 1], 127.0, ALU.mult, ALU.min)
                dve.drain()
                dve.tensor_scalar(tmp, tmp, -128.0, ROUND, ALU.max, ALU.add)
                dve.drain()
                return dve.tensor_scalar(out, tmp, ROUND, None, ALU.subtract)

            def scales(x, i):
                dve.tensor_reduce(top[:, i:i + 1], x, AX.X, ALU.max, apply_absolute_value=True)
                dve.drain()
                dve.tensor_scalar(top[:, i:i + 1], top[:, i:i + 1], 1e-5, None, ALU.max)
                dve.drain()
                dve.reciprocal(to_int[:, i:i + 1], top[:, i:i + 1])
                dve.tensor_scalar(top[:, i:i + 1], top[:, i:i + 1], 1.0 / 127.0, None, ALU.mult)
                dve.drain()
                dve.tensor_scalar(to_int[:, i:i + 1], to_int[:, i:i + 1], 127.0, None, ALU.mult)

            def front(t, first=False):
                dve.drain()
                normalise(dve, core, hn[:, :], t)
                dve.drain()
                scales(hn[:, :], 0)
                dve.tensor_scalar(g_scale[:, bass.ds(t, 1)], top[:, 0:1], s_w[:, 0:1], None, ALU.mult)
                dve.tensor_scalar(u_scale[:, bass.ds(t, 1)], top[:, 0:1], s_w[:, 1:2], None, ALU.mult)
                dve.drain()
                if not first:
                    dve.wait_ge(ht_ready, t)
                rounded(hq[:, :], hn[:, :], 0).then_inc(hq_ready, 1)

            def back(t):
                dve.drain()
                dve.wait_ge(sg_ready, t + 1)
                dve.scalar_tensor_tensor(a[:, :], u_ps[:, :], u_scale[:, bass.ds(t, 1)], sg[:, :], ALU.mult, ALU.mult)
                dve.drain()
                scales(a[:, :], 1)
                dve.tensor_scalar(o_scale[:, bass.ds(t, 1)], top[:, 1:2], s_w[:, 2:3], gate, ALU.mult, ALU.mult)
                dve.drain()
                rounded(aq[:, :], a[:, :], 1).then_inc(aq_ready, 1)

            def update(t):
                dve.wait_ge(o_ready, t + 1)
                dve.scalar_tensor_tensor(core.x[:, t, :], o_ps[:, :], o_scale[:, bass.ds(t, 1)], core.x[:, t, :],
                                         ALU.mult, ALU.add).then_inc(x_done, 1)

            dve.sem_inc(x_done, 1)
            dve.tensor_copy(identb[:, :], core.ident[:, :]).then_inc(ident_ready, 1)
            front(0, first=True)
            front(1)
            back(0)
            with dve.Fori(1, NT - 1) as t:
                front(t + 1)
                back(t)
                update(t - 1)
            back(NT - 1)
            update(NT - 2)
            update(NT - 1)

        @block.scalar
        def _(act):
            def front(t):
                act.wait_ge(ht_ready, t + 1)
                act.copy(hqT[:, :, :], h_ps[:, :, :]).then_inc(hT_ready, 1)

            def turn(t):
                act.wait_ge(at_ready, t + 1)
                act.copy(aqT[:, :, :], t_ps[:, :, :]).then_inc(aT_ready, 1)

            def silu(t):
                act.wait_ge(gu_ready, t + 1)
                act.activation(sg[:, :], g_ps[:, :], ACT.Silu, scale=g_scale[:, bass.ds(t, 1)]).then_inc(sg_ready, 1)

            front(0)
            silu(0)
            with act.Fori(0, NT - 1) as t:
                front(t + 1)
                turn(t)
                silu(t + 1)
            turn(NT - 1)

        @block.tensor
        def _(pe):
            def front(t):
                pe.wait_ge(hq_ready, t + 1)
                for c in range(DC):
                    mm = pe.transpose(h_ps[:, c, :], hq[:, c * P:(c + 1) * P], identb[:, :])
                mm.then_inc(ht_ready, 1)

            def products(t):
                pe.wait_ge(hT_ready, t + 1)
                for w, ps in ((wg, g_ps), (wu, u_ps)):
                    for n in range(2):
                        for c in range(DC):
                            mm = pe.matmul(ps[:, n * 512:(n + 1) * 512], hqT[:, c, :], w[:, c, n * 512:(n + 1) * 512],
                                           start=(c == 0), stop=(c == DC - 1))
                mm.then_inc(gu_ready, 1)

            def turn(t):
                pe.wait_ge(aq_ready, t + 1)
                for k in range(FC):
                    mm = pe.transpose(t_ps[:, k, :], aq[:, k * P:(k + 1) * P], identb[:, :])
                mm.then_inc(at_ready, 1)

            def output(t):
                pe.wait_ge(aT_ready, t + 1)
                pe.wait_ge(x_done, t + 1)
                for k in range(FC):
                    mm = pe.matmul(o_ps[:, :], aqT[:, k, :], wd[:, k, :], start=(k == 0), stop=(k == FC - 1))
                mm.then_inc(o_ready, 1)

            pe.wait_ge(ident_ready, 1)
            front(0)
            products(0)
            with pe.Fori(0, NT - 1) as t:
                front(t + 1)
                turn(t)
                products(t + 1)
                output(t)
            turn(NT - 1)
            output(NT - 1)


def layer3_ffn(core, A):
    with ExitStack() as stack:
        st = Stage(core, "L3f", stack)
        q = st.sb("q", [P, 3, DC * F], BF16)
        s_w = st.sb("s_w", [P, 3])
        ternary_weights(core, "L3w", {"w": A["L3_w"]}, q[:, :, :], s_w[:, :])
        row_stats(core, "L3t")
        bit_ffn(core, "L3b", A, q, s_w, core.gates[:, 1, 3:4], core.out)


def build(nc, A, out, stages):
    with ExitStack() as stack:
        core = Core(nc, stack, out)
        load_inputs(core, A)
        for s in stages:
            s(core, A)
            core.end_layer()


def layout(i):
    f = np.float32
    a = {}
    a["x"] = i["x"]
    a["ident"] = np.eye(P, dtype=f)
    a["ctxT"] = i["ctx_1024"].reshape(CT, D).T
    a["gates"] = np.broadcast_to(np.stack([i["g_xattn"], i["g_ffn"]]), (P, 2, 4))
    kv = i["L0_xattn_Wkv"].reshape(64, 2, 16, D)
    a["L0_wk"] = kv[:, 0].transpose(2, 1, 0).reshape(D, 1024)
    a["L0_wv"] = kv[:, 1].transpose(2, 1, 0).reshape(D, 1024)
    a["L0_wq"] = i["L0_xattn_Wq"].reshape(64, 16, D)
    a["L0_wo"] = i["L0_xattn_W0"].reshape(D, 16, 64).transpose(2, 1, 0)
    a["L0_bn"] = np.stack([i["L0_ffn_bn_gamma"], i["L0_ffn_bn_beta"]]).reshape(2, DC, P).transpose(2, 0, 1)
    a["L0_pq"] = i["L0_ffn_w_q"].reshape(16, 128, D).transpose(1, 0, 2)
    a["L0_keys"] = i["L0_ffn_keys_p"].transpose(3, 2, 0, 1).reshape(128, 16, 64)
    a["L0_table"] = np.concatenate([i["L0_ffn_down"], i["L0_ffn_up"]], axis=1)
    a["ctx"] = i["ctx_1024"].transpose(1, 0, 2)
    a["mask"] = i["mask_BxS2_bk0"].reshape(1, CT)
    for n in ("ln_x", "ln_l"):
        a["L1_" + n] = np.stack([i[f"L1_xattn_{n}_g"], i[f"L1_xattn_{n}_b"]]).reshape(2, DC, P).transpose(2, 0, 1)
    a["L1_ln_o"] = np.broadcast_to(np.stack([i["L1_xattn_ln_o_g"], i["L1_xattn_ln_o_b"]]), (P, 2, D))
    a["L1_wq"] = i["L1_xattn_Wq"].reshape(D, 8, P)
    a["L1_wk"] = i["L1_xattn_Wkv"][:, 0:1024].reshape(D, 8, P)
    a["L1_wv"] = i["L1_xattn_Wkv"][:, 1024:2048].reshape(D, 8, P)
    a["L1_wo"] = i["L1_xattn_Wout"]

    def chunked(w):
        return w.reshape(-1, P, w.shape[-1]).transpose(1, 0, 2).reshape(P, -1)

    a["L1_gw1"] = i["L1_ffn_gate_w1"].T
    a["L1_gb1"] = i["L1_ffn_gate_b1"].reshape(DC, P).T
    a["L1_gw2"] = i["L1_ffn_gate_w2"].T
    a["L1_gb2"] = np.broadcast_to(i["L1_ffn_gate_b2"], (P, E8))
    w1 = np.concatenate([i["L1_ffn_W1"][None], i["L1_ffn_TW1"]])
    w2 = np.concatenate([i["L1_ffn_W2"][None], i["L1_ffn_TW2"]])
    a["L1_tasks"] = np.stack([np.concatenate([chunked(u.T), chunked(v.T)], axis=1) for u, v in zip(w1, w2)])
    a["L1_tb1"] = np.concatenate([i["L1_ffn_b1"][None], i["L1_ffn_Tb1"]]).reshape(E8 + 1, FC, P).transpose(2, 0, 1)
    a["L1_tb2"] = np.concatenate([i["L1_ffn_b2"][None], i["L1_ffn_Tb2"]])[None]
    a["L2_wk"], a["L2_wv"], a["L2_wq"] = i["L2_xattn_Wk"], i["L2_xattn_Wv"], i["L2_xattn_Wq"].T
    a["L2_bqk"] = np.stack([i["L2_xattn_bq"], i["L2_xattn_bk"]]).reshape(2, DC, P).transpose(2, 0, 1)
    a["L2_bv"] = i["L2_xattn_bv"][None]
    a["L2_pq"] = i["L2_ffn_Wq"].reshape(8, 64, D).transpose(1, 0, 2)
    a["L2_keys"] = i["L2_ffn_keys"].transpose(3, 2, 0, 1).reshape(64, 8, 128)
    a["L2_table"] = np.concatenate([i["L2_ffn_down_embed"], i["L2_ffn_up_embed"]], axis=1)
    a["L2_wg"], a["L2_wu"], a["L2_wd"] = i["L2_ffn_Wg"].T, i["L2_ffn_Wu"].T, i["L2_ffn_Wd"].T
    for n in ("q", "k"):
        w = np.zeros((D, 4, 4, 32), f)
        w[:, :, :, 0:16] = i[f"L3_xattn_W{n}1"].transpose(1, 0, 2).reshape(D, 4, 4, 16)
        a["L3s_w" + n] = w.reshape(D, 4, P)
    bias = np.zeros((2, 4, 4, 32), f)
    bias[0, :, :, 0:16] = i["L3_xattn_bq1"].reshape(4, 4, 16)
    bias[1, :, :, 0:16] = i["L3_xattn_bk1"].reshape(4, 4, 16)
    a["L3s_qk_bias"] = bias.reshape(2, 4, P).transpose(2, 0, 1)
    a["L3s_wv"] = i["L3_xattn_Wv1"].transpose(1, 0, 2).reshape(D, 4, 64)
    a["L3s_v_bias"] = i["L3_xattn_bv1"].reshape(1, 4, 64)
    a["L3s_wo"] = i["L3_xattn_Wo1"]
    a["L3s_o_bias"] = i["L3_xattn_bo1"][None]
    a["L3c_wk"] = i["L3_xattn_Wk2"].transpose(1, 0, 2).reshape(D, D)
    a["L3c_wv"] = i["L3_xattn_Wv2"].transpose(1, 0, 2).reshape(D, D)
    a["L3c_wq"] = i["L3_xattn_Wq2"].transpose(2, 0, 1)
    a["L3c_wo"] = i["L3_xattn_Wo2"].reshape(16, 16, D).transpose(1, 0, 2)
    a["L3c_bias"] = np.stack([i["L3_xattn_bq2"], i["L3_xattn_bk2"], i["L3_xattn_bv2"]]).transpose(2, 0, 1)
    a["L3c_bo"] = i["L3_xattn_bo2"][None]
    a["L3_w"] = np.stack([chunked(i["L3_ffn_" + n].T) for n in ("w_gate", "w_up", "w_down")], axis=1)
    return a


ALL = [layer0_xattn, layer0_ffn, layer1_xattn, layer1_ffn, layer2_xattn, layer2_ffn, layer3_xattn, layer3_ffn]


def kernel(**inputs):
    import concourse.bacc as _bacc
    from concourse.bass_utils import run_bass_kernel_spmd as _run

    nc = _bacc.Bacc("TRN2", target_bir_lowering=False, num_devices=1)
    arrays = {"in_" + k: np.ascontiguousarray(v) for k, v in layout({k: np.asarray(v) for k, v in inputs.items()}).items()}
    aps = {k[3:]: nc.dram_tensor(k, v.shape, mybir.dt.from_np(v.dtype), kind="ExternalInput").ap() for k, v in arrays.items()}
    out = nc.dram_tensor("out_x", (B, S, D), F32, kind="ExternalOutput").ap()
    build(nc, aps, out, ALL)
    r = _run(nc, [arrays], core_ids=[0])
    return r.results[0]["out_x"]
```
